# Optimizing a Trainium2 kernel written in Bass

```python
import numpy as np
import jax
import jax.numpy as jnp

def _softmax(x, axis=-1):
    return jax.nn.softmax(x, axis=axis)

def _gelu(x):
    return jax.nn.gelu(x, approximate=True)

def _silu(x):
    return jax.nn.silu(x)

def _sigmoid(x):
    return jax.nn.sigmoid(x)

def _layernorm(x, axis=-1, eps=1e-05):
    m = jnp.mean(x, axis=axis, keepdims=True)
    v = jnp.var(x, axis=axis, keepdims=True)
    return (x - m) / jnp.sqrt(v + eps)

def _scatter_add(tgt, idx, src, axis=0):
    return tgt.at[idx].add(src)

def _segment_sum(src, seg, n):
    return jax.ops.segment_sum(src, seg, n)
kernel_name = 'mk_xattn_ffn_d1_seqx_r2_866993'

def setup_inputs(seed: int=0):
    np.random.seed(seed)
    _w = jnp.asarray

    def _rec_inputs():
        import jax
        import jax.numpy as jnp
        _rk = jax.random.key(seed)
        x = 7.22e-05 + 1 * jax.random.normal(jax.random.fold_in(_rk, 1), (8, 512, 512), jnp.float32)
        _lenS = 512 - jax.random.randint(jax.random.fold_in(_rk, 7), (8,), 0, max(1, 512 // 4) + 1, jnp.int32)
        _lenS2 = 77 - jax.random.randint(jax.random.fold_in(_rk, 8), (8,), 0, max(1, 77 // 4) + 1, jnp.int32)
        _ctx_1024P = jax.random.normal(jax.random.fold_in(_rk, 11), (8, 16, 512), jnp.float32)
        _ctx_1024c = jax.random.dirichlet(jax.random.fold_in(_rk, 511), 0.3 * jnp.ones((16,), jnp.float32), (8, 77))
        _ctx_1024t = jnp.einsum('bsk,bkd->bsd', _ctx_1024c, _ctx_1024P)
        _ctx_1024t = _ctx_1024t * jax.lax.rsqrt(jnp.mean(jnp.square(_ctx_1024t)) + 1e-12) * 0.953939
        ctx_1024 = -0.000514642 + 1.00011 * (_ctx_1024t + 0.3 * jax.random.normal(jax.random.fold_in(_rk, 611), (8, 77, 512), jnp.float32))
        return (x, ctx_1024)
    x, ctx_1024 = _rec_inputs()

    def _L0_xattn_setup():
        import jax, jax.numpy as jnp
        import numpy as np
        B, S, E, H = (4, 1024, 256, 512)
        key = jax.random.key(seed)
        ks = jax.random.split(key, 8)
        s = 1.0 / np.sqrt(H)
        return {'hidden_states': jax.random.normal(ks[0], (B, S, H), jnp.float32), 'external_embeddings': jax.random.normal(ks[1], (B, E, H), jnp.float32), 'Wq': jax.random.normal(ks[2], (H, H), jnp.float32) * s, 'bq': jax.random.normal(ks[3], (H,), jnp.float32) * 0.02, 'Wk': jax.random.normal(ks[4], (H, H), jnp.float32) * s, 'bk': jax.random.normal(ks[5], (H,), jnp.float32) * 0.02, 'Wv': jax.random.normal(ks[6], (H, H), jnp.float32) * s, 'bv': jax.random.normal(ks[7], (H,), jnp.float32) * 0.02}
    _L0_xattn_all = _L0_xattn_setup()
    _L0_xattn_in = {k: v for k, v in _L0_xattn_all.items() if k in ('Wq', 'bq', 'Wk', 'bk', 'Wv', 'bv')}
    del _L0_xattn_all

    def _L0_ffn_setup():
        import jax, jax.numpy as jnp
        import numpy as np
        NUM_HEADS = 16
        TOP_K = 2
        key = jax.random.key(seed)
        ks = jax.random.split(key, 5)
        B, S, D, E = (4, 1024, 512, 8)
        scale = 0.02
        return {'x': jax.random.normal(ks[0], (B, S, D), dtype=jnp.float32), 'W_qkv': jax.random.normal(ks[1], (D, 3 * D), dtype=jnp.float32) * scale, 'b_qkv': jnp.zeros((3 * D,), dtype=jnp.float32), 'W_gate': jax.random.normal(ks[2], (D, E), dtype=jnp.float32) * scale, 'b_gate': jnp.zeros((E,), dtype=jnp.float32), 'W_experts': jax.random.normal(ks[3], (E, D, D), dtype=jnp.float32) * scale, 'b_experts': jnp.zeros((E, D), dtype=jnp.float32)}
    _L0_ffn_all = _L0_ffn_setup()
    _L0_ffn_in = {k: v for k, v in _L0_ffn_all.items() if k in ('W_qkv', 'b_qkv', 'W_gate', 'b_gate', 'W_experts', 'b_experts')}
    del _L0_ffn_all
    return {'x': x, 'ctx_1024': ctx_1024, 'L0_xattn_Wq': _L0_xattn_in['Wq'], 'L0_xattn_bq': _L0_xattn_in['bq'], 'L0_xattn_Wk': _L0_xattn_in['Wk'], 'L0_xattn_bk': _L0_xattn_in['bk'], 'L0_xattn_Wv': _L0_xattn_in['Wv'], 'L0_xattn_bv': _L0_xattn_in['bv'], 'L0_ffn_W_qkv': _L0_ffn_in['W_qkv'], 'L0_ffn_b_qkv': _L0_ffn_in['b_qkv'], 'L0_ffn_W_gate': _L0_ffn_in['W_gate'], 'L0_ffn_b_gate': _L0_ffn_in['b_gate'], 'L0_ffn_W_experts': _L0_ffn_in['W_experts'], 'L0_ffn_b_experts': _L0_ffn_in['b_experts']}

def reference(x, ctx_1024, L0_xattn_Wq, L0_xattn_bq, L0_xattn_Wk, L0_xattn_bk, L0_xattn_Wv, L0_xattn_bv, L0_ffn_W_qkv, L0_ffn_b_qkv, L0_ffn_W_gate, L0_ffn_b_gate, L0_ffn_W_experts, L0_ffn_b_experts):
    import jax
    import jax.numpy as jnp

    def _L0_xattn_ref(hidden_states, external_embeddings, Wq, bq, Wk, bk, Wv, bv):
        import jax, jax.numpy as jnp
        import numpy as np
        B, S, E, H = (4, 1024, 256, 512)
        q = hidden_states @ Wq + bq
        k_tok = hidden_states @ Wk + bk
        v_tok = hidden_states @ Wv + bv
        k_ext = external_embeddings @ Wk + bk
        v_ext = external_embeddings @ Wv + bv
        s_self = jnp.einsum('bsh,bsh->bs', q, k_tok)[..., None]
        s_ext = jnp.einsum('bsh,beh->bse', q, k_ext)
        scores = jnp.concatenate([s_self, s_ext], axis=-1)
        probs = jax.nn.softmax(scores, axis=-1)
        ctx = probs[..., :1] * v_tok + jnp.einsum('bse,beh->bsh', probs[..., 1:], v_ext)
        return ctx

    def _L0_ffn_ref(x, W_qkv, b_qkv, W_gate, b_gate, W_experts, b_experts):
        import jax, jax.numpy as jnp
        import numpy as np
        NUM_HEADS = 16
        TOP_K = 2
        B, S, D = x.shape
        H = NUM_HEADS
        hd = D // H
        E = W_gate.shape[-1]
        qkv = (x @ W_qkv + b_qkv).reshape(B, S, 3, H, hd)
        q, k, v = (qkv[:, :, 0], qkv[:, :, 1], qkv[:, :, 2])
        attn = jnp.einsum('bqhd,bkhd->bhqk', q, k) / jnp.sqrt(jnp.asarray(hd, x.dtype))
        attn = jax.nn.softmax(attn, axis=-1)
        attn_out = jnp.einsum('bhqk,bkhd->bqhd', attn, v).reshape(B, S, D)
        gate = jax.nn.softmax(x @ W_gate + b_gate, axis=-1)
        top_g, top_i = jax.lax.top_k(gate, TOP_K)
        combine = jnp.sum(jax.nn.one_hot(top_i, E, dtype=x.dtype) * top_g[..., None], axis=2)
        expert_out = jnp.einsum('bsd,edf->bsef', x, W_experts) + b_experts
        moe_out = jnp.einsum('bsef,bse->bsf', expert_out, combine)
        return attn_out + moe_out
    x = x + _L0_xattn_ref(_layernorm(x, axis=-1), ctx_1024, L0_xattn_Wq, L0_xattn_bq, L0_xattn_Wk, L0_xattn_bk, L0_xattn_Wv, L0_xattn_bv)
    x = x + _L0_ffn_ref(_layernorm(x, axis=-1), L0_ffn_W_qkv, L0_ffn_b_qkv, L0_ffn_W_gate, L0_ffn_b_gate, L0_ffn_W_experts, L0_ffn_b_experts)
    return x

_drawn_inputs = setup_inputs


def setup_inputs(seed=0):
    import zlib

    import numpy as np

    out = dict(_drawn_inputs(seed))
    spreads = {'L0_ffn_b_qkv': (0.0, 0.1), 'L0_ffn_b_gate': (0.0, 0.3), 'L0_ffn_b_experts': (0.0, 0.424)}
    factors = {'L0_xattn_bk': 8.0, 'L0_xattn_bv': 3.831}
    for name, (base, spread) in spreads.items():
        noise = np.random.default_rng([zlib.crc32(name.encode()), seed]).standard_normal(out[name].shape)
        drawn = base * np.exp(spread * noise) if base else spread * noise
        out[name] = jnp.asarray(drawn.astype(out[name].dtype))
    for name, factor in factors.items():
        out[name] = (out[name] * factor).astype(out[name].dtype)
    return out
```

```python
from contextlib import ExitStack
import numpy as np
import concourse.bass as bass
from concourse import mybir

P = 128
ALU = mybir.AluOpType
ACT = mybir.ActivationFunctionType
AX = mybir.AxisListType
F32 = mybir.dt.float32
F32R = mybir.dt.float32r
U32 = mybir.dt.uint32
I32 = mybir.dt.int32


def program(nc, x, ctx, wq, bq, wk, bk, wv, bv, w_qkv, b_qkv, w_gate, b_gate, w_exp, b_exp, out):
    B, S, D = x.shape
    E = ctx.shape[1]
    C = D // P
    T = S // P
    W = E + 1
    HB = B // 2
    NE = w_gate.shape[1]
    EPS = 1e-5
    NB = B * T * 2 + NE - 1
    NB += NB % 2
    x1_dram = nc.dram_tensor("x1_rows", (B * S, D), F32, kind="Internal").ap()
    h2_dram = nc.dram_tensor("h2_rows", (B * S, D), F32, kind="Internal").ap()
    att_dram = nc.dram_tensor("attention_rows", (B * S, D), F32, kind="Internal").ap()
    slot_dram = nc.dram_tensor("slot_list", (NB * P, 2), F32, kind="Internal").ap()
    yb_dram = nc.dram_tensor("expert_rows", (NB * P, D), F32, kind="Internal").ap()
    with ExitStack() as stack:
        def sb(name, shape, dt=F32):
            return stack.enter_context(nc.sbuf_tensor(name, shape, dt))

        def sem(name):
            return stack.enter_context(nc.semaphore(name))

        bank = [stack.enter_context(nc.psum_tensor(f"bank{i}", [P, 512], F32)) for i in range(8)]
        PARTS, PLAIN = 34816, 15872
        parts = sb("parts", [P, PARTS], F32R)
        plain = sb("plain", [P, PLAIN])

        def area(arena, at, *shape):
            n = int(np.prod(shape))
            assert at + n <= (PARTS if arena is parts else PLAIN), (at, n)
            v = arena[:, at:at + n]
            if len(shape) == 2:
                v = v.rearrange("p (a b) -> p a b", a=shape[0])
            if len(shape) == 3:
                v = v.rearrange("p (a b c) -> p a b c", a=shape[0], b=shape[1])
            return v

        def pair(at, *shape):
            n = int(np.prod(shape))
            return area(parts, at, *shape), area(parts, at + n, *shape)

        def full(part):
            return part.bitcast(F32)

        CTX = C * B * W
        wqT = pair(0, C, D)
        wkT = pair(2 * C * D, C, D)
        vext = pair(0, B, D)
        wkp = pair(4 * C * D, C, D)
        A = pair(4 * C * D, C, D)
        wvp = pair(6 * C * D, C, D)
        r0 = 8 * C * D
        G = pair(r0, C, B * W)
        KE = pair(r0 + 2 * CTX, C, B * W)
        eT = pair(r0 + 4 * CTX, C, B * W)
        hT = [pair(r0 + 4 * CTX + 2 * C * P * i, C, P) for i in range(2)]
        h2T = [pair(r0 + 4 * CTX + 2 * C * P * (2 + i), C, P) for i in range(2)]
        pT = pair(r0 + 4 * CTX + 8 * C * P, P)
        gw = pair(r0 + 6 * CTX, C, NE)
        bqrep = pair(r0 + 6 * CTX + 2 * C * NE, C, P)
        wst = [area(plain, C * D * i, C, D) for i in range(3)]
        est = area(plain, 3 * C * D, B, D)
        p0 = 3 * C * D
        x1 = area(plain, p0, T, D)
        h = area(plain, p0 + T * D, 2, D)
        h2 = area(plain, p0 + (T + 2) * D, 2, D)
        p0 += B * D
        vst = area(plain, p0, D)
        gst = area(plain, p0, HB, W)
        scr = area(plain, p0, D)
        bv_all = area(plain, p0 + D, D)
        xin = area(plain, p0 + 2 * D, T, D)
        Q3 = w_qkv.shape[1]
        HD = 32
        NH = D // HD
        HG = P // HD
        NG = NH // HG
        wqkv = pair(0, C, Q3)
        r1 = 2 * C * Q3
        fT = pair(r1, C, S)
        r1 += 2 * C * S
        qk = [[pair(r1 + 4 * S * g + 2 * S * i, S) for i in range(2)] for g in range(2)]
        r1 += 8 * S
        QS = [area(parts, r1 + 2 * HG * S * g, HG, S) for g in range(2)]
        KS = [area(parts, r1 + 2 * HG * S * g + HG * S, HG, S) for g in range(2)]
        wraw = area(plain, 0, C, Q3)
        PT = [area(plain, T * S * j, T, S) for j in range(HG)]
        p1 = HG * T * S
        PR = [area(plain, p1 + T * S * i, T, S) for i in range(2)]
        p1 += 2 * T * S
        V = area(plain, p1, T, D)
        p1 += T * D
        h2f = full(area(parts, r1 + 4 * HG * S, 2, D))
        Osb = area(plain, p1, S)
        tmp = [area(plain, p1 + S * (i + 1), T, P) for i in range(2)]
        bvf = sb("bias_v_all", [P, D])
        bqk = sb("bias_qk_cols", [P, 2 * C])
        nmx = sb("neg_max", [P, NH, T])
        Z = sb("denominators", [P, T, NH])
        rZ = sb("inverse_denominators", [P, T, NH])

        ident = sb("ident", [P, P])
        ones = sb("ones", [P, P])
        sbias = sb("score_bias", [P, B * W])
        bqc = sb("bq_cols", [P, C])
        bkc = sb("bk_cols", [P, C])
        cq = sb("cq", [P, 2 * C])
        gws = sb("gate_stage", [P, C, NE])
        st1 = sb("st1", [P, 2, 6]); st2 = sb("st2", [P, 2, 6])
        mo1 = sb("mo1", [P, 2, 4]); mo2 = sb("mo2", [P, 2, 4])
        cst = sb("consts", [P, 2])
        fence = sb("fence", [P, 8])
        sc = sb("sc", [P, 2, W])
        NB = B * T * 2 + NE - 1
        NB += NB % 2
        NT = B * T
        temp = [area(plain, 3 * C * D + 8 * D + i * NT * NE, NT, NE) for i in range(10)]
        rec = sbias[:, 0:2 * NT * 3].rearrange("p (k t c) -> p k t c", k=2, c=3)
        lst = sbias[:, 6 * NT:6 * NT + 2 * NB].rearrange("p (i c) -> p i c", c=2)
        bexp = sbias[:, 6 * NT + 2 * NB:6 * NT + 3 * NB].bitcast(U32)
        sm = sbias[:, 6 * NT + 3 * NB:6 * NT + 3 * NB + 2 * NT + 6 * NE]
        iot = sb("count_int", [P, NB], I32)
        kk = sb("count", [P, NB])
        tri = sb("strict_triangle", [P, P])
        bg_all = sb("bias_gate_all", [P, NE])
        recs = sb("records", [P, 4, 3])
        idx = sb("row_numbers", [P, 4], U32)
        EW = 2 * C * D
        ew = [area(parts, EW * e, 2, C, D) for e in range(NE)]
        gT = [area(parts, EW * NE + 2 * C * P * i, 2, C, P) for i in range(2)]
        eraw = [area(plain, C * D * i, C, D) for i in range(2)]
        p2 = 2 * C * D
        be_all = area(plain, p2, NE * D)
        p2 += NE * D
        rows = [area(plain, p2 + D * i, D) for i in range(2)]
        ysb = [area(plain, p2 + D * (2 + i), D) for i in range(2)]
        p2 += 4 * D
        fin = [[area(plain, p2 + D * (4 * i + k), D) for k in range(4)] for i in range(2)]
        col = sb("col", [P, 2, 4])
        glog = sb("glog", [P, B * T, NE])

        names = """in_wk in_wq in_wv in_ctx in_bias made_ident made_ones made_consts
        w_hi w_ready set_full set_hi set_staged set_free
        ln1_stats ln1_var ln1_eps ln1_rstd h_ready h_tr hT_hi hT_ready s_full s_step s_max s_exp s_den p_ready p_tr pT_hi pT_ready
        e_full v_full x1_part x1_ready ln2_stats ln2_var ln2_eps ln2_rstd h2_ready h2_tr h2T_hi h2T_ready g_full g_copied
        in_wqkv in_fb f_wscaled f_whi f_wready f_raw0 f_raw1 f_h_tr f_hT_hi f_hT_ready f_d_full f_qk_hi f_proj
        f_stack0 f_stack1 f_s_full f_max f_exp f_t_full f_pt_a f_pt_d f_pv f_o_sb f_ot f_rz f_o_fin  x_in0 x_in1 x_in2 x_in3 in_bg sp_went_on pool_went_on made_count route r_gate r_pref r_zero r_zeroed r_tokens r_copied r_scat0 r_scat1 r_scat2 r_scat3 in_list
        in_be in_ew0 in_ew1 m_ehi m_elo m_idx m_rows0 m_rows1 m_tr m_hi m_hT m_full m_sum m_y m_out0 m_out1
        c_x0 c_x1 c_a0 c_a1 c_idx c_g0 c_g1 c_pair c_sum c_out0 c_out1 f_att_out0 f_att_out1
        x1_out0 x1_out1 x1_out2 x1_out3 h2_out0 h2_out1""".split()
        q = {n: sem(n) for n in names}
        block = stack.enter_context(nc.Block())
        x_t = x.rearrange("b (t p) d -> (b t) p d", p=P)
        x1_t = x1_dram.rearrange("(t p) d -> t p d", p=P)
        h2_t = h2_dram.rearrange("(t p) d -> t p d", p=P)
        out_t = out.rearrange("b (t p) d -> (b t) p d", p=P)
        att_t = att_dram.rearrange("(t p) d -> t p d", p=P)
        yb_t = yb_dram.rearrange("(t p) d -> t p d", p=P)

        def prod3(pe, out, stat, mov, first, last):
            pe.matmul(out, stat[0], mov[0], start=first, stop=False)
            pe.matmul(out, stat[0], mov[1], start=False, stop=False)
            return pe.matmul(out, stat[1], mov[0], start=False, stop=last)

        def at(p, *idx):
            return p[0][idx], p[1][idx]

        n_wqT, n_wkT, n_eT, n_KE = 0, C, 2 * C, 2 * C + B
        n_A = n_KE + 2 * C
        n_cq = n_A + C
        n_G = n_cq + 1
        n_sb = n_G + 2 * C
        n_ve = n_sb + 2
        n_end = n_ve + B

        ND = 2 * NG + T
        SB = (4, 5, 7)
        STACKED = 16 * 8 * HG

        def dense(g, i):
            return i if g == 0 else T + 2 * g + i

        N_PICKED = 19

        @block.sync
        def _(sp):
            for w, to, name in ((wk, 1, "in_wk"), (wq, 0, "in_wq"), (wv, 2, "in_wv")):
                sp.dma_start(wst[to], w.rearrange("(c p) n -> p c n", p=P)).then_inc(q[name], 16)
            for t in range(T):
                sp.dma_start(xin[:, t, :], x_t[t]).then_inc(q[f"x_in{t}"], 16)

            sp.wait_ge(q["set_free"], n_end)
            sp.dma_start(wraw, w_qkv.rearrange("(c p) n -> p c n", p=P)).then_inc(q["in_wqkv"], 16)
            sp.dma_start(bqk[:], b_qkv.rearrange("(c p) -> p c", p=P)[:, 0:2 * C], allow_slow_non_contiguous=True).then_inc(q["in_fb"], 16)
            sp.dma_start(bvf[:], b_qkv.rearrange("(a n) -> a n", a=3)[2:3, :].broadcast_to([P, D])).then_inc(q["in_fb"], 16)

            def tiles(b, more):
                for t in range(T):
                    sp.wait_ge(q["x1_ready"], b * T + t + 1)
                    sp.dma_start(x1_t[b * T + t], x1[:, t, :]).then_inc(q[f"x1_out{t}"], 16)
                    if more:
                        sp.dma_start(xin[:, t, :], x_t[b * T + t + T]).then_inc(q[f"x_in{t}"], 16)
                    sp.wait_ge(q["h2_ready"], b * T + t + 1)
                    sp.dma_start(h2_t[b * T + t], h2[:, t % 2, :]).then_inc(q[f"h2_out{t % 2}"], 16)

            with sp.Fori(0, B - 1) as b:
                tiles(b, True)
            tiles(B - 1, False)
            for t in range(T):
                sp.wait_ge(q[f"x1_out{t}"], 16 * B)
            for t in range(2):
                sp.wait_ge(q[f"h2_out{t}"], 16 * B * T // 2)

            def raw(i, t):
                sp.wait_ge(q["f_h_tr"], i - t + max(0, t - 1))
                sp.dma_start(h2f[:, t % 2, :], h2_t[i]).then_inc(q[f"f_raw{t % 2}"], 16)

            def stacks(b, g):
                sp.wait_ge(q["f_proj"], b * ND + dense(g, 1) + 1)
                sp.sem_inc(q["sp_went_on"], 1)
                sp.wait_ge(q["f_s_full"], b * NH * T + max(0, g - 1) * HG * T)
                for j in range(HG):
                    for i, (to, order) in enumerate(((QS, (0, 0, 1, 1)), (KS, (0, 1, 0, 1)))):
                        for k, part in enumerate(order):
                            sp.dma_start(full(to[g % 2][k * HD:(k + 1) * HD, j, :]),
                                         full(qk[g % 2][i][part][j * HD:(j + 1) * HD, :])).then_inc(q[f"f_stack{g % 2}"], 16)

            sp.wait_ge(q["r_zero"], 1)
            sp.dma_start(slot_dram.rearrange("(p i) c -> p i c", p=P), lst).then_inc(q["r_zeroed"], 16)
            sp.wait_ge(q["f_wready"], 2)

            def batch(b):
                for t in range(T):
                    raw(b * T + t, t)
                for g in range(NG):
                    stacks(b, g)

            with sp.Fori(0, B) as b:
                batch(b)
            for k in range(4):
                sp.wait_ge(q[f"r_scat{k}"], 16 * NT // 2)
            sp.dma_start(lst, slot_dram.rearrange("(i p) c -> p i c", p=P)).then_inc(q["in_list"], 16)
            sp.wait_ge(q["f_pv"], B * NG)
            sp.wait_ge(q["f_ot"], B * NG)
            for e in range(NE):
                if e >= 2:
                    sp.wait_ge(q["m_elo"], e - 1)
                sp.dma_start(eraw[e % 2], w_exp[e].rearrange("(c p) n -> p c n", p=P)).then_inc(q[f"in_ew{e % 2}"], 16)
            sp.dma_start(be_all, b_exp.rearrange("(a e) n -> a (e n)", a=1).broadcast_to([P, NE * D])).then_inc(q["in_be"], 16)

            def y_store(i, k):
                sp.wait_ge(q["m_y"], i + 1)
                sp.dma_start(yb_t[i], ysb[k]).then_inc(q[f"m_out{k}"], 16)

            with sp.Fori(0, NB // 2) as n:
                for k in range(2):
                    y_store(2 * n + k, k)

            for k in range(2):
                sp.dma_start(fin[k][0], x1_t[k]).then_inc(q[f"c_x{k}"], 16)
                sp.wait_ge(q[f"f_att_out{k}"], 16 * B * NG // 2)
            for k in range(2):
                sp.dma_start(fin[k][1], att_t[k]).then_inc(q[f"c_a{k}"], 16)

            def combine(n, more):
                for k in range(2):
                    i = 2 * n + k
                    sp.wait_ge(q["c_sum"], i + 1)
                    sp.dma_start(out_t[i], fin[k][0]).then_inc(q[f"c_out{k}"], 16)
                    if more:
                        sp.dma_start(fin[k][1], att_t[i + 2]).then_inc(q[f"c_a{k}"], 16)
                        sp.wait_ge(q[f"c_out{k}"], 16 * n + 16)
                        sp.dma_start(fin[k][0], x1_t[i + 2]).then_inc(q[f"c_x{k}"], 16)

            with sp.Fori(0, NT // 2 - 1) as n:
                combine(n, True)
            combine(NT // 2 - 1, False)
            for k in range(2):
                sp.wait_ge(q[f"c_out{k}"], 16 * NT // 2)

        @block.gpsimd
        def _(pool):
            pool.memset(ident[:], 0.0).then_inc(q["made_ident"], 1)
            pool.wait_ge(q["made_ident"], 1)
            pool.affine_select(out=ident[:], in_=ident[:], compare_op=ALU.not_equal, fill=1.0, base=0,
                               pattern=[[-1, P]], channel_multiplier=1).then_inc(q["made_ident"], 1)
            pool.memset(ones[:], 1.0).then_inc(q["made_ones"], 1)
            pool.wait_ge(q["made_ones"], 1)
            pool.memset(full(eT[0].rearrange("p c (b w) -> p (c b) w", w=W)[:, :, E:W]), 0.0).then_inc(q["made_ones"], 1)
            pool.memset(full(eT[1].rearrange("p c (b w) -> p (c b) w", w=W)[:, :, E:W]), 0.0).then_inc(q["made_ones"], 1)
            pool.memset(cst[:, 0:1], EPS).then_inc(q["made_consts"], 1)
            pool.memset(cst[:, 1:2], -0.5).then_inc(q["made_consts"], 1)
            pool.wait_ge(q["made_consts"], 2)
            pool.affine_select(out=tri[:], in_=ones[:], compare_op=ALU.is_gt, fill=0.0, base=0,
                               pattern=[[1, P]], channel_multiplier=-1).then_inc(q["made_count"], 1)
            pool.iota(iot[:], pattern=[[1, NB]], base=0, channel_multiplier=0).then_inc(q["made_count"], 1)
            pool.wait_ge(q["made_count"], 2)
            pool.tensor_copy(kk[:], iot[:]).then_inc(q["made_count"], 1)

            def rstd(mo, ln, i, slot):
                pool.wait_ge(q[f"{ln}_var"], i + 1)
                pool.tensor_tensor(mo[:, slot, 2:3], mo[:, slot, 1:2], cst[:, 0:1], ALU.add).then_inc(q[f"{ln}_eps"], 1)
                pool.wait_ge(q[f"{ln}_eps"], i + 1)
                pool.tensor_tensor(mo[:, slot, 3:4], mo[:, slot, 2:3], cst[:, 1:2], ALU.pow).then_inc(q[f"{ln}_rstd"], 1)

            def tiles(b, more):
                for t in range(T + 1):
                    if t + 2 < T or (more and t < T):
                        rstd(mo1, "ln1", b * T + t + 2, t % 2)
                    if t >= 1:
                        rstd(mo2, "ln2", b * T + t - 1, (t - 1) % 2)

            rstd(mo1, "ln1", 0, 0)
            rstd(mo1, "ln1", 1, 1)
            with pool.Fori(0, B - 1) as b:
                tiles(b, True)
            tiles(B - 1, False)
            pool.wait_ge(q["r_zero"], 1)
            pool.iota(rec[:, :, :, 1].bitcast(I32), pattern=[[0, 2], [P, NT]], base=0, channel_multiplier=1).then_inc(q["r_tokens"], 1)
            pool.wait_ge(q["r_tokens"], 1)
            pool.wait_ge(q["r_zeroed"], 16)
            with pool.Fori(0, NT // 2) as n:
                for k in range(4):
                    pool.wait_ge(q[f"r_scat{k}"], n * 16)
                    pool.sem_inc(q["pool_went_on"], 1)
                    pool.tensor_copy(recs[:, k:k + 1, :], rec.rearrange("p k t c -> p (k t) c")[:, bass.ds(4 * n + k, 1), :]).then_inc(q["r_copied"], 1)
                    pool.wait_ge(q["r_copied"], 4 * n + k + 1)
                    pool.sem_inc(q["pool_went_on"], 1)
                    pool.indirect_dma_start(out=slot_dram, out_offset=bass.IndirectOffsetOnAxis(ap=recs[:, k, 0:1].bitcast(U32), axis=0),
                                            in_=recs[:, k, 1:3], in_offset=None).then_inc(q[f"r_scat{k}"], 16)

            att_b = att_dram.rearrange("(b t p) d -> b p t d", p=P, t=T)
            with pool.Fori(0, B) as b:
                for g in range(NG):
                    pool.wait_ge(q["f_o_fin"], b * NG + g + 1)
                    pool.sem_inc(q["pool_went_on"], 1)
                    pool.dma_start(att_b[b][:, :, g * P:(g + 1) * P], tmp[g % 2]).then_inc(q[f"f_att_out{g % 2}"], 16)

            pool.wait_ge(q["in_list"], 16)
            pool.wait_ge(q["f_pv"], B * NG)
            pool.wait_ge(q["f_ot"], B * NG)
            with pool.Fori(0, NB // 2) as n:
                for k in range(2):
                    i = 2 * n + k
                    pool.wait_ge(q[f"m_rows{k}"], n * 16)
                    pool.sem_inc(q["pool_went_on"], 1)
                    pool.tensor_copy(idx[:, k:k + 1], lst[:, bass.ds(i, 1), 0].bitcast(U32)).then_inc(q["m_idx"], 1)
                    pool.wait_ge(q["m_idx"], i + 1)
                    pool.wait_ge(q["m_tr"], 2 * n)
                    pool.sem_inc(q["pool_went_on"], 1)
                    pool.indirect_dma_start(out=rows[k], out_offset=None, in_=h2_dram,
                                            in_offset=bass.IndirectOffsetOnAxis(ap=idx[:, k:k + 1], axis=0)).then_inc(q[f"m_rows{k}"], 16)
            for k in range(2):
                pool.wait_ge(q[f"m_out{k}"], 16 * NB // 2)
            with pool.Fori(0, NT // 2) as n:
                for k in range(2):
                    i = 2 * n + k
                    pool.wait_ge(q[f"c_g{k}"], n * 32)
                    pool.wait_ge(q["c_sum"], 2 * n)
                    pool.sem_inc(q["pool_went_on"], 1)
                    for a in range(2):
                        pool.tensor_copy(idx[:, 2 * k + a:2 * k + a + 1], rec[:, a, bass.ds(i, 1), 0].bitcast(U32)).then_inc(q["c_idx"], 1)
                    pool.wait_ge(q["c_idx"], 2 * i + 2)
                    pool.sem_inc(q["pool_went_on"], 1)
                    for a in range(2):
                        pool.indirect_dma_start(out=fin[k][2 + a], out_offset=None, in_=yb_dram,
                                                in_offset=bass.IndirectOffsetOnAxis(ap=idx[:, 2 * k + a:2 * k + a + 1], axis=0)).then_inc(q[f"c_g{k}"], 16)

        @block.scalar
        def _(act):
            act.dma_start(est[0:E, :, :], ctx.rearrange("b e d -> e b d")).then_inc(q["in_ctx"], 16)
            act.dma_start(bqc[:], bq.rearrange("(c p) -> p c", p=P), allow_slow_non_contiguous=True).then_inc(q["in_bias"], 16)
            act.dma_start(bkc[:], bk.rearrange("(c p) -> p c", p=P), allow_slow_non_contiguous=True).then_inc(q["in_bias"], 16)
            act.dma_start(bv_all[:], bv.rearrange("(a n) -> a n", a=1).broadcast_to([P, D])).then_inc(q["in_bias"], 16)
            act.dma_start(bg_all[:], b_gate.rearrange("(a n) -> a n", a=1).broadcast_to([P, NE])).then_inc(q["in_bg"], 16)
            act.dma_start(gws[:], w_gate.rearrange("(c p) n -> p c n", p=P)).then_inc(q["in_bias"], 16)

            def hi(n, out, src, bias=0.0):
                act.wait_ge(q["set_full"], n + 1)
                act.activation(out, src, ACT.Identity, bias=bias).then_inc(q["set_hi"], 1)

            act.wait_ge(q["in_wk"], 16)
            act.copy(wkp[0], wst[1]).then_inc(q["w_hi"], 1)
            for m in range(C):
                hi(n_wqT + m, wqT[0][:, m, :], bank[m][:])
            for m in range(C):
                hi(n_wkT + m, wkT[0][:, m, :], bank[C + m][:])
            for b in range(B):
                hi(n_eT + b, eT[0][:, :, b * W:b * W + E], bank[b][:, 0:C * W].rearrange("p (c w) -> p c w", c=C)[:, :, 0:E])
            act.wait_ge(q["in_wv"], 16)
            act.copy(wvp[0], wst[2]).then_inc(q["w_hi"], 1)
            act.wait_ge(q["in_bias"], 64)
            act.copy(gw[0], gws[:]).then_inc(q["w_hi"], 1)
            act.wait_ge(q["made_ones"], 3)
            for c in range(C):
                act.activation(bqrep[0][:, c, :], ones[:], ACT.Identity, scale=bqc[:, c:c + 1]).then_inc(q["w_hi"], 1)
            for m in range(C):
                for f in range(2):
                    n = n_KE + 2 * m + f
                    hi(n, KE[0][:, m, f * HB * W:(f + 1) * HB * W], bank[n % 8][:, 0:HB * W], bkc[:, m:m + 1])
            for m in range(C):
                hi(n_A + m, A[0][:, m, :], bank[(n_A + m) % 8][:])
            for k in range(2 * C):
                m, f = k // 2, k % 2
                act.wait_ge(q["set_staged"], 2 * k + 2)
                act.copy(G[0][:, m, f * HB * W:(f + 1) * HB * W], gst.rearrange("p b w -> p (b w)")).then_inc(q["set_hi"], 1)
            for b in range(B):
                act.wait_ge(q["set_staged"], 4 * C + b + 1)
                act.copy(vext[0][0:W, b, :], vst[0:W, :]).then_inc(q["set_hi"], 1)

            def h_hi(i, t):
                act.wait_ge(q["h_tr"], i + 1)
                act.copy(hT[t % 2][0].rearrange("p c n -> p (c n)"), bank[0][:]).then_inc(q["hT_hi"], 1)

            def tiles(b, more):
                for t in range(T + 2):
                    i = b * T + t
                    if t < T:
                        act.wait_ge(q["s_max"], i + 1)
                        act.activation(sc[:, t % 2, :], sc[:, t % 2, :], ACT.Exp, bias=col[:, t % 2, 1:2],
                                       accum_out=col[:, t % 2, 2:3]).then_inc(q["s_exp"], 1)
                    if t + 1 < T or (more and t + 1 == T):
                        h_hi(i + 1, t + 1)
                    if 1 <= t <= T:
                        act.wait_ge(q["p_tr"], i)
                        act.copy(pT[0][0:W, :], bank[6][0:W, 0:P]).then_inc(q["pT_hi"], 1)
                    if t >= 2:
                        act.wait_ge(q["h2_tr"], i - 1)
                        act.copy(h2T[t % 2][0].rearrange("p c n -> p (c n)"), bank[0][:]).then_inc(q["h2T_hi"], 1)

            h_hi(0, 0)
            with act.Fori(0, B - 1) as b:
                tiles(b, True)
            tiles(B - 1, False)

            act.wait_ge(q["in_wqkv"], 16)
            act.wait_ge(q["in_fb"], 32)
            act.wait_ge(q["g_full"], NT)
            act.wait_ge(q["route"], 3)
            act.activation(temp[2], temp[1], ACT.Exp).then_inc(q["r_gate"], 1)
            act.mul(bqk[:, 0:C], bqk[:, 0:C], HD ** -0.5).then_inc(q["f_wscaled"], 1)
            act.mul(wqkv[0][:, :, 0:D], wraw[:, :, 0:D], HD ** -0.5).then_inc(q["f_whi"], 1)
            act.copy(wqkv[0][:, :, D:Q3], wraw[:, :, D:Q3]).then_inc(q["f_whi"], 1)

            def qk_hi(b, g):
                for i in range(2):
                    n = dense(g, i)
                    act.wait_ge(q["f_d_full"], b * ND + n + 1)
                    act.wait_ge(q["f_wscaled"], 1)
                    act.wait_ge(q[f"f_stack{g % 2}"], (b * (NG // 2) + g // 2) * STACKED)
                    act.activation(qk[g % 2][i][0], bank[2 + n % 2][:], ACT.Identity,
                                   bias=bqk[:, i * C + g:i * C + g + 1]).then_inc(q["f_qk_hi"], 1)

            def exps(b, k):
                act.wait_ge(q["f_t_full"], b * NH * T + T * max(0, k - 1))
                for t in range(T):
                    n = k * T + t
                    act.wait_ge(q["f_max"], b * NH * T + n + 1)
                    act.activation(PR[k % 2][:, t, :], bank[SB[n % 3]][:], ACT.Exp, bias=nmx[:, k, t:t + 1],
                                   accum_out=Z[:, t, k:k + 1]).then_inc(q["f_exp"], 1)

            def turn(b, k):
                act.wait_ge(q["f_pv"], b * NG + k // HG)
                for c in (0, 2):
                    act.wait_ge(q["f_t_full"], b * NH * T + k * T + c + 1)
                    act.copy(PT[k % HG][:, c, :], bank[0][:]).then_inc(q["f_pt_a"], 1)

            def o_out(b, g):
                act.wait_ge(q["f_pv"], b * NG + g + 1)
                act.wait_ge(q["f_ot"], b * NG + g)
                act.copy(Osb, bank[6][:]).then_inc(q["f_o_sb"], 1)

            with act.Fori(0, B) as b:
                for t in range(T):
                    act.wait_ge(q["f_h_tr"], b * T + t + 1)
                    act.copy(fT[0][:, :, t * P:(t + 1) * P], bank[t % 2][:].rearrange("p (c n) -> p c n", c=C)).then_inc(q["f_hT_hi"], 1)
                qk_hi(b, 0)
                for g in range(NG):
                    exps(b, HG * g)
                    if g:
                        turn(b, HG * g - 1)
                    if g + 1 < NG:
                        qk_hi(b, g + 1)
                    exps(b, HG * g + 1)
                    if g:
                        o_out(b, g - 1)
                    turn(b, HG * g)
                    exps(b, HG * g + 2)
                    turn(b, HG * g + 1)
                    exps(b, HG * g + 3)
                    turn(b, HG * g + 2)
                turn(b, NH - 1)
                o_out(b, NG - 1)

            act.wait_ge(q["f_ot"], B * NG)
            for e in range(NE):
                act.wait_ge(q[f"in_ew{e % 2}"], 16 * (e // 2) + 16)
                act.copy(ew[e][:, 0], eraw[e % 2]).then_inc(q["m_ehi"], 1)

            def rows_hi(i, k):
                act.wait_ge(q["m_tr"], i + 1)
                act.copy(gT[k][:, 0].rearrange("p c n -> p (c n)"), bank[k][:]).then_inc(q["m_hi"], 1)

            def blocks(n, more):
                for k in range(2):
                    i = 2 * n + k
                    if more or k == 0:
                        rows_hi(i + 1, 1 - k)
                    act.wait_ge(q["m_sum"], i + 1)
                    act.activation(ysb[k], ysb[k], ACT.Copy, scale=lst[:, bass.ds(i, 1), 1]).then_inc(q["m_y"], 1)

            rows_hi(0, 0)
            with act.Fori(0, NB // 2 - 1) as n:
                blocks(n, True)
            blocks(NB // 2 - 1, False)

        @block.tensor
        def _(pe):
            pe.wait_ge(q["made_ident"], 2)

            def slot(n):
                if n >= 8:
                    pe.wait_ge(q["set_free"], n - 7)
                return bank[n % 8]

            for n0, src, name in ((n_wqT, 0, "in_wq"), (n_wkT, 1, "in_wk")):
                pe.wait_ge(q[name], 16)
                for m in range(C):
                    o = slot(n0 + m)
                    for c in range(C):
                        last = pe.transpose(o[:, c * P:(c + 1) * P], wst[src][:, c, m * P:(m + 1) * P], ident[:])
                    last.then_inc(q["set_full"], 1)
            pe.wait_ge(q["in_ctx"], 16)
            for b in range(B):
                o = slot(n_eT + b)
                for c in range(C):
                    last = pe.transpose(o[:, c * W:c * W + E], est[0:E, b, c * P:(c + 1) * P], ident[0:E, 0:E])
                last.then_inc(q["set_full"], 1)
            pe.wait_ge(q["w_ready"], 1)
            pe.wait_ge(q["made_ones"], 3)
            pe.wait_ge(q["set_free"], n_KE)
            half = [slice(f * HB * W, (f + 1) * HB * W) for f in range(2)]
            sl = slice(None)
            for m in range(C):
                for f in range(2):
                    o = slot(n_KE + 2 * m + f)
                    for c in range(C):
                        last = prod3(pe, o[:, 0:HB * W], at(wkp, sl, c, slice(m * P, (m + 1) * P)), at(eT, sl, c, half[f]),
                                     c == 0, c == C - 1)
                    last.then_inc(q["set_full"], 1)
            for m in range(C):
                o = slot(n_A + m)
                for c in range(C):
                    last = prod3(pe, o[:], at(wqT, sl, c, slice(m * P, (m + 1) * P)), at(wkT, sl, c), c == 0, c == C - 1)
                last.then_inc(q["set_full"], 1)
            pe.wait_ge(q["w_ready"], 3 + C)
            o = slot(n_cq)
            for m in range(C):
                for c in range(C):
                    last = prod3(pe, o[:, 2 * m:2 * m + 2], at(wkT, sl, c, slice(m * P, (m + 1) * P)),
                                 at(bqrep, sl, c, slice(0, 2)), c == 0, c == C - 1)
            last.then_inc(q["set_full"], 1)
            pe.wait_ge(q["set_free"], n_A)
            for m in range(C):
                for f in range(2):
                    o = slot(n_G + 2 * m + f)
                    for c in range(C):
                        last = prod3(pe, o[:, 0:HB * W], at(wqT, sl, c, slice(m * P, (m + 1) * P)), at(KE, sl, c, half[f]),
                                     c == 0, c == C - 1)
                    last.then_inc(q["set_full"], 1)
            for f in range(2):
                o = slot(n_sb + f)
                for c in range(C):
                    last = prod3(pe, o[:, 0:HB * W], at(bqrep, sl, c), at(KE, sl, c, half[f]), c == 0, c == C - 1)
                last.then_inc(q["set_full"], 1)
            for b in range(B):
                o = slot(n_ve + b)
                for c in range(C):
                    last = prod3(pe, o[0:W, :], at(eT, sl, c, slice(b * W, (b + 1) * W)), at(wvp, sl, c), c == 0, c == C - 1)
                last.then_inc(q["set_full"], 1)

            def t1(i, t):
                pe.wait_ge(q["h_ready"], i + 1)
                for c in range(C):
                    last = pe.transpose(bank[0][:, c * P:(c + 1) * P], h[:, t % 2, c * P:(c + 1) * P], ident[:])
                last.then_inc(q["h_tr"], 1)

            def tiles(b, more):
                for t in range(T + 2):
                    i = b * T + t
                    if t < T:
                        pe.wait_ge(q["hT_ready"], i + 1)
                        for c in range(C):
                            prod3(pe, bank[1][:], at(hT[t % 2], sl, c), at(A, sl, c), c == 0, c == C - 1)
                        for c in range(C):
                            last = prod3(pe, bank[5][:, 0:W], at(hT[t % 2], sl, c), at(G, sl, c, bass.ds(b * W, W)),
                                         c == 0, c == C - 1)
                        last.then_inc(q["s_full"], 1)
                    turned = t + 1 < T or (more and t + 1 == T)
                    if turned:
                        t1(i + 1, t + 1)
                    if 1 <= t <= T:
                        pe.wait_ge(q["p_ready"], i)
                        pe.wait_ge(q["g_copied"], b * T + max(0, t - 2))
                        pe.transpose(bank[6][0:W, 0:P], sc[:, (t - 1) % 2, :], ident[:]).then_inc(q["p_tr"], 1)
                        pe.wait_ge(q["pT_ready"], i)
                        pe.wait_ge(q["x1_ready"], i - 1)
                        prod3(pe, bank[7][:], (pT[0][0:W, :], pT[1][0:W, :]),
                              (vext[0][0:W].rearrange("p b d -> p (b d)")[:, bass.ds(b * D, D)],
                               vext[1][0:W].rearrange("p b d -> p (b d)")[:, bass.ds(b * D, D)]),
                              True, True).then_inc(q["e_full"], 1)
                    if t < T:
                        for c in range(C):
                            last = prod3(pe, bank[3 + t % 2][:], at(hT[t % 2], sl, c), at(wvp, sl, c), c == 0, c == C - 1)
                        last.then_inc(q["v_full"], 1)
                    if t >= 2:
                        pe.wait_ge(q["h2_ready"], i - 1)
                        if turned:
                            pe.wait_ge(q["hT_ready"], i + 2)
                        elif more and t == T:
                            pe.wait_ge(q["hT_ready"], i + 1)
                        for c in range(C):
                            last = pe.transpose(bank[0][:, c * P:(c + 1) * P], h2[:, t % 2, c * P:(c + 1) * P], ident[:])
                        last.then_inc(q["h2_tr"], 1)
                        pe.wait_ge(q["h2T_ready"], i - 1)
                        pe.wait_ge(q["g_copied"], i - 2)
                        for c in range(C):
                            last = prod3(pe, bank[6][:, 256:256 + NE], at(h2T[t % 2], sl, c), at(gw, sl, c), c == 0, c == C - 1)
                        last.then_inc(q["g_full"], 1)

            pe.wait_ge(q["set_free"], n_end)
            t1(0, 0)
            with pe.Fori(0, B - 1) as b:
                tiles(b, True)
            tiles(B - 1, False)

            pe.wait_ge(q["route"], N_PICKED)
            pe.matmul(bank[2][:, 0:NT * NE], tri[:], temp[9].rearrange("p t e -> p (t e)"), start=True, stop=True)
            pe.matmul(bank[2][:, NT * NE:2 * NT * NE], ones[:], temp[9].rearrange("p t e -> p (t e)"), start=True, stop=True).then_inc(q["r_pref"], 1)
            pe.wait_ge(q["f_wready"], 2)

            def qk_project(b, g):
                for i in range(2):
                    n = dense(g, i)
                    pe.wait_ge(q["f_proj"], b * ND + max(0, n - 1))
                    for c in range(C):
                        last = prod3(pe, bank[2 + n % 2][:], at(wqkv, sl, c, slice(i * D + g * P, i * D + (g + 1) * P)),
                                     at(fT, sl, c), c == 0, c == C - 1)
                    last.then_inc(q["f_d_full"], 1)

            def scores(b, k):
                g, j = k // HG, k % HG
                if j == 0:
                    pe.wait_ge(q[f"f_stack{g % 2}"], (b * (NG // 2) + g // 2) * STACKED + STACKED)
                for t in range(T):
                    n = k * T + t
                    pe.wait_ge(q["f_exp"], b * NH * T + max(0, n - 2))
                    pe.matmul(bank[SB[n % 3]][:], QS[g % 2][:, j, t * P:(t + 1) * P], KS[g % 2][:, j, :],
                              start=True, stop=True).then_inc(q["f_s_full"], 1)

            def turn(b, k):
                pe.wait_ge(q["f_exp"], b * NH * T + k * T + T)
                for c in range(T):
                    pe.wait_ge(q[("f_pt_a", "f_pt_d")[c % 2]], b * 2 * NH + 2 * k + c // 2)
                    for t in range(T):
                        last = pe.transpose(bank[c % 2][:, t * P:(t + 1) * P], PR[k % 2][:, t, c * P:(c + 1) * P], ident[:])
                    last.then_inc(q["f_t_full"], 1)

            def pv(b, g):
                pe.wait_ge(q["f_pt_a"], b * 2 * NH + 2 * HG * (g + 1))
                pe.wait_ge(q["f_pt_d"], b * 2 * NH + 2 * HG * (g + 1))
                pe.wait_ge(q["f_proj"], b * ND + 2 + T)
                pe.wait_ge(q["f_o_fin"], b * NG + g)
                for c in range(T):
                    for j in range(HG):
                        k = g * HG + j
                        last = pe.matmul(bank[6][j * HD:(j + 1) * HD, :], V[:, c, k * HD:(k + 1) * HD], PT[j][:, c, :],
                                         start=(c == 0), stop=(c == T - 1))
                last.then_inc(q["f_pv"], 1)

            def o_turn(b, g):
                pe.wait_ge(q["f_o_sb"], b * NG + g + 1)
                for t in range(T):
                    last = pe.transpose(bank[6][:, t * P:(t + 1) * P], Osb[:, t * P:(t + 1) * P], ident[:])
                last.then_inc(q["f_ot"], 1)

            with pe.Fori(0, B) as b:
                for t in range(T):
                    pe.wait_ge(q[f"f_raw{t % 2}"], b * 32 + 16 * (t // 2) + 16)
                    if t < 2:
                        pe.wait_ge(q[("f_pt_a", "f_pt_d")[t]], b * 2 * NH)
                    else:
                        pe.wait_ge(q["f_hT_ready"], b * T + t - 1)
                    for c in range(C):
                        last = pe.transpose(bank[t % 2][:, c * P:(c + 1) * P], h2f[:, t % 2, c * P:(c + 1) * P], ident[:])
                    last.then_inc(q["f_h_tr"], 1)
                pe.wait_ge(q["f_hT_ready"], b * T + T)
                qk_project(b, 0)
                for t in range(T):
                    n = 2 + t
                    pe.wait_ge(q["f_proj"], b * ND + n - 1)
                    for c in range(C):
                        last = prod3(pe, bank[2 + n % 2][:], at(fT, sl, c, slice(t * P, (t + 1) * P)),
                                     at(wqkv, sl, c, slice(2 * D, Q3)), c == 0, c == C - 1)
                    last.then_inc(q["f_d_full"], 1)
                for g in range(NG):
                    scores(b, HG * g)
                    if g:
                        turn(b, HG * g - 1)
                    if g + 1 < NG:
                        qk_project(b, g + 1)
                    if g:
                        pv(b, g - 1)
                    scores(b, HG * g + 1)
                    turn(b, HG * g)
                    if g:
                        o_turn(b, g - 1)
                    scores(b, HG * g + 2)
                    turn(b, HG * g + 1)
                    scores(b, HG * g + 3)
                    turn(b, HG * g + 2)
                turn(b, NH - 1)
                pv(b, NG - 1)
                o_turn(b, NG - 1)

            def rows_turn(i, k):
                pe.wait_ge(q[f"m_rows{k}"], (i - k) * 8 + 16)
                for c in range(C):
                    last = pe.transpose(bank[k][:, c * P:(c + 1) * P], rows[k][:, c * P:(c + 1) * P], ident[:])
                last.then_inc(q["m_tr"], 1)

            def blocks(n, more):
                for k in range(2):
                    i = 2 * n + k
                    if more or k == 0:
                        pe.wait_ge(q["m_hT"], i)
                        rows_turn(i + 1, 1 - k)
                    pe.wait_ge(q["m_hT"], i + 1)
                    if k == 0:
                        pe.wait_ge(q["m_sum"], 2 * n)
                    else:
                        pe.wait_ge(q["m_sum"], 2 * n)
                    e = pe.value_load(bexp[0:1, bass.ds(i, 1)], min_val=0, max_val=NE - 1)
                    for c in range(C):
                        last = prod3(pe, bank[2 + k][:], (gT[k][:, 0, c], gT[k][:, 1, c]),
                                     (parts[:, bass.ds(e * EW + c * D, D)], parts[:, bass.ds(e * EW + (C + c) * D, D)]), c == 0, c == C - 1)
                    last.then_inc(q["m_full"], 1)

            pe.wait_ge(q["f_o_fin"], B * NG)
            rows_turn(0, 0)
            pe.wait_ge(q["m_elo"], NE)
            with pe.Fori(0, NB // 2 - 1) as n:
                blocks(n, True)
            blocks(NB // 2 - 1, False)

        @block.vector
        def _(dve):
            def lo(n, out, src, high, bias=None):
                dve.wait_ge(q["set_hi"], n + 1)
                if bias is None:
                    ins = dve.tensor_tensor(out, src, full(high), ALU.subtract)
                else:
                    ins = dve.scalar_tensor_tensor(out=out, in0=src, scalar=bias, in1=full(high), op0=ALU.add, op1=ALU.subtract)
                return ins

            dve.wait_ge(q["w_hi"], 1)
            dve.tensor_tensor(wkp[1], wst[1], full(wkp[0]), ALU.subtract).then_inc(q["w_ready"], 1)
            for m in range(C):
                lo(m, wqT[1][:, m, :], bank[m][:], wqT[0][:, m, :]).then_inc(q["set_free"], 1)
            for m in range(C):
                lo(n_wkT + m, wkT[1][:, m, :], bank[C + m][:], wkT[0][:, m, :]).then_inc(q["set_free"], 1)
            for b in range(B):
                cols = slice(b * W, b * W + E)
                lo(n_eT + b, eT[1][:, :, cols], bank[b][:, 0:C * W].rearrange("p (c w) -> p c w", c=C)[:, :, 0:E],
                   eT[0][:, :, cols]).then_inc(q["set_free"], 1)
            dve.wait_ge(q["w_hi"], 2)
            dve.tensor_tensor(wvp[1], wst[2], full(wvp[0]), ALU.subtract).then_inc(q["w_ready"], 1)
            dve.wait_ge(q["w_hi"], 3)
            dve.tensor_tensor(gw[1], gws[:], full(gw[0]), ALU.subtract).then_inc(q["w_ready"], 1)
            for c in range(C):
                dve.wait_ge(q["w_hi"], 4 + c)
                dve.scalar_tensor_tensor(out=bqrep[1][:, c, :], in0=ones[:], scalar=bqc[:, c:c + 1], in1=full(bqrep[0][:, c, :]),
                                         op0=ALU.mult, op1=ALU.subtract).then_inc(q["w_ready"], 1)
            for m in range(C):
                for f in range(2):
                    n = n_KE + 2 * m + f
                    cols = slice(f * HB * W, (f + 1) * HB * W)
                    lo(n, KE[1][:, m, cols], bank[n % 8][:, 0:HB * W], KE[0][:, m, cols], bkc[:, m:m + 1]).then_inc(q["set_free"], 1)
            for m in range(C):
                n = n_A + m
                lo(n, A[1][:, m, :], bank[n % 8][:], A[0][:, m, :]).then_inc(q["set_free"], 1)
            dve.wait_ge(q["set_full"], n_cq + 1)
            dve.tensor_copy(cq[:], bank[n_cq % 8][:, 0:2 * C]).then_inc(q["set_free"], 1)
            dve.wait_ge(q["set_free"], n_cq + 1)
            flat = gst.rearrange("p b w -> p (b w)")
            for k in range(2 * C):
                n, m, f = n_G + k, k // 2, k % 2
                cols = slice(f * HB * W, (f + 1) * HB * W)
                dve.wait_ge(q["set_full"], n + 1)
                dve.wait_ge(q["set_free"], n)
                dve.tensor_copy(flat, bank[n % 8][:, 0:HB * W]).then_inc(q["set_staged"], 1)
                dve.wait_ge(q["set_staged"], 2 * k + 1)
                dve.tensor_scalar(gst[:, :, E:W], gst[:, :, E:W], cq[:, 2 * m:2 * m + 1], None, ALU.add).then_inc(q["set_staged"], 1)
                lo(n - 1, G[1][:, m, cols], flat, G[0][:, m, cols]).then_inc(q["set_free"], 1)
            for f in range(2):
                n = n_sb + f
                dve.wait_ge(q["set_full"], n + 1)
                dve.tensor_copy(sbias[:, f * HB * W:(f + 1) * HB * W], bank[n % 8][:, 0:HB * W]).then_inc(q["set_free"], 1)
            for b in range(B):
                n = n_ve + b
                dve.wait_ge(q["set_full"], n + 1)
                dve.wait_ge(q["set_free"], n)
                dve.tensor_tensor(vst[0:W, :], bank[n % 8][0:W, :], bv_all[0:W, :], ALU.add).then_inc(q["set_staged"], 1)
                lo(n - 3, vext[1][0:W, b, :], vst[0:W, :], vext[0][0:W, b, :]).then_inc(q["set_free"], 1)

            def norm(ln, i, slot, src, st, mo, f):
                dve.bn_stats(st[:, slot, :], src).then_inc(q[f"{ln}_stats"], 1)
                dve.wait_ge(q[f"{ln}_stats"], i + 1)
                dve.tensor_copy(fence[:, f:f + 1], st[:, slot, 0:1])
                dve.bn_aggr(mo[:, slot, 0:2], st[:, slot, :]).then_inc(q[f"{ln}_var"], 1)

            def normed(ln, i, slot, src, out, mo):
                dve.wait_ge(q[f"{ln}_rstd"], i + 1)
                return dve.tensor_scalar(out, src, mo[:, slot, 0:1], mo[:, slot, 3:4], ALU.subtract, ALU.mult)

            def ln1_a(i, t):
                dve.wait_ge(q[f"x_in{t % T}"], (i - t + T * (t // T)) * (16 // T) + 16)
                norm("ln1", i, t % 2, xin[:, t % T, :], st1, mo1, 0)

            def ln1_b(i, t):
                normed("ln1", i, t % 2, xin[:, t % T, :], h[:, t % 2, :], mo1).then_inc(q["h_ready"], 1)

            def h_lo(i, t):
                dve.wait_ge(q["hT_hi"], i + 1)
                dve.tensor_tensor(hT[t % 2][1].rearrange("p c n -> p (c n)"), bank[0][:],
                                  full(hT[t % 2][0].rearrange("p c n -> p (c n)")), ALU.subtract).then_inc(q["hT_ready"], 1)

            def tiles(b, more):
                for t in range(T + 2):
                    i = b * T + t
                    k = t % 2
                    nxt = t + 2 < T or (more and t < T)
                    if t < T:
                        dve.wait_ge(q["s_full"], i + 1)
                        dve.tensor_tensor(sc[:, k, :], bank[5][:, 0:W], sbias[:, bass.ds(b * W, W)], ALU.add).then_inc(q["s_step"], 1)
                        dve.tensor_tensor_reduce(scr, bank[1][:], h[:, k, :], 1.0, 0.0, ALU.mult, ALU.add,
                                                 col[:, k, 0:1]).then_inc(q["s_step"], 1)
                        dve.wait_ge(q["s_step"], 3 * i + 2)
                        dve.tensor_tensor(sc[:, k, E:W], sc[:, k, E:W], col[:, k, 0:1], ALU.add).then_inc(q["s_step"], 1)
                        dve.wait_ge(q["s_step"], 3 * i + 3)
                        dve.tensor_reduce(col[:, k, 1:2], sc[:, k, :], AX.X, ALU.max, negate=True).then_inc(q["s_max"], 1)
                    if nxt:
                        ln1_a(i + 2, t + 2)
                    if t + 1 < T or (more and t + 1 == T):
                        h_lo(i + 1, t + 1)
                    if 1 <= t <= T:
                        dve.wait_ge(q["pT_hi"], i)
                        dve.tensor_tensor(pT[1][0:W, :], bank[6][0:W, 0:P], full(pT[0][0:W, :]), ALU.subtract).then_inc(q["pT_ready"], 1)
                    if t < T:
                        dve.wait_ge(q["s_exp"], i + 1)
                        dve.reciprocal(col[:, k, 3:4], col[:, k, 2:3]).then_inc(q["s_den"], 1)
                        dve.wait_ge(q["s_den"], i + 1)
                        dve.tensor_scalar(sc[:, k, :], sc[:, k, :], col[:, k, 3:4], None, ALU.mult).then_inc(q["p_ready"], 1)
                    if nxt:
                        ln1_b(i + 2, t + 2)
                    if 1 <= t <= T:
                        u = t - 1
                        dve.wait_ge(q["v_full"], i)
                        dve.wait_ge(q["p_ready"], i)
                        dve.wait_ge(q[f"x1_out{u}"], b * 16)
                        dve.scalar_tensor_tensor(out=x1[:, u, :], in0=bank[3 + u % 2][:], scalar=sc[:, u % 2, E:W],
                                                 in1=xin[:, u, :], op0=ALU.mult, op1=ALU.add).then_inc(q["x1_part"], 1)
                        dve.wait_ge(q["e_full"], i)
                        dve.wait_ge(q["x1_part"], i)
                        dve.tensor_tensor(x1[:, u, :], bank[7][:], x1[:, u, :], ALU.add).then_inc(q["x1_ready"], 1)
                        dve.wait_ge(q["x1_ready"], i)
                        norm("ln2", i - 1, u % 2, x1[:, u, :], st2, mo2, 1)
                        dve.wait_ge(q[f"h2_out{u % 2}"], b * 32 + 16 * (u // 2))
                        dve.wait_ge(q["ln2_rstd"], i)
                        normed("ln2", i - 1, u % 2, x1[:, u, :], h2[:, u % 2, :], mo2).then_inc(q["h2_ready"], 1)
                    if t >= 2:
                        dve.wait_ge(q["h2T_hi"], i - 1)
                        dve.tensor_tensor(h2T[k][1].rearrange("p c n -> p (c n)"), bank[0][:],
                                          full(h2T[k][0].rearrange("p c n -> p (c n)")), ALU.subtract).then_inc(q["h2T_ready"], 1)
                        dve.wait_ge(q["g_full"], i - 1)
                        dve.tensor_copy(glog[:, bass.ds(i - 2, 1), :], bank[6][:, 256:256 + NE].rearrange("p (a n) -> p a n", a=1)).then_inc(q["g_copied"], 1)

            ln1_a(0, 0)
            ln1_b(0, 0)
            ln1_a(1, 1)
            ln1_b(1, 1)
            h_lo(0, 0)
            with dve.Fori(0, B - 1) as b:
                tiles(b, True)
            tiles(B - 1, False)

            route = [0]

            def then(ins):
                ins.then_inc(q["route"], 1)
                route[0] += 1
                dve.wait_ge(q["route"], route[0])

            t_lg, t_ex, t_gate, t_first, t_second, t_eq, t_place, t_in, t_sel = (temp[i] for i in (1, 2, 3, 4, 5, 6, 7, 8, 9))
            row = temp[0].rearrange("p t e -> p (t e)")
            mx, den, tie, desc = row[:, 0:NT], row[:, NT:2 * NT], row[:, 2 * NT:3 * NT], row[:, 3 * NT:3 * NT + NE]
            gates = [row[:, 4 * NT:5 * NT], row[:, 5 * NT:6 * NT]]

            def wide(v):
                return v.unsqueeze(2).broadcast_to([P, NT, NE])

            def every(v):
                return v.unsqueeze(1).broadcast_to([P, NT, NE])

            dve.wait_ge(q["g_copied"], NT)
            dve.wait_ge(q["in_bg"], 16)
            dve.wait_ge(q["made_count"], 3)
            then(dve.tensor_tensor(t_lg, glog[:], every(bg_all[:]), ALU.add))
            then(dve.tensor_reduce(mx, t_lg, AX.X, ALU.max))
            then(dve.tensor_tensor(t_lg, t_lg, wide(mx), ALU.subtract))
            then(dve.tensor_scalar(desc, kk[:, 0:NE], -1.0, float(NE), ALU.mult, ALU.add))
            dve.wait_ge(q["r_gate"], 1)
            then(dve.tensor_reduce(den, t_ex, AX.X, ALU.add))
            then(dve.reciprocal(den, den))
            then(dve.tensor_tensor(t_gate, t_ex, wide(den), ALU.mult))

            def pick(gate, out, choice):
                then(dve.tensor_reduce(out, gate, AX.X, ALU.max))
                then(dve.tensor_tensor(t_eq, gate, wide(out), ALU.is_equal))
                then(dve.tensor_tensor(t_eq, t_eq, every(desc), ALU.mult))
                then(dve.tensor_reduce(tie, t_eq, AX.X, ALU.max))
                then(dve.tensor_tensor(choice, t_eq, wide(tie), ALU.is_equal))

            pick(t_gate, gates[0], t_first)
            then(dve.scalar_tensor_tensor(out=t_gate, in0=t_first, scalar=-2.0, in1=t_gate, op0=ALU.mult, op1=ALU.add))
            pick(t_gate, gates[1], t_second)
            then(dve.tensor_tensor(t_sel, t_first, t_second, ALU.add))
            assert route[0] == N_PICKED
            dve.wait_ge(q["r_pref"], 1)
            tot = bank[2][:, NT * NE:2 * NT * NE].rearrange("p (t e) -> p t e", e=NE)
            then(dve.tensor_copy(t_in, tot))
            run, nxt, s = t_in, t_lg, 1
            while s < NT:
                then(dve.tensor_copy(nxt[:, 0:s], run[:, 0:s]))
                then(dve.tensor_tensor(nxt[:, s:NT], run[:, s:NT], run[:, 0:NT - s], ALU.add))
                run, nxt, s = nxt, run, 2 * s
            k128 = sm[:, 0:NT]
            then(dve.tensor_scalar(k128, kk[:, 0:NT], float(P), None, ALU.mult))
            cmp = t_eq.rearrange("p t e -> p (t e)").rearrange("p (e t) -> p e t", t=NT)
            then(dve.tensor_tensor(cmp, run[:, NT - 1, :].unsqueeze(2).broadcast_to([P, NE, NT]),
                                   k128.unsqueeze(1).broadcast_to([P, NE, NT]), ALU.is_gt))
            small = [sm[:, 2 * NT + NE * i:2 * NT + NE * (i + 1)] for i in range(4)]
            blk = small[0]
            then(dve.tensor_reduce(blk, cmp, AX.X, ALU.add))
            cur, oth, s = small[1], small[2], 1
            then(dve.tensor_copy(cur, blk))
            while s < NE:
                then(dve.tensor_copy(oth[:, 0:s], cur[:, 0:s]))
                then(dve.tensor_tensor(oth[:, s:NE], cur[:, s:NE], cur[:, 0:NE - s], ALU.add))
                cur, oth, s = oth, cur, 2 * s
            start, base = oth, small[3]
            then(dve.tensor_tensor(start, cur, blk, ALU.subtract))
            then(dve.tensor_scalar(base, start, float(P), None, ALU.mult))
            then(dve.tensor_tensor(t_place, run, tot, ALU.subtract))
            then(dve.tensor_tensor(t_place, t_place, bank[2][:, 0:NT * NE].rearrange("p (t e) -> p t e", e=NE), ALU.add))
            then(dve.tensor_tensor(t_place, t_place, every(base), ALU.add))
            for a, choice in enumerate((t_first, t_second)):
                then(dve.tensor_tensor(t_eq, choice, t_place, ALU.mult))
                then(dve.tensor_reduce(mx, t_eq, AX.X, ALU.add))
                then(dve.tensor_copy(rec[:, a, :, 0].bitcast(U32), mx))
                then(dve.tensor_copy(rec[:, a, :, 2], gates[a]))
            big = area(plain, 3 * C * D + 8 * D + NT * NE, NB, NE)
            bsum = row[:, 0:NB]
            then(dve.tensor_tensor(big, kk[:].unsqueeze(2).broadcast_to([P, NB, NE]), start.unsqueeze(1).broadcast_to([P, NB, NE]), ALU.is_ge))
            then(dve.tensor_reduce(bsum, big, AX.X, ALU.add))
            then(dve.tensor_scalar(bexp, bsum, -1.0, None, ALU.add))
            dve.memset(lst, 0.0).then_inc(q["r_zero"], 1)

            dve.wait_ge(q["f_whi"], 1)
            dve.scalar_tensor_tensor(out=wqkv[1][:, :, 0:D], in0=wraw[:, :, 0:D], scalar=HD ** -0.5, in1=full(wqkv[0][:, :, 0:D]),
                                     op0=ALU.mult, op1=ALU.subtract).then_inc(q["f_wready"], 1)
            dve.wait_ge(q["f_whi"], 2)
            dve.tensor_tensor(wqkv[1][:, :, D:Q3], wraw[:, :, D:Q3], full(wqkv[0][:, :, D:Q3]), ALU.subtract).then_inc(q["f_wready"], 1)

            def qk_lo(b, g):
                for i in range(2):
                    n = dense(g, i)
                    dve.wait_ge(q["f_qk_hi"], (b * NG + g) * 2 + i + 1)
                    dve.scalar_tensor_tensor(out=qk[g % 2][i][1], in0=bank[2 + n % 2][:], scalar=bqk[:, i * C + g:i * C + g + 1],
                                             in1=full(qk[g % 2][i][0]), op0=ALU.add, op1=ALU.subtract).then_inc(q["f_proj"], 1)

            def maxes(b, k):
                for t in range(T):
                    n = k * T + t
                    dve.wait_ge(q["f_s_full"], b * NH * T + n + 1)
                    dve.tensor_reduce(nmx[:, k, t:t + 1], bank[SB[n % 3]][:], AX.X, ALU.max, negate=True).then_inc(q["f_max"], 1)

            def turn(b, k):
                dve.wait_ge(q["f_pv"], b * NG + k // HG)
                for c in (1, 3):
                    dve.wait_ge(q["f_t_full"], b * NH * T + k * T + c + 1)
                    dve.tensor_copy(PT[k % HG][:, c, :], bank[1][:]).then_inc(q["f_pt_d"], 1)

            def finish(b, g):
                hs = slice(g * HG, (g + 1) * HG)
                dve.wait_ge(q["f_exp"], b * NH * T + T * HG * (g + 1))
                dve.reciprocal(rZ[:, :, hs], Z[:, :, hs]).then_inc(q["f_rz"], 1)
                dve.wait_ge(q["f_rz"], b * NG + g + 1)
                dve.wait_ge(q["f_ot"], b * NG + g + 1)
                dve.wait_ge(q[f"f_att_out{g % 2}"], b * 32 + 16 * (g // 2))
                dve.tensor_tensor(tmp[g % 2].rearrange("p t (j d) -> p t j d", j=HG),
                                  bank[6][:].rearrange("p (t j d) -> p t j d", t=T, j=HG),
                                  rZ[:, :, hs].unsqueeze(3).broadcast_to([P, T, HG, HD]), ALU.mult).then_inc(q["f_o_fin"], 1)

            with dve.Fori(0, B) as b:
                for t in range(T):
                    dve.wait_ge(q["f_hT_hi"], b * T + t + 1)
                    cols = slice(t * P, (t + 1) * P)
                    ins = dve.tensor_tensor(fT[1][:, :, cols], bank[t % 2][:].rearrange("p (c n) -> p c n", c=C),
                                            full(fT[0][:, :, cols]), ALU.subtract)
                    ins.then_inc(q["f_hT_ready"], 1)
                qk_lo(b, 0)
                for t in range(T):
                    n = 2 + t
                    dve.wait_ge(q["f_d_full"], b * ND + n + 1)
                    dve.tensor_tensor(V[:, t, :], bank[2 + n % 2][:], bvf[:], ALU.add).then_inc(q["f_proj"], 1)
                for g in range(NG):
                    maxes(b, HG * g)
                    if g:
                        turn(b, HG * g - 1)
                    if g + 1 < NG:
                        qk_lo(b, g + 1)
                    maxes(b, HG * g + 1)
                    turn(b, HG * g)
                    if g:
                        finish(b, g - 1)
                    maxes(b, HG * g + 2)
                    turn(b, HG * g + 1)
                    maxes(b, HG * g + 3)
                    turn(b, HG * g + 2)
                turn(b, NH - 1)
                finish(b, NG - 1)

            for e in range(NE):
                dve.wait_ge(q["m_ehi"], e + 1)
                dve.tensor_tensor(ew[e][:, 1], eraw[e % 2], full(ew[e][:, 0]), ALU.subtract).then_inc(q["m_elo"], 1)

            def rows_lo(i, k):
                dve.wait_ge(q["m_hi"], i + 1)
                dve.tensor_tensor(gT[k][:, 1].rearrange("p c n -> p (c n)"), bank[k][:],
                                  full(gT[k][:, 0].rearrange("p c n -> p (c n)")), ALU.subtract).then_inc(q["m_hT"], 1)

            def blocks(n, more):
                for k in range(2):
                    i = 2 * n + k
                    if more or k == 0:
                        rows_lo(i + 1, 1 - k)
                    e = dve.value_load(bexp[0:1, bass.ds(i, 1)], min_val=0, max_val=NE - 1)
                    dve.wait_ge(q["m_full"], i + 1)
                    dve.wait_ge(q[f"m_out{k}"], n * 16)
                    dve.tensor_tensor(ysb[k], bank[2 + k][:], be_all[:, bass.ds(e * D, D)], ALU.add).then_inc(q["m_sum"], 1)

            dve.wait_ge(q["in_be"], 16)
            dve.wait_ge(q["in_list"], 16)
            rows_lo(0, 0)
            with dve.Fori(0, NB // 2 - 1) as n:
                blocks(n, True)
            blocks(NB // 2 - 1, False)

            with dve.Fori(0, NT // 2) as n:
                for k in range(2):
                    i = 2 * n + k
                    dve.wait_ge(q[f"c_x{k}"], 16 * n + 16)
                    dve.wait_ge(q[f"c_a{k}"], 16 * n + 16)
                    dve.tensor_tensor(fin[k][0], fin[k][0], fin[k][1], ALU.add).then_inc(q["c_pair"], 1)
                    dve.wait_ge(q[f"c_g{k}"], 32 * n + 32)
                    dve.tensor_tensor(fin[k][2], fin[k][2], fin[k][3], ALU.add).then_inc(q["c_pair"], 1)
                    dve.wait_ge(q["c_pair"], 2 * i + 2)
                    dve.tensor_tensor(fin[k][0], fin[k][0], fin[k][2], ALU.add).then_inc(q["c_sum"], 1)


_INS = ("x", "ctx_1024", "L0_xattn_Wq", "L0_xattn_bq", "L0_xattn_Wk", "L0_xattn_bk", "L0_xattn_Wv", "L0_xattn_bv",
        "L0_ffn_W_qkv", "L0_ffn_b_qkv", "L0_ffn_W_gate", "L0_ffn_b_gate", "L0_ffn_W_experts", "L0_ffn_b_experts")
_OUTS = (((8, 512, 512), "float32"),)


def kernel(**inputs):
    import numpy as _np
    import concourse.bacc as _bacc
    from concourse import mybir as _mybir
    from concourse.bass_utils import run_bass_kernel_spmd as _run

    nc = _bacc.Bacc("TRN2", target_bir_lowering=False, num_devices=1)
    arrays, args = {}, []
    for name in _INS:
        a = _np.ascontiguousarray(inputs[name])
        arrays[f"in_{name}_dram"] = a
        args.append(nc.dram_tensor(f"in_{name}_dram", a.shape, _mybir.dt.from_np(a.dtype), kind="ExternalInput").ap())
    for i, (shape, dtype) in enumerate(_OUTS):
        dt = _mybir.dt.from_np(_np.dtype(dtype))
        args.append(nc.dram_tensor(f"out_{i}_dram", shape, dt, kind="ExternalOutput").ap())
    program(nc, *args)
    r = _run(nc, [arrays], core_ids=[0])
    got = tuple(r.results[0][f"out_{i}_dram"] for i in range(len(_OUTS)))
    return got[0]
```

```python
from contextlib import ExitStack
import numpy as np
import concourse.bass as bass
from concourse import mybir

P = 128
ALU = mybir.AluOpType
ACT = mybir.ActivationFunctionType
AX = mybir.AxisListType
F32 = mybir.dt.float32
F32R = mybir.dt.float32r
U32 = mybir.dt.uint32
I32 = mybir.dt.int32


def program(nc, x, ctx, wq, bq, wk, bk, wv, bv, w_qkv, b_qkv, w_gate, b_gate, w_exp, b_exp, out):
    B, S, D = x.shape
    E = ctx.shape[1]
    C = D // P
    T = S // P
    W = E + 1
    HB = B // 2
    NE = w_gate.shape[1]
    EPS = 1e-5
    NB = B * T * 2 + NE - 1
    NB += NB % 2
    x1_dram = nc.dram_tensor("x1_rows", (B * S, D), F32, kind="Internal").ap()
    h2_dram = nc.dram_tensor("h2_rows", (B * S, D), F32, kind="Internal").ap()
    att_dram = nc.dram_tensor("attention_rows", (B * S, D), F32, kind="Internal").ap()
    slot_dram = nc.dram_tensor("slot_list", (NB * P, 2), F32, kind="Internal").ap()
    yb_dram = nc.dram_tensor("expert_rows", (NB * P, D), F32, kind="Internal").ap()
    with ExitStack() as stack:
        def sb(name, shape, dt=F32):
            return stack.enter_context(nc.sbuf_tensor(name, shape, dt))

        def sem(name):
            return stack.enter_context(nc.semaphore(name))

        bank = [stack.enter_context(nc.psum_tensor(f"bank{i}", [P, 512], F32)) for i in range(8)]
        PARTS, PLAIN = 34816, 15872
        parts = sb("parts", [P, PARTS], F32R)
        plain = sb("plain", [P, PLAIN])

        def area(arena, at, *shape):
            n = int(np.prod(shape))
            assert at + n <= (PARTS if arena is parts else PLAIN), (at, n)
            v = arena[:, at:at + n]
            if len(shape) == 2:
                v = v.rearrange("p (a b) -> p a b", a=shape[0])
            if len(shape) == 3:
                v = v.rearrange("p (a b c) -> p a b c", a=shape[0], b=shape[1])
            return v

        def pair(at, *shape):
            n = int(np.prod(shape))
            return area(parts, at, *shape), area(parts, at + n, *shape)

        def full(part):
            return part.bitcast(F32)

        CTX = C * B * W
        wqT = pair(0, C, D)
        wkT = pair(2 * C * D, C, D)
        vext = pair(0, B, D)
        wkp = pair(4 * C * D, C, D)
        A = pair(4 * C * D, C, D)
        wvp = pair(6 * C * D, C, D)
        r0 = 8 * C * D
        G = pair(r0, C, B * W)
        KE = pair(r0 + 2 * CTX, C, B * W)
        eT = pair(r0 + 4 * CTX, C, B * W)
        hT = [pair(r0 + 4 * CTX + 2 * C * P * i, C, P) for i in range(2)]
        h2T = [pair(r0 + 4 * CTX + 2 * C * P * (2 + i), C, P) for i in range(2)]
        pT = pair(r0 + 4 * CTX + 8 * C * P, P)
        gw = pair(r0 + 6 * CTX, C, NE)
        bqrep = pair(r0 + 6 * CTX + 2 * C * NE, C, P)
        wst = [area(plain, C * D * i, C, D) for i in range(3)]
        est = area(plain, 3 * C * D, B, D)
        p0 = 3 * C * D
        x1 = area(plain, p0, T, D)
        h = area(plain, p0 + T * D, 2, D)
        h2 = area(plain, p0 + (T + 2) * D, 2, D)
        p0 += B * D
        vst = area(plain, p0, D)
        gst = area(plain, p0, HB, W)
        scr = area(plain, p0, D)
        bv_all = area(plain, p0 + D, D)
        xin = area(plain, p0 + 2 * D, T, D)
        Q3 = w_qkv.shape[1]
        HD = 32
        NH = D // HD
        HG = P // HD
        NG = NH // HG
        wqkv = pair(0, C, Q3)
        r1 = 2 * C * Q3
        fT = pair(r1, C, S)
        r1 += 2 * C * S
        qkp = [[[area(parts, r1 + S * (4 * i + 2 * m + part), S) for part in range(2)] for m in range(2)] for i in range(2)]
        qk2 = [[parts[:, r1 + S * (4 * i + part):r1 + S * (4 * i + part + 4)].rearrange("p (m x) -> p m x", m=2)[:, :, 0:S]
                for part in range(2)] for i in range(2)]
        r1 += 8 * S
        NSLOT = 5
        stk = [[area(parts, r1 + 2 * S * (2 * s + i), 2, S) for i in range(2)] for s in range(NSLOT)]
        r1 += 4 * S * NSLOT
        h2f = full(area(parts, r1, T, D))
        r1 += T * D
        V = full(area(parts, r1, T, D))
        wraw = area(plain, 0, C, Q3)
        PT = [area(plain, T * S * j, T, S) for j in range(HG)]
        p1 = HG * T * S
        PR = [area(plain, p1 + T * S * i, T, S) for i in range(2)]
        p1 += 2 * T * S
        Vst = area(plain, p1, T, D)
        p1 += T * D
        Osb = area(plain, p1, S)
        tmp = area(plain, p1 + S, T, D // 2)
        bvf = sb("bias_v_all", [P, D])
        bqk = sb("bias_qk_cols", [P, 2 * C])
        nmx = sb("neg_max", [P, NH, T])
        Z = sb("denominators", [P, T, NH])
        rZ = sb("inverse_denominators", [P, T, NH])

        ident = sb("ident", [P, P])
        ones = sb("ones", [P, P])
        sbias = sb("score_bias", [P, B * W])
        bqc = sb("bq_cols", [P, C])
        bkc = sb("bk_cols", [P, C])
        cq = sb("cq", [P, 2 * C])
        gws = sb("gate_stage", [P, C, NE])
        st1 = sb("st1", [P, 2, 6]); st2 = sb("st2", [P, 2, 6])
        mo1 = sb("mo1", [P, 2, 6]); mo2 = sb("mo2", [P, 2, 6])
        cst = sb("consts", [P, 3])
        fence = sb("fence", [P, 8])
        sc = sb("sc", [P, 2, W])
        NB = B * T * 2 + NE - 1
        NB += NB % 2
        NT = B * T
        temp = [area(plain, 3 * C * D + 8 * D + i * NT * NE, NT, NE) for i in range(10)]
        rec = sbias[:, 0:2 * NT * 3].rearrange("p (k t c) -> p k t c", k=2, c=3)
        lst = sbias[:, 6 * NT:6 * NT + 2 * NB].rearrange("p (i c) -> p i c", c=2)
        bexp = sbias[:, 6 * NT + 2 * NB:6 * NT + 3 * NB].bitcast(U32)
        sm = sbias[:, 6 * NT + 3 * NB:6 * NT + 3 * NB + 2 * NT + 6 * NE]
        iot = sb("count_int", [P, NB], I32)
        kk = sb("count", [P, NB])
        tri = sb("strict_triangle", [P, P])
        bg_all = sb("bias_gate_all", [P, NE])
        recs = sb("records", [P, 4, 3])
        idx = sb("row_numbers", [P, 4], U32)
        EW = 2 * C * D
        ew = [area(parts, EW * e, 2, C, D) for e in range(NE)]
        gT = [area(parts, EW * NE + 2 * C * P * i, 2, C, P) for i in range(2)]
        eraw = [area(plain, C * D * i, C, D) for i in range(2)]
        p2 = 2 * C * D
        be_all = area(plain, p2, NE * D)
        p2 += NE * D
        rows = [area(plain, p2 + D * i, D) for i in range(2)]
        ysb = [area(plain, p2 + D * (2 + i), D) for i in range(2)]
        p2 += 4 * D
        fin = [[area(plain, p2 + D * (4 * i + k), D) for k in range(4)] for i in range(2)]
        col = sb("col", [P, 2, 4])
        glog = sb("glog", [P, B * T, NE])

        names = """in_wk in_wq in_wv in_ctx in_bias made_ident made_ones made_consts
        w_hi w_ready set_full set_hi set_staged set_free
        ln1_stats ln1_var ln1_eps ln1_pow ln1_neg ln1_rstd h_ready h_tr hT_hi hT_ready s_full s_step s_max s_exp s_den p_ready p_tr pT_hi pT_ready
        e_full v_full x1_part x1_ready ln2_stats ln2_var ln2_eps ln2_pow ln2_neg ln2_rstd h2_ready h2_tr h2T_hi h2T_ready g_full g_copied
        in_wqkv in_fb f_wscaled f_whi f_wready f_raw f_d_full f_d_hi f_d_free f_v_in
        f_stack0 f_stack1 f_stack2 f_stack3 f_stack4 f_s_full f_max f_exp f_t_full f_pt_a f_pt_d f_pv f_o_sb f_ot f_rz f_o_fin x_in0 x_in1 x_in2 x_in3 in_bg sp_went_on pool_went_on made_count route r_gate r_pref r_zero r_zeroed r_tokens r_copied r_scat0 r_scat1 r_scat2 r_scat3 in_list
        in_be in_ew0 in_ew1 m_ehi m_elo m_idx m_rows0 m_rows1 m_tr m_hi m_hT m_full m_sum m_y m_out0 m_out1
        c_x0 c_x1 c_a0 c_a1 c_idx c_g0 c_g1 c_pair c_sum c_out0 c_out1 f_att_out
        x1_out0 x1_out1 x1_out2 x1_out3 h2_out0 h2_out1""".split()
        q = {n: sem(n) for n in names}
        block = stack.enter_context(nc.Block())
        x_t = x.rearrange("b (t p) d -> (b t) p d", p=P)
        x1_t = x1_dram.rearrange("(t p) d -> t p d", p=P)
        h2_t = h2_dram.rearrange("(t p) d -> t p d", p=P)
        out_t = out.rearrange("b (t p) d -> (b t) p d", p=P)
        att_t = att_dram.rearrange("(t p) d -> t p d", p=P)
        yb_t = yb_dram.rearrange("(t p) d -> t p d", p=P)

        def prod3(pe, out, stat, mov, first, last):
            pe.matmul(out, stat[0], mov[0], start=first, stop=False)
            pe.matmul(out, stat[0], mov[1], start=False, stop=False)
            return pe.matmul(out, stat[1], mov[0], start=False, stop=last)

        def at(p, *idx):
            return p[0][idx], p[1][idx]

        n_wqT, n_wkT, n_eT, n_KE = 0, C, 2 * C, 2 * C + B
        n_A = n_KE + 2 * C
        n_cq = n_A + C
        n_G = n_cq + 1
        n_sb = n_G + 2 * C
        n_ve = n_sb + 2
        n_end = n_ve + B

        PLAN = ["R0", "PV3", "R1", "R2 OT3", "R3", "PV0 H0 H1", "H2 H3 N0", "N1 OT0", "N2", "PV1", "N3", "V0 OT1", "V1", "PV2", "V2", "V3 OT2"]
        ITEMS = ["R0", "R1", "R2", "R3", "H0", "H1", "H2", "H3", "N0", "N1", "N2", "N3", "V0", "V1", "V2", "V3"]
        HIS = ITEMS[0:12]
        BEFORE = ITEMS[4:]
        DB = (2, 3, 4, 5, 7)
        SB = (3, 4, 5, 7)
        FILL = 8 * 16

        def number(b, item):
            return len(BEFORE) + len(ITEMS) * b + ITEMS.index(item), len(HIS) - 4 + len(HIS) * b + HIS.index(item) if item in HIS else None

        def early(item):
            return BEFORE.index(item), HIS.index(item) - 4 if item in HIS else None

        def plan(k, engine, first, last):
            work = PLAN[k].split()
            main = [w for w in work if w[0:2] != "OT"]
            ot = [w for w in work if w[0:2] == "OT"]
            if "H0" in work:
                order = {"pe": "S H0 PV0 H1 T01 T23", "act": "e0 H0 e1 e2 e3 PV0 H1 t0 t2", "dve": "m0 m1 H0 m2 m3 H1 t1 t3"}[engine].split()
            elif "H2" in work:
                order = {"pe": "S H2 T01 H3 T23 N0", "act": "e0 H2 t0 e1 H3 t2 e2 e3 N0", "dve": "m0 H2 m1 t1 m2 H3 t3 m3 N0"}[engine].split()
            elif main[0][0:2] == "PV":
                order = {"pe": ["S", *main, "T01", "T23"], "act": ["e0", "e1", "e2", "e3", *main, "t0", "t2"],
                         "dve": ["m0", "m1", "m2", "m3", "t1", "t3"]}[engine]
            else:
                order = {"pe": ["S", "T01", *ot, *main, "T23"], "act": ["e0", "t0", "e1", "e2", "e3", *main, "t2"],
                         "dve": ["m0", "m1", "t1", *ot, "m2", "m3", *main, "t3"]}[engine]
            return [w for w in order if not (first and (w in ("PV3", "OT3") or (k == 0 and w[0] in "Tt")))
                    and not (last and w[0] in "HNV")]

        def await_ge(eng, name, value):
            if not isinstance(value, int) or value > 0:
                eng.wait_ge(q[name], value)

        def piece(item):
            return int(item[1]) // 2, int(item[1]) % 2

        def batches(eng, steps):
            steps(0, "first")
            with eng.Fori(1, B - 1) as b:
                steps(b, "middle")
            steps(B - 1, "last")
            steps(B, "after")

        def tile(b, t, d, part):
            u = t + d
            if (part == "first" and u < 0) or (part == "last" and u >= T) or (part == "after" and u >= 0):
                return None
            return b * T + u, u % T, b + u // T

        def stack_use(b, h, j):
            if j < 3:
                return j, 2 * b + h, T * (8 * (2 * b + h) - 8 + 2 * j + 2)
            return 3 + h, b, T * (16 * b - 16 + 8 * h + 8)

        N_PICKED = 19

        @block.sync
        def _(sp):
            for w, to, name in ((wk, 1, "in_wk"), (wq, 0, "in_wq"), (wv, 2, "in_wv")):
                sp.dma_start(wst[to], w.rearrange("(c p) n -> p c n", p=P)).then_inc(q[name], 16)
            for t in range(T):
                sp.dma_start(xin[:, t, :], x_t[t]).then_inc(q[f"x_in{t}"], 16)

            sp.wait_ge(q["set_free"], n_end)
            sp.dma_start(wraw, w_qkv.rearrange("(c p) n -> p c n", p=P)).then_inc(q["in_wqkv"], 16)
            sp.dma_start(bqk[:], b_qkv.rearrange("(c p) -> p c", p=P)[:, 0:2 * C], allow_slow_non_contiguous=True).then_inc(q["in_fb"], 16)
            sp.dma_start(bvf[:], b_qkv.rearrange("(a n) -> a n", a=3)[2:3, :].broadcast_to([P, D])).then_inc(q["in_fb"], 16)

            def tiles(b, more):
                for t in range(T):
                    if more:
                        sp.wait_ge(q["x1_part"], b * T + t + 1)
                        sp.dma_start(xin[:, t, :], x_t[b * T + t + T]).then_inc(q[f"x_in{t}"], 16)
                    sp.wait_ge(q["x1_ready"], b * T + t + 1)
                    sp.dma_start(x1_t[b * T + t], x1[:, t, :]).then_inc(q[f"x1_out{t}"], 16)
                    sp.wait_ge(q["h2_ready"], b * T + t + 1)
                    sp.dma_start(h2_t[b * T + t], h2[:, t % 2, :]).then_inc(q[f"h2_out{t % 2}"], 16)

            with sp.Fori(0, B - 1) as b:
                tiles(b, True)
            tiles(B - 1, False)
            for t in range(T):
                sp.wait_ge(q[f"x1_out{t}"], 16 * B)
            for t in range(2):
                sp.wait_ge(q[f"h2_out{t}"], 16 * B * T // 2)

            h2_b = h2_dram.rearrange("(b t p) d -> b p t d", p=P, t=T)

            def stacks(b, h, i, js, n):
                await_ge(sp, "f_d_free", n)
                for j in js:
                    slot, fills, used = stack_use(b, h, j)
                    sp.sem_inc(q["sp_went_on"], 1)
                    await_ge(sp, "f_s_full", used)
                    for k, part in enumerate(((0, 0, 1, 1), (0, 1, 0, 1))[i]):
                        sp.dma_start(full(stk[slot][i][k * HD:(k + 1) * HD]),
                                     full(qk2[i][part][j * HD:(j + 1) * HD])).then_inc(q[f"f_stack{slot}"], 16)

            sp.wait_ge(q["r_zero"], 1)
            sp.dma_start(slot_dram.rearrange("(p i) c -> p i c", p=P), lst).then_inc(q["r_zeroed"], 16)
            sp.wait_ge(q["f_wready"], 2)
            sp.dma_start(h2f, h2_b[0]).then_inc(q["f_raw"], 16)
            stacks(0, 0, 0, range(HG), early("N1")[0] + 1)
            stacks(0, 0, 1, range(HG), early("N3")[0] + 1)

            def batch(b, first, last):
                if not last:
                    sp.wait_ge(q["f_d_full"], early("H3")[0] + 1 if first else number(b - 1, "H3")[0] + 1)
                    sp.sem_inc(q["sp_went_on"], 1)
                    sp.dma_start(h2f, h2_b[b + 1]).then_inc(q["f_raw"], 16)
                sp.wait_ge(q["f_d_free"], number(b, "R0")[0])
                sp.sem_inc(q["sp_went_on"], 1)
                await_ge(sp, "f_pv", b * NG)
                sp.dma_start(V, Vst).then_inc(q["f_v_in"], 16)
                for js in ((0, 3, 1), (2,)):
                    stacks(b, 1, 0, js, number(b, "R1")[0] + 1)
                    stacks(b, 1, 1, js, number(b, "R3")[0] + 1)
                if not last:
                    for js in ((0, 3, 1), (2,)):
                        stacks(b + 1, 0, 0, js, number(b, "N1")[0] + 1)
                        stacks(b + 1, 0, 1, js, number(b, "N3")[0] + 1)

            batch(0, True, False)
            with sp.Fori(1, B - 1) as b:
                batch(b, False, False)
            batch(B - 1, False, True)
            for k in range(4):
                sp.wait_ge(q[f"r_scat{k}"], 16 * NT // 2)
            sp.dma_start(lst, slot_dram.rearrange("(i p) c -> p i c", p=P)).then_inc(q["in_list"], 16)
            sp.wait_ge(q["f_pv"], B * NG)
            sp.wait_ge(q["f_ot"], B * NG)
            for e in range(NE):
                if e >= 2:
                    sp.wait_ge(q["m_elo"], e - 1)
                sp.dma_start(eraw[e % 2], w_exp[e].rearrange("(c p) n -> p c n", p=P)).then_inc(q[f"in_ew{e % 2}"], 16)
            sp.dma_start(be_all, b_exp.rearrange("(a e) n -> a (e n)", a=1).broadcast_to([P, NE * D])).then_inc(q["in_be"], 16)

            def y_store(i, k):
                sp.wait_ge(q["m_y"], i + 1)
                sp.dma_start(yb_t[i], ysb[k]).then_inc(q[f"m_out{k}"], 16)

            with sp.Fori(0, NB // 2) as n:
                for k in range(2):
                    y_store(2 * n + k, k)

            sp.wait_ge(q["f_att_out"], 16 * 2 * B)
            for k in range(2):
                sp.dma_start(fin[k][0], x1_t[k]).then_inc(q[f"c_x{k}"], 16)
            for k in range(2):
                sp.dma_start(fin[k][1], att_t[k]).then_inc(q[f"c_a{k}"], 16)

            def combine(n, more):
                for k in range(2):
                    i = 2 * n + k
                    sp.wait_ge(q["c_sum"], i + 1)
                    sp.dma_start(out_t[i], fin[k][0]).then_inc(q[f"c_out{k}"], 16)
                    if more:
                        sp.dma_start(fin[k][1], att_t[i + 2]).then_inc(q[f"c_a{k}"], 16)
                        sp.wait_ge(q[f"c_out{k}"], 16 * n + 16)
                        sp.dma_start(fin[k][0], x1_t[i + 2]).then_inc(q[f"c_x{k}"], 16)

            with sp.Fori(0, NT // 2 - 1) as n:
                combine(n, True)
            combine(NT // 2 - 1, False)
            for k in range(2):
                sp.wait_ge(q[f"c_out{k}"], 16 * NT // 2)

        @block.gpsimd
        def _(pool):
            pool.memset(ident[:], 0.0).then_inc(q["made_ident"], 1)
            pool.wait_ge(q["made_ident"], 1)
            pool.affine_select(out=ident[:], in_=ident[:], compare_op=ALU.not_equal, fill=1.0, base=0,
                               pattern=[[-1, P]], channel_multiplier=1).then_inc(q["made_ident"], 1)
            pool.memset(ones[:], 1.0).then_inc(q["made_ones"], 1)
            pool.wait_ge(q["made_ones"], 1)
            pool.memset(full(eT[0].rearrange("p c (b w) -> p (c b) w", w=W)[:, :, E:W]), 0.0).then_inc(q["made_ones"], 1)
            pool.memset(full(eT[1].rearrange("p c (b w) -> p (c b) w", w=W)[:, :, E:W]), 0.0).then_inc(q["made_ones"], 1)
            pool.memset(cst[:, 0:1], EPS).then_inc(q["made_consts"], 1)
            pool.memset(cst[:, 1:2], -0.5).then_inc(q["made_consts"], 1)
            pool.memset(cst[:, 2:3], -1.0).then_inc(q["made_consts"], 1)
            pool.wait_ge(q["made_consts"], 3)
            pool.affine_select(out=tri[:], in_=ones[:], compare_op=ALU.is_gt, fill=0.0, base=0,
                               pattern=[[1, P]], channel_multiplier=-1).then_inc(q["made_count"], 1)
            pool.iota(iot[:], pattern=[[1, NB]], base=0, channel_multiplier=0).then_inc(q["made_count"], 1)
            pool.wait_ge(q["made_count"], 2)
            pool.tensor_copy(kk[:], iot[:]).then_inc(q["made_count"], 1)

            def rstd(mo, ln, i, slot):
                pool.wait_ge(q[f"{ln}_var"], i + 1)
                pool.tensor_tensor(mo[:, slot, 2:3], mo[:, slot, 1:2], cst[:, 0:1], ALU.add).then_inc(q[f"{ln}_eps"], 1)
                pool.tensor_tensor(mo[:, slot, 4:5], mo[:, slot, 0:1], cst[:, 2:3], ALU.mult).then_inc(q[f"{ln}_neg"], 1)
                pool.wait_ge(q[f"{ln}_eps"], i + 1)
                pool.tensor_tensor(mo[:, slot, 3:4], mo[:, slot, 2:3], cst[:, 1:2], ALU.pow).then_inc(q[f"{ln}_pow"], 1)
                pool.wait_ge(q[f"{ln}_neg"], i + 1)
                pool.wait_ge(q[f"{ln}_pow"], i + 1)
                pool.tensor_tensor(mo[:, slot, 5:6], mo[:, slot, 4:5], mo[:, slot, 3:4], ALU.mult).then_inc(q[f"{ln}_rstd"], 1)

            def steps(b, part):
                for t in range(T):
                    if now := tile(b, t, 2, part):
                        rstd(mo1, "ln1", now[0], now[1] % 2)
                    if now := tile(b, t, -1, part):
                        rstd(mo2, "ln2", now[0], now[1] % 2)

            rstd(mo1, "ln1", 0, 0)
            rstd(mo1, "ln1", 1, 1)
            batches(pool, steps)

            pool.wait_ge(q["r_zero"], 1)
            pool.iota(rec[:, :, :, 1].bitcast(I32), pattern=[[0, 2], [P, NT]], base=0, channel_multiplier=1).then_inc(q["r_tokens"], 1)
            pool.wait_ge(q["r_tokens"], 1)
            pool.wait_ge(q["r_zeroed"], 16)
            with pool.Fori(0, NT // 2) as n:
                for k in range(4):
                    pool.wait_ge(q[f"r_scat{k}"], n * 16)
                    pool.sem_inc(q["pool_went_on"], 1)
                    pool.tensor_copy(recs[:, k:k + 1, :], rec.rearrange("p k t c -> p (k t) c")[:, bass.ds(4 * n + k, 1), :]).then_inc(q["r_copied"], 1)
                    pool.wait_ge(q["r_copied"], 4 * n + k + 1)
                    pool.sem_inc(q["pool_went_on"], 1)
                    pool.indirect_dma_start(out=slot_dram, out_offset=bass.IndirectOffsetOnAxis(ap=recs[:, k, 0:1].bitcast(U32), axis=0),
                                            in_=recs[:, k, 1:3], in_offset=None).then_inc(q[f"r_scat{k}"], 16)

            att_b = att_dram.rearrange("(b t p) d -> b p t d", p=P, t=T)
            with pool.Fori(0, B) as b:
                for h in range(2):
                    pool.wait_ge(q["f_o_fin"], b * NG + 2 * h + 2)
                    pool.sem_inc(q["pool_went_on"], 1)
                    pool.dma_start(att_b[b][:, :, h * (D // 2):(h + 1) * (D // 2)], tmp).then_inc(q["f_att_out"], 16)

            pool.wait_ge(q["in_list"], 16)
            pool.wait_ge(q["f_pv"], B * NG)
            pool.wait_ge(q["f_ot"], B * NG)
            with pool.Fori(0, NB // 2) as n:
                for k in range(2):
                    i = 2 * n + k
                    pool.wait_ge(q[f"m_rows{k}"], n * 16)
                    pool.sem_inc(q["pool_went_on"], 1)
                    pool.tensor_copy(idx[:, k:k + 1], lst[:, bass.ds(i, 1), 0].bitcast(U32)).then_inc(q["m_idx"], 1)
                    pool.wait_ge(q["m_idx"], i + 1)
                    pool.wait_ge(q["m_tr"], 2 * n)
                    pool.sem_inc(q["pool_went_on"], 1)
                    pool.indirect_dma_start(out=rows[k], out_offset=None, in_=h2_dram,
                                            in_offset=bass.IndirectOffsetOnAxis(ap=idx[:, k:k + 1], axis=0)).then_inc(q[f"m_rows{k}"], 16)
            for k in range(2):
                pool.wait_ge(q[f"m_out{k}"], 16 * NB // 2)
            with pool.Fori(0, NT // 2) as n:
                for k in range(2):
                    i = 2 * n + k
                    pool.wait_ge(q[f"c_g{k}"], n * 32)
                    pool.wait_ge(q["c_sum"], 2 * n)
                    pool.sem_inc(q["pool_went_on"], 1)
                    for a in range(2):
                        pool.tensor_copy(idx[:, 2 * k + a:2 * k + a + 1], rec[:, a, bass.ds(i, 1), 0].bitcast(U32)).then_inc(q["c_idx"], 1)
                    pool.wait_ge(q["c_idx"], 2 * i + 2)
                    pool.sem_inc(q["pool_went_on"], 1)
                    for a in range(2):
                        pool.indirect_dma_start(out=fin[k][2 + a], out_offset=None, in_=yb_dram,
                                                in_offset=bass.IndirectOffsetOnAxis(ap=idx[:, 2 * k + a:2 * k + a + 1], axis=0)).then_inc(q[f"c_g{k}"], 16)

        @block.scalar
        def _(act):
            act.dma_start(est[0:E, :, :], ctx.rearrange("b e d -> e b d")).then_inc(q["in_ctx"], 16)
            act.dma_start(bqc[:], bq.rearrange("(c p) -> p c", p=P), allow_slow_non_contiguous=True).then_inc(q["in_bias"], 16)
            act.dma_start(bkc[:], bk.rearrange("(c p) -> p c", p=P), allow_slow_non_contiguous=True).then_inc(q["in_bias"], 16)
            act.dma_start(bv_all[:], bv.rearrange("(a n) -> a n", a=1).broadcast_to([P, D])).then_inc(q["in_bias"], 16)
            act.dma_start(bg_all[:], b_gate.rearrange("(a n) -> a n", a=1).broadcast_to([P, NE])).then_inc(q["in_bg"], 16)
            act.dma_start(gws[:], w_gate.rearrange("(c p) n -> p c n", p=P)).then_inc(q["in_bias"], 16)

            def hi(n, out, src, bias=0.0):
                act.wait_ge(q["set_full"], n + 1)
                act.activation(out, src, ACT.Identity, bias=bias).then_inc(q["set_hi"], 1)

            act.wait_ge(q["in_wk"], 16)
            act.copy(wkp[0], wst[1]).then_inc(q["w_hi"], 1)
            for m in range(C):
                hi(n_wqT + m, wqT[0][:, m, :], bank[m][:])
            for m in range(C):
                hi(n_wkT + m, wkT[0][:, m, :], bank[C + m][:])
            for b in range(B):
                hi(n_eT + b, eT[0][:, :, b * W:b * W + E], bank[b][:, 0:C * W].rearrange("p (c w) -> p c w", c=C)[:, :, 0:E])
            act.wait_ge(q["in_wv"], 16)
            act.copy(wvp[0], wst[2]).then_inc(q["w_hi"], 1)
            act.wait_ge(q["in_bias"], 64)
            act.copy(gw[0], gws[:]).then_inc(q["w_hi"], 1)
            act.wait_ge(q["made_ones"], 3)
            for c in range(C):
                act.activation(bqrep[0][:, c, :], ones[:], ACT.Identity, scale=bqc[:, c:c + 1]).then_inc(q["w_hi"], 1)
            for m in range(C):
                for f in range(2):
                    n = n_KE + 2 * m + f
                    hi(n, KE[0][:, m, f * HB * W:(f + 1) * HB * W], bank[n % 8][:, 0:HB * W], bkc[:, m:m + 1])
            for m in range(C):
                hi(n_A + m, A[0][:, m, :], bank[(n_A + m) % 8][:])
            for k in range(2 * C):
                m, f = k // 2, k % 2
                act.wait_ge(q["set_staged"], 2 * k + 2)
                act.copy(G[0][:, m, f * HB * W:(f + 1) * HB * W], gst.rearrange("p b w -> p (b w)")).then_inc(q["set_hi"], 1)
            for b in range(B):
                act.wait_ge(q["set_staged"], 4 * C + b + 1)
                act.copy(vext[0][0:W, b, :], vst[0:W, :]).then_inc(q["set_hi"], 1)

            def normed(ln, i, u, src, out, mo, name):
                act.wait_ge(q[f"{ln}_rstd"], i + 1)
                act.activation(out, src, ACT.Identity, bias=mo[:, u % 2, 5:6], scale=mo[:, u % 2, 3:4]).then_inc(q[name], 1)

            def h_norm(i, u, bb):
                await_ge(act, "s_step", 3 * i - 4)
                normed("ln1", i, u, xin[:, u, :], h[:, u % 2, :], mo1, "h_ready")

            def h_hi(i, u, bb):
                await_ge(act, "v_full", i - 1)
                act.wait_ge(q["h_tr"], i + 1)
                act.copy(hT[u % 2][0].rearrange("p c n -> p (c n)"), bank[0][:]).then_inc(q["hT_hi"], 1)

            def h2_norm(i, u, bb):
                await_ge(act, "h2_tr", i - 1)
                await_ge(act, f"h2_out{u % 2}", bb * 32 + 16 * (u // 2))
                normed("ln2", i, u, x1[:, u, :], h2[:, u % 2, :], mo2, "h2_ready")

            def h2_hi(i, u, bb):
                await_ge(act, "g_full", i - 1)
                act.wait_ge(q["h2_tr"], i + 1)
                act.copy(h2T[u % 2][0].rearrange("p c n -> p (c n)"), bank[2][:]).then_inc(q["h2T_hi"], 1)

            def p_hi(i, u, bb):
                await_ge(act, "e_full", i)
                act.wait_ge(q["p_tr"], i + 1)
                act.copy(pT[0][0:W, :], bank[6][0:W, 0:P]).then_inc(q["pT_hi"], 1)

            def weigh(i, u, bb):
                act.wait_ge(q["s_max"], i + 1)
                act.activation(sc[:, u % 2, :], sc[:, u % 2, :], ACT.Exp, bias=col[:, u % 2, 1:2],
                               accum_out=col[:, u % 2, 2:3]).then_inc(q["s_exp"], 1)

            def steps(b, part):
                for t in range(T):
                    for d, work in ((-1, p_hi), (0, weigh), (1, h_hi), (2, h_norm), (-2, h2_hi), (-1, h2_norm)):
                        if now := tile(b, t, d, part):
                            work(*now)

            h_norm(0, 0, 0)
            h_norm(1, 1, 0)
            h_hi(0, 0, 0)
            batches(act, steps)

            act.wait_ge(q["in_wqkv"], 16)
            act.wait_ge(q["in_fb"], 32)
            act.wait_ge(q["g_full"], NT)
            act.wait_ge(q["route"], 3)
            act.activation(temp[2], temp[1], ACT.Exp).then_inc(q["r_gate"], 1)
            act.mul(bqk[:, 0:C], bqk[:, 0:C], HD ** -0.5).then_inc(q["f_wscaled"], 1)
            act.mul(wqkv[0][:, :, 0:D], wraw[:, :, 0:D], HD ** -0.5).then_inc(q["f_whi"], 1)
            act.copy(wqkv[0][:, :, D:Q3], wraw[:, :, D:Q3]).then_inc(q["f_whi"], 1)

            def split(b, item, n, hn, bank_in):
                act.wait_ge(q["f_d_full"], n + 1)
                if item[0] == "H":
                    t = int(item[1])
                    act.copy(fT[0][:, :, t * P:(t + 1) * P], bank_in[:].rearrange("p (c n) -> p c n", c=C)).then_inc(q["f_d_hi"], 1)
                    return
                i, m = piece(item)
                h = 1 if item[0] == "R" else 0
                if item[1] == "0" and n >= len(BEFORE) if isinstance(n, int) else item[1] == "0":
                    for j in range(HG):
                        slot, fills, used = stack_use(b if h else b + 1, h, j)
                        if j == 3:
                            slot, fills = 3 + (1 - h), b + 1
                        act.wait_ge(q[f"f_stack{slot}"], fills * FILL)
                act.activation(qkp[i][m][0], bank_in[:], ACT.Identity,
                               bias=bqk[:, i * C + 2 * h + m:i * C + 2 * h + m + 1]).then_inc(q["f_d_hi"], 1)

            def exps(b, k, ts):
                if ts[0] == 0:
                    await_ge(act, "f_t_full", (b * NH + k - 1) * T)
                for t in ts:
                    act.wait_ge(q["f_max"], (b * NH + k) * T + t + 1)
                    act.activation(PR[k % 2][:, t, :], bank[SB[t]][:], ACT.Exp, bias=nmx[:, k, t:t + 1],
                                   accum_out=Z[:, t, k:k + 1]).then_inc(q["f_exp"], 1)

            def turned(b, k, c):
                if c == 0:
                    await_ge(act, "f_pv", b * NG + k // HG)
                act.wait_ge(q["f_t_full"], (b * NH + k) * T + c + 1)
                act.copy(PT[k % HG][:, c, :], bank[c % 2][:]).then_inc(q["f_pt_a"], 1)

            def o_out(b, g):
                act.wait_ge(q["f_pv"], b * NG + g + 1)
                act.copy(Osb, bank[6][:]).then_inc(q["f_o_sb"], 1)

            def batch(b, first, last):
                for k in range(NH):
                    before = (b, k - 1) if k else (b - 1, NH - 1)
                    for work in plan(k, "act", first, last):
                        if work[0] == "e":
                            exps(b, k, (int(work[1]),))
                        elif work[0] == "t":
                            turned(*before, int(work[1]))
                        elif work in HIS:
                            split(b, work, *number(b, work), bank[DB[0]])
                        elif work[0:2] == "PV":
                            o_out(b - 1 if work == "PV3" else b, int(work[2]))

            for item in BEFORE:
                if item in HIS:
                    n, hn = early(item)
                    split(0, item, n, hn, bank[DB[n % len(DB)]])
            batch(0, True, False)
            with act.Fori(1, B - 1) as b:
                batch(b, False, False)
            batch(B - 1, False, True)
            turned(B - 1, NH - 1, 0)
            turned(B - 1, NH - 1, 2)
            o_out(B - 1, NG - 1)

            act.wait_ge(q["f_ot"], B * NG)
            for e in range(NE):
                act.wait_ge(q[f"in_ew{e % 2}"], 16 * (e // 2) + 16)
                act.copy(ew[e][:, 0], eraw[e % 2]).then_inc(q["m_ehi"], 1)

            def rows_hi(i, k):
                act.wait_ge(q["m_tr"], i + 1)
                act.copy(gT[k][:, 0].rearrange("p c n -> p (c n)"), bank[k][:]).then_inc(q["m_hi"], 1)

            def blocks(n, more):
                for k in range(2):
                    i = 2 * n + k
                    if more or k == 0:
                        rows_hi(i + 1, 1 - k)
                    act.wait_ge(q["m_sum"], i + 1)
                    act.activation(ysb[k], ysb[k], ACT.Copy, scale=lst[:, bass.ds(i, 1), 1]).then_inc(q["m_y"], 1)

            rows_hi(0, 0)
            with act.Fori(0, NB // 2 - 1) as n:
                blocks(n, True)
            blocks(NB // 2 - 1, False)

        @block.tensor
        def _(pe):
            pe.wait_ge(q["made_ident"], 2)

            def slot(n):
                if n >= 8:
                    pe.wait_ge(q["set_free"], n - 7)
                return bank[n % 8]

            for n0, src, name in ((n_wqT, 0, "in_wq"), (n_wkT, 1, "in_wk")):
                pe.wait_ge(q[name], 16)
                for m in range(C):
                    o = slot(n0 + m)
                    for c in range(C):
                        last = pe.transpose(o[:, c * P:(c + 1) * P], wst[src][:, c, m * P:(m + 1) * P], ident[:])
                    last.then_inc(q["set_full"], 1)
            pe.wait_ge(q["in_ctx"], 16)
            for b in range(B):
                o = slot(n_eT + b)
                for c in range(C):
                    last = pe.transpose(o[:, c * W:c * W + E], est[0:E, b, c * P:(c + 1) * P], ident[0:E, 0:E])
                last.then_inc(q["set_full"], 1)
            pe.wait_ge(q["w_ready"], 1)
            pe.wait_ge(q["made_ones"], 3)
            pe.wait_ge(q["set_free"], n_KE)
            half = [slice(f * HB * W, (f + 1) * HB * W) for f in range(2)]
            sl = slice(None)
            for m in range(C):
                for f in range(2):
                    o = slot(n_KE + 2 * m + f)
                    for c in range(C):
                        last = prod3(pe, o[:, 0:HB * W], at(wkp, sl, c, slice(m * P, (m + 1) * P)), at(eT, sl, c, half[f]),
                                     c == 0, c == C - 1)
                    last.then_inc(q["set_full"], 1)
            for m in range(C):
                o = slot(n_A + m)
                for c in range(C):
                    last = prod3(pe, o[:], at(wqT, sl, c, slice(m * P, (m + 1) * P)), at(wkT, sl, c), c == 0, c == C - 1)
                last.then_inc(q["set_full"], 1)
            pe.wait_ge(q["w_ready"], 3 + C)
            o = slot(n_cq)
            for m in range(C):
                for c in range(C):
                    last = prod3(pe, o[:, 2 * m:2 * m + 2], at(wkT, sl, c, slice(m * P, (m + 1) * P)),
                                 at(bqrep, sl, c, slice(0, 2)), c == 0, c == C - 1)
            last.then_inc(q["set_full"], 1)
            pe.wait_ge(q["set_free"], n_A)
            for m in range(C):
                for f in range(2):
                    o = slot(n_G + 2 * m + f)
                    for c in range(C):
                        last = prod3(pe, o[:, 0:HB * W], at(wqT, sl, c, slice(m * P, (m + 1) * P)), at(KE, sl, c, half[f]),
                                     c == 0, c == C - 1)
                    last.then_inc(q["set_full"], 1)
            for f in range(2):
                o = slot(n_sb + f)
                for c in range(C):
                    last = prod3(pe, o[:, 0:HB * W], at(bqrep, sl, c), at(KE, sl, c, half[f]), c == 0, c == C - 1)
                last.then_inc(q["set_full"], 1)
            for b in range(B):
                o = slot(n_ve + b)
                for c in range(C):
                    last = prod3(pe, o[0:W, :], at(eT, sl, c, slice(b * W, (b + 1) * W)), at(wvp, sl, c), c == 0, c == C - 1)
                last.then_inc(q["set_full"], 1)

            def h_turn(i, u, bb):
                await_ge(pe, "hT_ready", i)
                pe.wait_ge(q["h_ready"], i + 1)
                for c in range(C):
                    last = pe.transpose(bank[0][:, c * P:(c + 1) * P], h[:, u % 2, c * P:(c + 1) * P], ident[:])
                last.then_inc(q["h_tr"], 1)

            def score(i, u, bb):
                await_ge(pe, "s_step", 3 * i)
                pe.wait_ge(q["hT_ready"], i + 1)
                for c in range(C):
                    prod3(pe, bank[1][:], at(hT[u % 2], sl, c), at(A, sl, c), c == 0, c == C - 1)
                for c in range(C):
                    last = prod3(pe, bank[5][:, 0:W], at(hT[u % 2], sl, c), at(G, sl, c, bass.ds(bb * W, W)), c == 0, c == C - 1)
                last.then_inc(q["s_full"], 1)

            def value(i, u, bb):
                await_ge(pe, "x1_part", i)
                for c in range(C):
                    last = prod3(pe, bank[3][:], at(hT[u % 2], sl, c), at(wvp, sl, c), c == 0, c == C - 1)
                last.then_inc(q["v_full"], 1)

            def p_turn(i, u, bb):
                await_ge(pe, "pT_ready", i)
                pe.wait_ge(q["p_ready"], i + 1)
                pe.transpose(bank[6][0:W, 0:P], sc[:, u % 2, :], ident[:]).then_inc(q["p_tr"], 1)

            def extend(i, u, bb):
                await_ge(pe, "x1_ready", i)
                pe.wait_ge(q["pT_ready"], i + 1)
                prod3(pe, bank[7][:], (pT[0][0:W, :], pT[1][0:W, :]),
                      (vext[0][0:W].rearrange("p b d -> p (b d)")[:, bass.ds(bb * D, D)],
                       vext[1][0:W].rearrange("p b d -> p (b d)")[:, bass.ds(bb * D, D)]),
                      True, True).then_inc(q["e_full"], 1)

            def h2_turn(i, u, bb):
                await_ge(pe, "h2T_ready", i)
                pe.wait_ge(q["h2_ready"], i + 1)
                for c in range(C):
                    last = pe.transpose(bank[2][:, c * P:(c + 1) * P], h2[:, u % 2, c * P:(c + 1) * P], ident[:])
                last.then_inc(q["h2_tr"], 1)

            def gate(i, u, bb):
                await_ge(pe, "g_copied", i)
                pe.wait_ge(q["h2T_ready"], i + 1)
                for c in range(C):
                    last = prod3(pe, bank[4][:, 0:NE], at(h2T[u % 2], sl, c), at(gw, sl, c), c == 0, c == C - 1)
                last.then_inc(q["g_full"], 1)

            def steps(b, part):
                for t in range(T):
                    for d, work in ((0, score), (-1, extend), (1, h_turn), (-2, h2_turn), (-3, gate), (0, value), (0, p_turn)):
                        if now := tile(b, t, d, part):
                            work(*now)

            pe.wait_ge(q["set_free"], n_end)
            h_turn(0, 0, 0)
            batches(pe, steps)

            pe.wait_ge(q["route"], N_PICKED)
            pe.matmul(bank[2][:, 0:NT * NE], tri[:], temp[9].rearrange("p t e -> p (t e)"), start=True, stop=True)
            pe.matmul(bank[2][:, NT * NE:2 * NT * NE], ones[:], temp[9].rearrange("p t e -> p (t e)"), start=True, stop=True).then_inc(q["r_pref"], 1)
            pe.wait_ge(q["f_wready"], 2)

            def dense(b, item, n, o):
                kind, t = item[0], int(item[1])
                if kind == "H":
                    pe.wait_ge(q["f_raw"], b * 16 + 16)
                    for c in range(C):
                        last = pe.transpose(o[:, c * P:(c + 1) * P], h2f[:, t, c * P:(c + 1) * P], ident[:])
                elif kind == "V":
                    for c in range(C):
                        last = prod3(pe, o[:], at(fT, sl, c, slice(t * P, (t + 1) * P)),
                                     at(wqkv, sl, c, slice(2 * D, Q3)), c == 0, c == C - 1)
                else:
                    i, m = piece(item)
                    col = i * D + (2 * (kind == "R") + m) * P
                    for c in range(C):
                        last = prod3(pe, o[:], at(wqkv, sl, c, slice(col, col + P)), at(fT, sl, c), c == 0, c == C - 1)
                last.then_inc(q["f_d_full"], 1)

            def scores(b, k):
                h, j, m = k // 8, k % 8 // 2, k % 2
                slot, fills, used = stack_use(b, h, j)
                if m == 0:
                    pe.wait_ge(q[f"f_stack{slot}"], (fills + 1) * FILL)
                for t in range(T):
                    await_ge(pe, "f_exp", (b * NH + k) * T + t - T + 1)
                    pe.matmul(bank[SB[t]][:], stk[slot][0][:, m, t * P:(t + 1) * P], stk[slot][1][:, m, :],
                              start=True, stop=True).then_inc(q["f_s_full"], 1)

            def turn(b, k, cs):
                if cs[0] == 0:
                    pe.wait_ge(q["f_exp"], (b * NH + k) * T + T)
                for c in cs:
                    await_ge(pe, ("f_pt_a", "f_pt_d")[c % 2], (b * NH + k) * 2 + c // 2)
                    for t in range(T):
                        last = pe.transpose(bank[c % 2][:, t * P:(t + 1) * P], PR[k % 2][:, t, c * P:(c + 1) * P], ident[:])
                    last.then_inc(q["f_t_full"], 1)

            def pv(b, g):
                pe.wait_ge(q["f_pt_a"], b * 2 * NH + 2 * HG * (g + 1))
                pe.wait_ge(q["f_pt_d"], b * 2 * NH + 2 * HG * (g + 1))
                pe.wait_ge(q["f_v_in"], b * 16 + 16)
                await_ge(pe, "f_o_fin", b * NG + g)
                for c in range(T):
                    for i in range(HG):
                        jj, m = i // 2, i % 2
                        at_o, head = 2 * m + jj, 8 * (g // 2) + HG * m + 2 * (g % 2) + jj
                        last = pe.matmul(bank[6][at_o * HD:(at_o + 1) * HD, :], V[:, c, head * HD:(head + 1) * HD], PT[i][:, c, :],
                                         start=(c == 0), stop=(c == T - 1))
                last.then_inc(q["f_pv"], 1)

            def o_turn(b, g):
                pe.wait_ge(q["f_o_sb"], b * NG + g + 1)
                for t in range(T):
                    last = pe.transpose(bank[6][:, t * P:(t + 1) * P], Osb[:, t * P:(t + 1) * P], ident[:])
                last.then_inc(q["f_ot"], 1)

            def batch(b, first, last):
                for k in range(NH):
                    before = (b, k - 1) if k else (b - 1, NH - 1)
                    for work in plan(k, "pe", first, last):
                        if work == "S":
                            scores(b, k)
                        elif work[0] == "T":
                            turn(*before, (int(work[1]), int(work[2])))
                        elif work in ITEMS:
                            n = number(b, work)[0]
                            pe.wait_ge(q["f_d_free"], n)
                            dense(b if work[0] == "R" else b + 1, work, n, bank[DB[0]])
                        else:
                            (pv if work[0:2] == "PV" else o_turn)(b - 1 if work[2] == "3" else b, int(work[2]))

            for item in BEFORE:
                n = early(item)[0]
                if item == "N0":
                    pe.wait_ge(q["f_d_free"], 4)
                await_ge(pe, "f_d_free", n - len(DB) + 1)
                dense(0, item, n, bank[DB[n % len(DB)]])
            pe.wait_ge(q["f_d_free"], len(BEFORE))
            batch(0, True, False)
            with pe.Fori(1, B - 1) as b:
                batch(b, False, False)
            batch(B - 1, False, True)
            turn(B - 1, NH - 1, (0, 1, 2, 3))
            pv(B - 1, NG - 1)
            o_turn(B - 1, NG - 1)

            def rows_turn(i, k):
                pe.wait_ge(q[f"m_rows{k}"], (i - k) * 8 + 16)
                for c in range(C):
                    last = pe.transpose(bank[k][:, c * P:(c + 1) * P], rows[k][:, c * P:(c + 1) * P], ident[:])
                last.then_inc(q["m_tr"], 1)

            def blocks(n, more):
                for k in range(2):
                    i = 2 * n + k
                    if more or k == 0:
                        pe.wait_ge(q["m_hT"], i)
                        rows_turn(i + 1, 1 - k)
                    pe.wait_ge(q["m_hT"], i + 1)
                    if k == 0:
                        pe.wait_ge(q["m_sum"], 2 * n)
                    else:
                        pe.wait_ge(q["m_sum"], 2 * n)
                    e = pe.value_load(bexp[0:1, bass.ds(i, 1)], min_val=0, max_val=NE - 1)
                    for c in range(C):
                        last = prod3(pe, bank[2 + k][:], (gT[k][:, 0, c], gT[k][:, 1, c]),
                                     (parts[:, bass.ds(e * EW + c * D, D)], parts[:, bass.ds(e * EW + (C + c) * D, D)]), c == 0, c == C - 1)
                    last.then_inc(q["m_full"], 1)

            pe.wait_ge(q["f_o_fin"], B * NG)
            rows_turn(0, 0)
            pe.wait_ge(q["m_elo"], NE)
            with pe.Fori(0, NB // 2 - 1) as n:
                blocks(n, True)
            blocks(NB // 2 - 1, False)

        @block.vector
        def _(dve):
            def lo(n, out, src, high, bias=None):
                dve.wait_ge(q["set_hi"], n + 1)
                if bias is None:
                    ins = dve.tensor_tensor(out, src, full(high), ALU.subtract)
                else:
                    ins = dve.scalar_tensor_tensor(out=out, in0=src, scalar=bias, in1=full(high), op0=ALU.add, op1=ALU.subtract)
                return ins

            dve.wait_ge(q["w_hi"], 1)
            dve.tensor_tensor(wkp[1], wst[1], full(wkp[0]), ALU.subtract).then_inc(q["w_ready"], 1)
            for m in range(C):
                lo(m, wqT[1][:, m, :], bank[m][:], wqT[0][:, m, :]).then_inc(q["set_free"], 1)
            for m in range(C):
                lo(n_wkT + m, wkT[1][:, m, :], bank[C + m][:], wkT[0][:, m, :]).then_inc(q["set_free"], 1)
            for b in range(B):
                cols = slice(b * W, b * W + E)
                lo(n_eT + b, eT[1][:, :, cols], bank[b][:, 0:C * W].rearrange("p (c w) -> p c w", c=C)[:, :, 0:E],
                   eT[0][:, :, cols]).then_inc(q["set_free"], 1)
            dve.wait_ge(q["w_hi"], 2)
            dve.tensor_tensor(wvp[1], wst[2], full(wvp[0]), ALU.subtract).then_inc(q["w_ready"], 1)
            dve.wait_ge(q["w_hi"], 3)
            dve.tensor_tensor(gw[1], gws[:], full(gw[0]), ALU.subtract).then_inc(q["w_ready"], 1)
            for c in range(C):
                dve.wait_ge(q["w_hi"], 4 + c)
                dve.scalar_tensor_tensor(out=bqrep[1][:, c, :], in0=ones[:], scalar=bqc[:, c:c + 1], in1=full(bqrep[0][:, c, :]),
                                         op0=ALU.mult, op1=ALU.subtract).then_inc(q["w_ready"], 1)
            for m in range(C):
                for f in range(2):
                    n = n_KE + 2 * m + f
                    cols = slice(f * HB * W, (f + 1) * HB * W)
                    lo(n, KE[1][:, m, cols], bank[n % 8][:, 0:HB * W], KE[0][:, m, cols], bkc[:, m:m + 1]).then_inc(q["set_free"], 1)
            for m in range(C):
                n = n_A + m
                lo(n, A[1][:, m, :], bank[n % 8][:], A[0][:, m, :]).then_inc(q["set_free"], 1)
            dve.wait_ge(q["set_full"], n_cq + 1)
            dve.tensor_copy(cq[:], bank[n_cq % 8][:, 0:2 * C]).then_inc(q["set_free"], 1)
            dve.wait_ge(q["set_free"], n_cq + 1)
            flat = gst.rearrange("p b w -> p (b w)")
            for k in range(2 * C):
                n, m, f = n_G + k, k // 2, k % 2
                cols = slice(f * HB * W, (f + 1) * HB * W)
                dve.wait_ge(q["set_full"], n + 1)
                dve.wait_ge(q["set_free"], n)
                dve.tensor_copy(flat, bank[n % 8][:, 0:HB * W]).then_inc(q["set_staged"], 1)
                dve.wait_ge(q["set_staged"], 2 * k + 1)
                dve.tensor_scalar(gst[:, :, E:W], gst[:, :, E:W], cq[:, 2 * m:2 * m + 1], None, ALU.add).then_inc(q["set_staged"], 1)
                lo(n - 1, G[1][:, m, cols], flat, G[0][:, m, cols]).then_inc(q["set_free"], 1)
            for f in range(2):
                n = n_sb + f
                dve.wait_ge(q["set_full"], n + 1)
                dve.tensor_copy(sbias[:, f * HB * W:(f + 1) * HB * W], bank[n % 8][:, 0:HB * W]).then_inc(q["set_free"], 1)
            for b in range(B):
                n = n_ve + b
                dve.wait_ge(q["set_full"], n + 1)
                dve.wait_ge(q["set_free"], n)
                dve.tensor_tensor(vst[0:W, :], bank[n % 8][0:W, :], bv_all[0:W, :], ALU.add).then_inc(q["set_staged"], 1)
                lo(n - 3, vext[1][0:W, b, :], vst[0:W, :], vext[0][0:W, b, :]).then_inc(q["set_free"], 1)

            def norm(ln, i, u, src, st, mo, f, normed):
                await_ge(dve, normed, i - 1)
                dve.bn_stats(st[:, u % 2, :], src).then_inc(q[f"{ln}_stats"], 1)
                dve.wait_ge(q[f"{ln}_stats"], i + 1)
                dve.tensor_copy(fence[:, f:f + 1], st[:, u % 2, 0:1])
                dve.bn_aggr(mo[:, u % 2, 0:2], st[:, u % 2, :]).then_inc(q[f"{ln}_var"], 1)

            def h_stats(i, u, bb):
                dve.wait_ge(q[f"x_in{u}"], bb * 16 + 16)
                norm("ln1", i, u, xin[:, u, :], st1, mo1, 0, "h_ready")

            def h_lo(i, u, bb):
                dve.wait_ge(q["hT_hi"], i + 1)
                dve.tensor_tensor(hT[u % 2][1].rearrange("p c n -> p (c n)"), bank[0][:],
                                  full(hT[u % 2][0].rearrange("p c n -> p (c n)")), ALU.subtract).then_inc(q["hT_ready"], 1)

            def p_lo(i, u, bb):
                dve.wait_ge(q["pT_hi"], i + 1)
                dve.tensor_tensor(pT[1][0:W, :], bank[6][0:W, 0:P], full(pT[0][0:W, :]), ALU.subtract).then_inc(q["pT_ready"], 1)

            def x1_begun(i, u, bb):
                dve.wait_ge(q["v_full"], i + 1)
                dve.wait_ge(q["p_ready"], i + 1)
                await_ge(dve, f"x1_out{u}", bb * 16)
                dve.scalar_tensor_tensor(out=x1[:, u, :], in0=bank[3][:], scalar=sc[:, u % 2, E:W],
                                         in1=xin[:, u, :], op0=ALU.mult, op1=ALU.add).then_inc(q["x1_part"], 1)

            def largest(i, u, bb):
                k = u % 2
                dve.wait_ge(q["s_full"], i + 1)
                dve.tensor_tensor(sc[:, k, :], bank[5][:, 0:W], sbias[:, bass.ds(bb * W, W)], ALU.add).then_inc(q["s_step"], 1)
                dve.tensor_tensor_reduce(scr, bank[1][:], h[:, k, :], 1.0, 0.0, ALU.mult, ALU.add,
                                         col[:, k, 0:1]).then_inc(q["s_step"], 1)
                dve.wait_ge(q["s_step"], 3 * i + 2)
                dve.tensor_tensor(sc[:, k, E:W], sc[:, k, E:W], col[:, k, 0:1], ALU.add).then_inc(q["s_step"], 1)
                dve.wait_ge(q["s_step"], 3 * i + 3)
                dve.tensor_reduce(col[:, k, 1:2], sc[:, k, :], AX.X, ALU.max, negate=True).then_inc(q["s_max"], 1)

            def x1_whole(i, u, bb):
                dve.wait_ge(q["e_full"], i + 1)
                dve.wait_ge(q["x1_part"], i + 1)
                dve.tensor_tensor(x1[:, u, :], bank[7][:], x1[:, u, :], ALU.add).then_inc(q["x1_ready"], 1)

            def share(i, u, bb):
                k = u % 2
                dve.wait_ge(q["s_exp"], i + 1)
                dve.reciprocal(col[:, k, 3:4], col[:, k, 2:3]).then_inc(q["s_den"], 1)
                dve.wait_ge(q["s_den"], i + 1)
                dve.tensor_scalar(sc[:, k, :], sc[:, k, :], col[:, k, 3:4], None, ALU.mult).then_inc(q["p_ready"], 1)

            def h2_stats(i, u, bb):
                dve.wait_ge(q["x1_ready"], i + 1)
                norm("ln2", i, u, x1[:, u, :], st2, mo2, 1, "h2_ready")

            def h2_lo(i, u, bb):
                dve.wait_ge(q["h2T_hi"], i + 1)
                dve.tensor_tensor(h2T[u % 2][1].rearrange("p c n -> p (c n)"), bank[2][:],
                                  full(h2T[u % 2][0].rearrange("p c n -> p (c n)")), ALU.subtract).then_inc(q["h2T_ready"], 1)

            def g_copy(i, u, bb):
                dve.wait_ge(q["g_full"], i + 1)
                dve.tensor_copy(glog[:, bass.ds(i, 1), :], bank[4][:, 0:NE].rearrange("p (a n) -> p a n", a=1)).then_inc(q["g_copied"], 1)

            def steps(b, part):
                for t in range(T):
                    for d, work in ((-1, p_lo), (-1, x1_begun), (2, h_stats), (0, largest), (-1, x1_whole), (0, share),
                                    (-1, h2_stats), (1, h_lo), (-2, h2_lo), (-3, g_copy)):
                        if now := tile(b, t, d, part):
                            work(*now)

            h_stats(0, 0, 0)
            h_stats(1, 1, 0)
            h_lo(0, 0, 0)
            batches(dve, steps)

            route = [0]

            def then(ins):
                ins.then_inc(q["route"], 1)
                route[0] += 1
                dve.wait_ge(q["route"], route[0])

            t_lg, t_ex, t_gate, t_first, t_second, t_eq, t_place, t_in, t_sel = (temp[i] for i in (1, 2, 3, 4, 5, 6, 7, 8, 9))
            row = temp[0].rearrange("p t e -> p (t e)")
            mx, den, tie, desc = row[:, 0:NT], row[:, NT:2 * NT], row[:, 2 * NT:3 * NT], row[:, 3 * NT:3 * NT + NE]
            gates = [row[:, 4 * NT:5 * NT], row[:, 5 * NT:6 * NT]]

            def wide(v):
                return v.unsqueeze(2).broadcast_to([P, NT, NE])

            def every(v):
                return v.unsqueeze(1).broadcast_to([P, NT, NE])

            dve.wait_ge(q["g_copied"], NT)
            dve.wait_ge(q["in_bg"], 16)
            dve.wait_ge(q["made_count"], 3)
            then(dve.tensor_tensor(t_lg, glog[:], every(bg_all[:]), ALU.add))
            then(dve.tensor_reduce(mx, t_lg, AX.X, ALU.max))
            then(dve.tensor_tensor(t_lg, t_lg, wide(mx), ALU.subtract))
            then(dve.tensor_scalar(desc, kk[:, 0:NE], -1.0, float(NE), ALU.mult, ALU.add))
            dve.wait_ge(q["r_gate"], 1)
            then(dve.tensor_reduce(den, t_ex, AX.X, ALU.add))
            then(dve.reciprocal(den, den))
            then(dve.tensor_tensor(t_gate, t_ex, wide(den), ALU.mult))

            def pick(gate, out, choice):
                then(dve.tensor_reduce(out, gate, AX.X, ALU.max))
                then(dve.tensor_tensor(t_eq, gate, wide(out), ALU.is_equal))
                then(dve.tensor_tensor(t_eq, t_eq, every(desc), ALU.mult))
                then(dve.tensor_reduce(tie, t_eq, AX.X, ALU.max))
                then(dve.tensor_tensor(choice, t_eq, wide(tie), ALU.is_equal))

            pick(t_gate, gates[0], t_first)
            then(dve.scalar_tensor_tensor(out=t_gate, in0=t_first, scalar=-2.0, in1=t_gate, op0=ALU.mult, op1=ALU.add))
            pick(t_gate, gates[1], t_second)
            then(dve.tensor_tensor(t_sel, t_first, t_second, ALU.add))
            assert route[0] == N_PICKED
            dve.wait_ge(q["r_pref"], 1)
            tot = bank[2][:, NT * NE:2 * NT * NE].rearrange("p (t e) -> p t e", e=NE)
            then(dve.tensor_copy(t_in, tot))
            run, nxt, s = t_in, t_lg, 1
            while s < NT:
                then(dve.tensor_copy(nxt[:, 0:s], run[:, 0:s]))
                then(dve.tensor_tensor(nxt[:, s:NT], run[:, s:NT], run[:, 0:NT - s], ALU.add))
                run, nxt, s = nxt, run, 2 * s
            k128 = sm[:, 0:NT]
            then(dve.tensor_scalar(k128, kk[:, 0:NT], float(P), None, ALU.mult))
            cmp = t_eq.rearrange("p t e -> p (t e)").rearrange("p (e t) -> p e t", t=NT)
            then(dve.tensor_tensor(cmp, run[:, NT - 1, :].unsqueeze(2).broadcast_to([P, NE, NT]),
                                   k128.unsqueeze(1).broadcast_to([P, NE, NT]), ALU.is_gt))
            small = [sm[:, 2 * NT + NE * i:2 * NT + NE * (i + 1)] for i in range(4)]
            blk = small[0]
            then(dve.tensor_reduce(blk, cmp, AX.X, ALU.add))
            cur, oth, s = small[1], small[2], 1
            then(dve.tensor_copy(cur, blk))
            while s < NE:
                then(dve.tensor_copy(oth[:, 0:s], cur[:, 0:s]))
                then(dve.tensor_tensor(oth[:, s:NE], cur[:, s:NE], cur[:, 0:NE - s], ALU.add))
                cur, oth, s = oth, cur, 2 * s
            start, base = oth, small[3]
            then(dve.tensor_tensor(start, cur, blk, ALU.subtract))
            then(dve.tensor_scalar(base, start, float(P), None, ALU.mult))
            then(dve.tensor_tensor(t_place, run, tot, ALU.subtract))
            then(dve.tensor_tensor(t_place, t_place, bank[2][:, 0:NT * NE].rearrange("p (t e) -> p t e", e=NE), ALU.add))
            then(dve.tensor_tensor(t_place, t_place, every(base), ALU.add))
            for a, choice in enumerate((t_first, t_second)):
                then(dve.tensor_tensor(t_eq, choice, t_place, ALU.mult))
                then(dve.tensor_reduce(mx, t_eq, AX.X, ALU.add))
                then(dve.tensor_copy(rec[:, a, :, 0].bitcast(U32), mx))
                then(dve.tensor_copy(rec[:, a, :, 2], gates[a]))
            big = area(plain, 3 * C * D + 8 * D + NT * NE, NB, NE)
            bsum = row[:, 0:NB]
            then(dve.tensor_tensor(big, kk[:].unsqueeze(2).broadcast_to([P, NB, NE]), start.unsqueeze(1).broadcast_to([P, NB, NE]), ALU.is_ge))
            then(dve.tensor_reduce(bsum, big, AX.X, ALU.add))
            then(dve.tensor_scalar(bexp, bsum, -1.0, None, ALU.add))
            dve.memset(lst, 0.0).then_inc(q["r_zero"], 1)

            dve.wait_ge(q["f_whi"], 1)
            dve.scalar_tensor_tensor(out=wqkv[1][:, :, 0:D], in0=wraw[:, :, 0:D], scalar=HD ** -0.5, in1=full(wqkv[0][:, :, 0:D]),
                                     op0=ALU.mult, op1=ALU.subtract).then_inc(q["f_wready"], 1)
            dve.wait_ge(q["f_whi"], 2)
            dve.tensor_tensor(wqkv[1][:, :, D:Q3], wraw[:, :, D:Q3], full(wqkv[0][:, :, D:Q3]), ALU.subtract).then_inc(q["f_wready"], 1)

            def split(b, item, n, hn, bank_in):
                if item[0] == "V":
                    t = int(item[1])
                    if t == 0:
                        await_ge(dve, "f_v_in", n // len(ITEMS) * 16 if isinstance(n, int) else b * 16 + 16)
                    dve.wait_ge(q["f_d_full"], n + 1)
                    dve.tensor_tensor(Vst[:, t, :], bank_in[:], bvf[:], ALU.add).then_inc(q["f_d_free"], 1)
                    return
                dve.wait_ge(q["f_d_hi"], hn + 1)
                if item[0] == "H":
                    t = int(item[1])
                    cols = slice(t * P, (t + 1) * P)
                    dve.tensor_tensor(fT[1][:, :, cols], bank_in[:].rearrange("p (c n) -> p c n", c=C),
                                      full(fT[0][:, :, cols]), ALU.subtract).then_inc(q["f_d_free"], 1)
                else:
                    i, m = piece(item)
                    h = 1 if item[0] == "R" else 0
                    dve.scalar_tensor_tensor(out=qkp[i][m][1], in0=bank_in[:], scalar=bqk[:, i * C + 2 * h + m:i * C + 2 * h + m + 1],
                                             in1=full(qkp[i][m][0]), op0=ALU.add, op1=ALU.subtract).then_inc(q["f_d_free"], 1)

            def maxes(b, k, ts):
                for t in ts:
                    dve.wait_ge(q["f_s_full"], (b * NH + k) * T + t + 1)
                    dve.tensor_reduce(nmx[:, k, t:t + 1], bank[SB[t]][:], AX.X, ALU.max, negate=True).then_inc(q["f_max"], 1)

            def turned(b, k, c):
                if c == 1:
                    await_ge(dve, "f_pv", b * NG + k // HG)
                dve.wait_ge(q["f_t_full"], (b * NH + k) * T + c + 1)
                dve.tensor_copy(PT[k % HG][:, c, :], bank[c % 2][:]).then_inc(q["f_pt_d"], 1)

            def finish(b, g):
                hs = slice(g * HG, (g + 1) * HG)
                dve.wait_ge(q["f_exp"], b * NH * T + T * HG * (g + 1))
                dve.reciprocal(rZ[:, :, hs], Z[:, :, hs]).then_inc(q["f_rz"], 1)
                dve.wait_ge(q["f_rz"], b * NG + g + 1)
                dve.wait_ge(q["f_ot"], b * NG + g + 1)
                if g % 2 == 0:
                    await_ge(dve, "f_att_out", (2 * b + g // 2) * 16)
                for m in range(2):
                    ins = dve.tensor_tensor(
                        tmp[:, :, m * P + g % 2 * 2 * HD:m * P + (g % 2 + 1) * 2 * HD].rearrange("p t (j d) -> p t j d", j=2),
                        bank[6][:].rearrange("p (t j d) -> p t j d", t=T, j=HG)[:, :, 2 * m:2 * m + 2],
                        rZ[:, :, g * HG + m:g * HG + m + 3:2].unsqueeze(3).broadcast_to([P, T, 2, HD]), ALU.mult)
                ins.then_inc(q["f_o_fin"], 1)

            def batch(b, first, last):
                for k in range(NH):
                    before = (b, k - 1) if k else (b - 1, NH - 1)
                    for work in plan(k, "dve", first, last):
                        if work[0] == "m":
                            maxes(b, k, (int(work[1]),))
                        elif work[0] == "t":
                            turned(*before, int(work[1]))
                        elif work in ITEMS:
                            split(b, work, *number(b, work), bank[DB[0]])
                        elif work[0:2] == "OT":
                            finish(b - 1 if work == "OT3" else b, int(work[2]))

            for item in BEFORE:
                n, hn = early(item)
                split(0, item, n, hn, bank[DB[n % len(DB)]])
            batch(0, True, False)
            with dve.Fori(1, B - 1) as b:
                batch(b, False, False)
            batch(B - 1, False, True)
            turned(B - 1, NH - 1, 1)
            turned(B - 1, NH - 1, 3)
            finish(B - 1, NG - 1)

            for e in range(NE):
                dve.wait_ge(q["m_ehi"], e + 1)
                dve.tensor_tensor(ew[e][:, 1], eraw[e % 2], full(ew[e][:, 0]), ALU.subtract).then_inc(q["m_elo"], 1)

            def rows_lo(i, k):
                dve.wait_ge(q["m_hi"], i + 1)
                dve.tensor_tensor(gT[k][:, 1].rearrange("p c n -> p (c n)"), bank[k][:],
                                  full(gT[k][:, 0].rearrange("p c n -> p (c n)")), ALU.subtract).then_inc(q["m_hT"], 1)

            def blocks(n, more):
                for k in range(2):
                    i = 2 * n + k
                    if more or k == 0:
                        rows_lo(i + 1, 1 - k)
                    e = dve.value_load(bexp[0:1, bass.ds(i, 1)], min_val=0, max_val=NE - 1)
                    dve.wait_ge(q["m_full"], i + 1)
                    dve.wait_ge(q[f"m_out{k}"], n * 16)
                    dve.tensor_tensor(ysb[k], bank[2 + k][:], be_all[:, bass.ds(e * D, D)], ALU.add).then_inc(q["m_sum"], 1)

            dve.wait_ge(q["in_be"], 16)
            dve.wait_ge(q["in_list"], 16)
            rows_lo(0, 0)
            with dve.Fori(0, NB // 2 - 1) as n:
                blocks(n, True)
            blocks(NB // 2 - 1, False)

            with dve.Fori(0, NT // 2) as n:
                for k in range(2):
                    i = 2 * n + k
                    dve.wait_ge(q[f"c_x{k}"], 16 * n + 16)
                    dve.wait_ge(q[f"c_a{k}"], 16 * n + 16)
                    dve.tensor_tensor(fin[k][0], fin[k][0], fin[k][1], ALU.add).then_inc(q["c_pair"], 1)
                    dve.wait_ge(q[f"c_g{k}"], 32 * n + 32)
                    dve.tensor_tensor(fin[k][2], fin[k][2], fin[k][3], ALU.add).then_inc(q["c_pair"], 1)
                    dve.wait_ge(q["c_pair"], 2 * i + 2)
                    dve.tensor_tensor(fin[k][0], fin[k][0], fin[k][2], ALU.add).then_inc(q["c_sum"], 1)


_INS = ("x", "ctx_1024", "L0_xattn_Wq", "L0_xattn_bq", "L0_xattn_Wk", "L0_xattn_bk", "L0_xattn_Wv", "L0_xattn_bv",
        "L0_ffn_W_qkv", "L0_ffn_b_qkv", "L0_ffn_W_gate", "L0_ffn_b_gate", "L0_ffn_W_experts", "L0_ffn_b_experts")
_OUTS = (((8, 512, 512), "float32"),)


def kernel(**inputs):
    import numpy as _np
    import concourse.bacc as _bacc
    from concourse import mybir as _mybir
    from concourse.bass_utils import run_bass_kernel_spmd as _run

    nc = _bacc.Bacc("TRN2", target_bir_lowering=False, num_devices=1)
    arrays, args = {}, []
    for name in _INS:
        a = _np.ascontiguousarray(inputs[name])
        arrays[f"in_{name}_dram"] = a
        args.append(nc.dram_tensor(f"in_{name}_dram", a.shape, _mybir.dt.from_np(a.dtype), kind="ExternalInput").ap())
    for i, (shape, dtype) in enumerate(_OUTS):
        dt = _mybir.dt.from_np(_np.dtype(dtype))
        args.append(nc.dram_tensor(f"out_{i}_dram", shape, dt, kind="ExternalOutput").ap())
    program(nc, *args)
    r = _run(nc, [arrays], core_ids=[0])
    got = tuple(r.results[0][f"out_{i}_dram"] for i in range(len(_OUTS)))
    return got[0]
```

```python
from contextlib import ExitStack
import numpy as np
import concourse.bass as bass
from concourse import mybir

P = 128
ALU = mybir.AluOpType
ACT = mybir.ActivationFunctionType
AX = mybir.AxisListType
F32 = mybir.dt.float32
F32R = mybir.dt.float32r
U32 = mybir.dt.uint32
I32 = mybir.dt.int32


def program(nc, x, ctx, wq, bq, wk, bk, wv, bv, w_qkv, b_qkv, w_gate, b_gate, w_exp, b_exp, out):
    B, S, D = x.shape
    E = ctx.shape[1]
    C = D // P
    T = S // P
    W = E + 1
    HB = B // 2
    NE = w_gate.shape[1]
    EPS = 1e-5
    NB = B * T * 2 + NE - 1
    NB += -NB % 4
    h2_dram = nc.dram_tensor("h2_rows", (B * S, D), F32, kind="Internal").ap()
    slot_dram = nc.dram_tensor("slot_list", (NB * P, 2), F32, kind="Internal").ap()
    we_dram = nc.dram_tensor("expert_weights", w_exp.shape, F32, kind="Internal").ap()
    with ExitStack() as stack:
        def sb(name, shape, dt=F32):
            return stack.enter_context(nc.sbuf_tensor(name, shape, dt))

        def sem(name):
            return stack.enter_context(nc.semaphore(name))

        banks = [stack.enter_context(nc.psum_tensor(f"banks{i}", [P, 2, 512], F32)) for i in range(4)]
        bank = [banks[i // 2][:, i % 2] for i in range(8)]
        PARTS, PLAIN = 34816, 15872
        parts = sb("parts", [P, PARTS], F32R)
        plain = sb("plain", [P, PLAIN])

        def area(arena, at, *shape):
            n = int(np.prod(shape))
            assert at + n <= (PARTS if arena is parts else PLAIN), (at, n)
            v = arena[:, at:at + n]
            if len(shape) == 2:
                v = v.rearrange("p (a b) -> p a b", a=shape[0])
            if len(shape) == 3:
                v = v.rearrange("p (a b c) -> p a b c", a=shape[0], b=shape[1])
            return v

        def pair(at, *shape):
            n = int(np.prod(shape))
            return area(parts, at, *shape), area(parts, at + n, *shape)

        def full(part):
            return part.bitcast(F32)

        CTX = C * B * W
        wqT = pair(0, C, D)
        wkT = pair(2 * C * D, C, D)
        vext = pair(0, B, D)
        wkp = pair(4 * C * D, C, D)
        A = pair(4 * C * D, C, D)
        wvp = pair(6 * C * D, C, D)
        r0 = 8 * C * D
        G = area(parts, r0, C * B, 2, W)
        KE = pair(r0 + 2 * CTX, C, B * W)
        eT = pair(r0 + 4 * CTX, C, B * W)
        hT = [pair(r0 + 4 * CTX + 2 * C * P * i, C, P) for i in range(2)]
        h2T = [pair(r0 + 4 * CTX + 2 * C * P * (2 + i), C, P) for i in range(2)]
        pT = pair(r0 + 4 * CTX + 8 * C * P, P)
        gw = area(parts, r0 + 6 * CTX, C, 2, NE)
        bqrep = pair(r0 + 6 * CTX + 2 * C * NE, C, P)
        wst = [area(plain, C * D * i, C, D) for i in range(3)]
        est = area(plain, 3 * C * D, B, D)
        p0 = 3 * C * D
        x1 = area(plain, p0, T, D)
        h = area(plain, p0 + T * D, 2, D)
        h2 = area(plain, p0 + (T + 2) * D, 2, D)
        p0 += B * D
        vst = area(plain, p0, D)
        gst = area(plain, p0, HB, W)
        scr = area(plain, p0, D)
        bv_all = area(plain, p0 + D, D)
        xin = area(plain, p0 + 2 * D, T, D)
        Q3 = w_qkv.shape[1]
        HD = 32
        NH = D // HD
        HG = P // HD
        NG = NH // HG
        wqkv = pair(0, C, Q3)
        r1 = 2 * C * Q3
        fT = pair(r1, C, S)
        r1 += 2 * C * S
        qkp = [[[area(parts, r1 + S * (4 * i + 2 * m + part), S) for part in range(2)] for m in range(2)] for i in range(2)]
        qk2 = [[parts[:, r1 + S * (4 * i + part):r1 + S * (4 * i + part + 4)].rearrange("p (m x) -> p m x", m=2)[:, :, 0:S]
                for part in range(2)] for i in range(2)]
        r1 += 8 * S
        NSLOT = 5
        stk = [[area(parts, r1 + 2 * S * (2 * s + i), 2, S) for i in range(2)] for s in range(NSLOT)]
        r1 += 4 * S * NSLOT
        h2f = full(area(parts, r1, T, D))
        r1 += T * D
        V = full(area(parts, r1, T, D))
        wraw = area(plain, 0, C, Q3)
        PT = [area(plain, T * S * j, T, S) for j in range(HG)]
        p1 = HG * T * S
        p3 = p1 + 2 * T * S - 2 * S
        nmx = area(plain, p3, NH, T)
        Z = area(plain, p3 + NH * T, T, NH)
        rZ = area(plain, p3 + 2 * NH * T, T, NH)
        own = area(plain, p1 + 2 * T * S - S, T, P)
        p1 += 2 * T * S
        Vst = area(plain, p1, T, D)
        p1 += T * D
        Osb = area(plain, p1, S)
        tmp = area(plain, p1 + S, T, D // 2)
        bvf = sb("bias_v_all", [P, D])
        bqk = sb("bias_qk_cols", [P, 2 * C])
        nparts = sb("neg_max_parts", [P, 2, T], F32R)
        M0, M1 = 3 * HD, 3 * HD + 2 * T

        ident = sb("ident", [P, P])
        ones = sb("ones", [P, P])
        sbias = sb("score_bias", [P, B * W])
        bqc = sb("bq_cols", [P, C])
        bkc = sb("bk_cols", [P, C])
        cq = sb("cq", [P, 2 * C])
        gws = sb("gate_stage", [P, C, NE])
        st1 = sb("st1", [P, 2, 6]); st2 = sb("st2", [P, 2, 6])
        mo1 = sb("mo1", [P, 2, 6]); mo2 = sb("mo2", [P, 2, 6])
        cst = sb("consts", [P, 3])
        fence = sb("fence", [P, 8])
        sc = sb("sc", [P, 2, W])
        NB = B * T * 2 + NE - 1
        NB += -NB % 4
        NT = B * T
        temp = [area(plain, 3 * C * D + T * D + i * NT * NE + (D * 2 if i >= 4 else 0), NT, NE) for i in range(10)]
        rec = sbias[:, 0:2 * NT * 3].rearrange("p (k t c) -> p k t c", k=2, c=3)
        lst = sbias[:, 6 * NT:6 * NT + 2 * NB].rearrange("p (i c) -> p i c", c=2)
        bexp = sbias[:, 6 * NT + 2 * NB:6 * NT + 3 * NB].bitcast(U32)
        zrec = sbias[:, 6 * NT + 3 * NB:6 * NT + 3 * NB + 2 * NT].rearrange("p (t c) -> p t c", c=2)
        assert 8 * NT + 3 * NB <= B * W
        tok = sb("token_numbers", [P, NT])
        iot = sb("count_int", [P, NB], I32)
        kk = sb("count", [P, NB])
        tri = sb("strict_triangle", [P, P])
        bg_all = sb("bias_gate_all", [P, NE])
        recs = sb("records", [P, 4, 3])
        zrecs = sb("filler_records", [P, 2, 2])
        zslots = sb("filler_slots", [P, 2, NE], U32)
        idx = sb("row_numbers", [P, 8], U32)
        EW = 2 * C * D
        ew = [area(parts, EW * e, 2, C, D) for e in range(NE)]
        gT = [area(parts, EW * NE + 2 * C * P * i, 2, C, P) for i in range(2)]
        p2 = 2 * C * D
        be_all = area(plain, p2, NE * D)
        p2 += NE * D
        rows = [area(plain, p2 + D * i, D) for i in range(4)]
        ysb = [area(plain, p2 + D * (4 + i), D) for i in range(4)]
        col = sb("col", [P, 2, 4])
        glog = sb("glog", [P, B * T, NE])

        names = """in_wk in_wq in_wv in_ctx in_bias made_ident made_ones made_consts w_hi w_ready set_full set_hi set_staged set_free ln1_stats
        ln1_var ln1_eps ln1_pow ln1_neg ln1_rstd h_ready h_tr hT_hi hT_ready s_full s_step s_max s_exp s_den p_ready p_tr pT_hi pT_ready
        e_full v_full x1_part x1_ready ln2_stats ln2_var ln2_eps ln2_pow ln2_neg ln2_rstd h2_ready h2_tr h2T_hi h2T_ready g_full g_copied
        in_wqkv in_fb f_wscaled f_whi f_wready f_raw f_d_full f_d_hi f_d_free f_v_in f_stack0 f_stack1 f_stack2 f_stack3 f_stack4 f_ones
        f_s_full f_max f_nhi f_nparts f_n_tr f_n_in f_exp f_t_full f_pt f_pv f_o_sb f_ot f_rz f_o_fin x_in0 x_in1 x_in2 x_in3 in_bg
        sp_went_on pool_went_on made_count made_own route r_gate r_pref r_zero r_zeroed r_tokens r_copied r_scat0 r_scat1 r_scat2 r_scat3
        in_list in_be ew_moved in_ew0 in_ew1 in_ew2 in_ew3 in_ew4 in_ew5 in_ew6 in_ew7 m_early_hi m_ehi m_elo m_idx m_rows0 m_rows1
        m_rows2 m_rows3 m_tr m_hi m_hT m_full m_sum m_y m_added m_to z_copied z_scat0 z_scat1 f_att_out x1_out0 x1_out1 x1_out2 x1_out3
        h2_out0 h2_out1""".split()
        q = {n: sem(n) for n in names}
        block = stack.enter_context(nc.Block())
        x_t = x.rearrange("b (t p) d -> (b t) p d", p=P)
        h2_t = h2_dram.rearrange("(t p) d -> t p d", p=P)
        out_t = out.rearrange("b (t p) d -> (b t) p d", p=P)
        out_b = out.rearrange("b (t p) d -> b p t d", p=P)
        out_rows = out.rearrange("b s d -> (b s) d")

        def prod3(pe, out, stat, mov, first, last):
            pe.matmul(out, stat[0], mov[0], start=first, stop=False)
            pe.matmul(out, stat[0], mov[1], start=False, stop=False)
            return pe.matmul(out, stat[1], mov[0], start=False, stop=last)

        def at(p, *idx):
            return p[0][idx], p[1][idx]

        n_wqT, n_wkT, n_eT, n_KE = 0, C, 2 * C, 2 * C + B
        n_A = n_KE + 2 * C
        n_cq = n_A + C
        n_G = n_cq + 1
        n_sb = n_G + 2 * C
        n_ve = n_sb + 2
        n_end = n_ve + B

        PLAN = ["R0", "PV3", "R1", "R2 OT3", "R3", "PV0 H0 H1 H2 H3", "V0", "V1 OT0", "N0", "PV1", "N1", "N2 OT1", "N3", "PV2", "V2", "V3 OT2"]
        ITEMS = ["R0", "R1", "R2", "R3", "H0", "H1", "H2", "H3", "V0", "V1", "N0", "N1", "N2", "N3", "V2", "V3"]
        HIS = [item for item in ITEMS if item[0] != "V"]
        BEFORE = sorted(ITEMS[4:], key=lambda item: "HNV".index(item[0]))
        DB = (2, 3, 4, 5, 7)
        SB = (3, 4, 5, 7)
        FILL = 6 * 16

        def number(b, item):
            return len(BEFORE) + len(ITEMS) * b + ITEMS.index(item), len(HIS) - 4 + len(HIS) * b + HIS.index(item) if item in HIS else None

        def early(item):
            return BEFORE.index(item), HIS.index(item) - 4 if item in HIS else None

        STEP = {
            "dense": {"pe": "S0 S1 T2@2 n@1 S2 Da S3 OT T0@1 Db",
                      "act": "E3@1 t2@2 E0 E1 t0@1 D E2",
                      "dve": "s@1 D@1 m0 n@1 m1 m2 m3 OT"},
            "PV": {"pe": "T2@2 S0 n@1 S1 S2 PVa S3 T0@1 PVb",
                   "act": "t2@2 E3@1 E0 E1 t0@1 E2 PV",
                   "dve": "s@1 n@1 D@1 m0 m1 m2 m3"},
            "PV H": {"pe": "T2@2 S0 n@1 S1 H0 S2 T0@1 H1 PVa H2 PVb S3 H3",
                     "act": "t2@2 H0 E3@1 H1 E0 t0@1 H2 E1 E2 H3 PV",
                     "dve": "s@1 D@1 n@1 H0 m0 H1 m1 m2 H2 m3"}}

        def plan(b, k, engine, first, last):
            work = PLAN[k].split()
            kind = "PV H" if "H0" in work else work[0][0:2] if "PV" in work[0] else "dense"
            for token in STEP[kind][engine].split():
                what, _, lag = token.partition("@")
                of, head = (b, k - int(lag or 0)) if k >= int(lag or 0) else (b - 1, k - int(lag) + NH)
                if first and of is not b:
                    continue
                if what[0] == "D":
                    item = [w for w in PLAN[head].split() if w in ITEMS][-1:]
                    if not item or (last and of is b and item[0][0] in "HNV") or (engine == "act" and item[0] not in HIS):
                        continue
                    what = item[0] + what[1:]
                elif what[0:2] in ("OT", "PV"):
                    g = [w for w in work if w[0:2] == what[0:2]]
                    if not g or (first and g[0][2] == "3"):
                        continue
                    of, head, what = (b - 1 if g[0][2] == "3" else b), int(g[0][2]), g[0][0:2] + what[2:]
                elif what[0] == "H" and last:
                    continue
                yield what, of, head

        def await_ge(eng, name, value):
            if not isinstance(value, int) or value > 0:
                eng.wait_ge(q[name], value)

        def piece(item):
            return int(item[1]) // 2, int(item[1]) % 2

        def batches(eng, steps):
            steps(0, "first")
            with eng.Fori(1, B - 1) as b:
                steps(b, "middle")
            steps(B - 1, "last")
            steps(B, "after")

        def tile(b, t, d, part):
            u = t + d
            if (part == "first" and u < 0) or (part == "last" and u >= T) or (part == "after" and u >= 0):
                return None
            return b * T + u, u % T, b + u // T

        def stack_use(b, h, j):
            if j < 3:
                return j, 2 * b + h, T * (8 * (2 * b + h) - 8 + 2 * j + 2)
            return 3 + h, b, T * (16 * b - 16 + 8 * h + 8)

        N_PICKED = 19
        EARLY = NE // 2

        @block.sync
        def _(sp):
            for w, to, name in ((wk, 1, "in_wk"), (wq, 0, "in_wq"), (wv, 2, "in_wv")):
                sp.dma_start(wst[to], w.rearrange("(c p) n -> p c n", p=P)).then_inc(q[name], 16)
            for t in range(T):
                sp.dma_start(xin[:, t, :], x_t[t]).then_inc(q[f"x_in{t}"], 16)

            sp.wait_ge(q["set_free"], n_end)
            sp.dma_start(wraw, w_qkv.rearrange("(c p) n -> p c n", p=P)).then_inc(q["in_wqkv"], 16)
            sp.dma_start(bqk[:], b_qkv.rearrange("(c p) -> p c", p=P)[:, 0:2 * C], allow_slow_non_contiguous=True).then_inc(q["in_fb"], 16)
            sp.dma_start(bvf[:], b_qkv.rearrange("(a n) -> a n", a=3)[2:3, :].broadcast_to([P, D])).then_inc(q["in_fb"], 16)

            def tiles(b, more):
                for t in range(T):
                    if more:
                        sp.wait_ge(q["x1_part"], b * T + t + 1)
                        sp.dma_start(xin[:, t, :], x_t[b * T + t + T]).then_inc(q[f"x_in{t}"], 16)
                    sp.wait_ge(q["x1_ready"], b * T + t + 1)
                    sp.dma_start(out_t[b * T + t], x1[:, t, :]).then_inc(q[f"x1_out{t}"], 16)
                    sp.wait_ge(q["h2_ready"], b * T + t + 1)
                    sp.dma_start(h2_t[b * T + t], h2[:, t % 2, :]).then_inc(q[f"h2_out{t % 2}"], 16)

            with sp.Fori(0, B - 1) as b:
                tiles(b, True)
            sp.dma_start(we_dram, w_exp).then_inc(q["ew_moved"], 16)
            tiles(B - 1, False)
            for t in range(T):
                sp.wait_ge(q[f"x1_out{t}"], 16 * B)
            for t in range(2):
                sp.wait_ge(q[f"h2_out{t}"], 16 * B * T // 2)

            h2_b = h2_dram.rearrange("(b t p) d -> b p t d", p=P, t=T)

            def stacks(b, h, i, js, n):
                await_ge(sp, "f_d_free", n)
                for j in js:
                    slot, fills, used = stack_use(b, h, j)
                    sp.sem_inc(q["sp_went_on"], 1)
                    await_ge(sp, "f_t_full", used)
                    for k, part in enumerate(((0, 0, 1), (0, 1, 0))[i]):
                        sp.dma_start(full(stk[slot][i][k * HD:(k + 1) * HD]),
                                     full(qk2[i][part][j * HD:(j + 1) * HD])).then_inc(q[f"f_stack{slot}"], 16)

            sp.wait_ge(q["g_full"], NT)
            sp.dma_start(h2f, h2_b[0]).then_inc(q["f_raw"], 16)
            for js in ((0, 1), (2, 3)):
                stacks(0, 0, 0, js, early("N1")[0] + 1)
                stacks(0, 0, 1, js, early("N3")[0] + 1)
            sp.wait_ge(q["r_zero"], 1)
            sp.dma_start(slot_dram.rearrange("(p i) c -> p i c", p=P), lst).then_inc(q["r_zeroed"], 16)

            def batch(b, first, last):
                if not last:
                    sp.wait_ge(q["f_d_full"], early("H3")[0] + 1 if first else number(b - 1, "H3")[0] + 1)
                    sp.sem_inc(q["sp_went_on"], 1)
                    sp.dma_start(h2f, h2_b[b + 1]).then_inc(q["f_raw"], 16)
                sp.wait_ge(q["f_d_free"], number(b, "R0")[0])
                sp.sem_inc(q["sp_went_on"], 1)
                await_ge(sp, "f_pv", 2 * b * NG)
                sp.dma_start(V, Vst).then_inc(q["f_v_in"], 16)
                for js in ((0, 3, 1), (2,)):
                    stacks(b, 1, 0, js, number(b, "R1")[0] + 1)
                    stacks(b, 1, 1, js, number(b, "R3")[0] + 1)
                if not last:
                    for js in ((0, 3, 1), (2,)):
                        stacks(b + 1, 0, 0, js, number(b, "N1")[0] + 1)
                        stacks(b + 1, 0, 1, js, number(b, "N3")[0] + 1)

            batch(0, True, False)
            with sp.Fori(1, B - 1) as b:
                batch(b, False, False)
            batch(B - 1, False, True)

            def read_list():
                for k in range(4):
                    sp.wait_ge(q[f"r_scat{k}"], 16 * NT // 2)
                for k in range(2):
                    sp.wait_ge(q[f"z_scat{k}"], 16 * NE * NT // 2)
                sp.dma_start(lst, slot_dram.rearrange("(i p) c -> p i c", p=P)).then_inc(q["in_list"], 16)

            read_list()
            sp.wait_ge(q["f_t_full"], B * NH * T)
            for e in range(EARLY, NE):
                sp.dma_start(full(ew[e][:, 1]), we_dram[e].rearrange("(c p) n -> p c n", p=P)).then_inc(q[f"in_ew{e}"], 16)
            sp.wait_ge(q["f_pv"], 2 * B * NG)
            sp.dma_start(be_all, b_exp.rearrange("(a e) n -> a (e n)", a=1).broadcast_to([P, NE * D])).then_inc(q["in_be"], 16)

            sp.wait_ge(q["m_added"], 16 * NB)

        @block.gpsimd
        def _(pool):
            pool.memset(ident[:], 0.0).then_inc(q["made_ident"], 1)
            pool.wait_ge(q["made_ident"], 1)
            pool.affine_select(out=ident[:], in_=ident[:], compare_op=ALU.not_equal, fill=1.0, base=0,
                               pattern=[[-1, P]], channel_multiplier=1).then_inc(q["made_ident"], 1)
            pool.memset(ones[:], 1.0).then_inc(q["made_ones"], 1)
            pool.wait_ge(q["made_ones"], 1)
            pool.memset(full(eT[0].rearrange("p c (b w) -> p (c b) w", w=W)[:, :, E:W]), 0.0).then_inc(q["made_ones"], 1)
            pool.memset(full(eT[1].rearrange("p c (b w) -> p (c b) w", w=W)[:, :, E:W]), 0.0).then_inc(q["made_ones"], 1)
            pool.memset(cst[:, 0:1], EPS).then_inc(q["made_consts"], 1)
            pool.memset(cst[:, 1:2], -0.5).then_inc(q["made_consts"], 1)
            pool.memset(cst[:, 2:3], -1.0).then_inc(q["made_consts"], 1)
            pool.wait_ge(q["made_consts"], 3)
            pool.affine_select(out=tri[:], in_=ones[:], compare_op=ALU.is_gt, fill=0.0, base=0,
                               pattern=[[1, P]], channel_multiplier=-1).then_inc(q["made_count"], 1)
            pool.iota(iot[:], pattern=[[1, NB]], base=0, channel_multiplier=0).then_inc(q["made_count"], 1)
            pool.wait_ge(q["made_count"], 2)
            pool.tensor_copy(kk[:], iot[:]).then_inc(q["made_count"], 1)
            pool.wait_ge(q["made_count"], 3)
            pool.iota(iot[:, 0:NT], pattern=[[P, NT]], base=0, channel_multiplier=1).then_inc(q["made_count"], 1)
            pool.wait_ge(q["made_count"], 4)
            pool.tensor_copy(tok[:], iot[:, 0:NT]).then_inc(q["made_count"], 1)
            pool.wait_ge(q["made_count"], 5)
            pool.iota(iot[:], pattern=[[1, NB]], base=0, channel_multiplier=NB).then_inc(q["made_count"], 1)

            def rstd(mo, ln, i, slot):
                pool.wait_ge(q[f"{ln}_var"], i + 1)
                pool.tensor_tensor(mo[:, slot, 2:3], mo[:, slot, 1:2], cst[:, 0:1], ALU.add).then_inc(q[f"{ln}_eps"], 1)
                pool.tensor_tensor(mo[:, slot, 4:5], mo[:, slot, 0:1], cst[:, 2:3], ALU.mult).then_inc(q[f"{ln}_neg"], 1)
                pool.wait_ge(q[f"{ln}_eps"], i + 1)
                pool.tensor_tensor(mo[:, slot, 3:4], mo[:, slot, 2:3], cst[:, 1:2], ALU.pow).then_inc(q[f"{ln}_pow"], 1)
                pool.wait_ge(q[f"{ln}_neg"], i + 1)
                pool.wait_ge(q[f"{ln}_pow"], i + 1)
                pool.tensor_tensor(mo[:, slot, 5:6], mo[:, slot, 4:5], mo[:, slot, 3:4], ALU.mult).then_inc(q[f"{ln}_rstd"], 1)

            def steps(b, part):
                for t in range(T):
                    if now := tile(b, t, 2, part):
                        rstd(mo1, "ln1", now[0], now[1] % 2)
                    if now := tile(b, t, -1, part):
                        rstd(mo2, "ln2", now[0], now[1] % 2)

            rstd(mo1, "ln1", 0, 0)
            rstd(mo1, "ln1", 1, 1)
            batches(pool, steps)

            pool.wait_ge(q["x1_part"], NT)
            pool.memset(own, 0.0).then_inc(q["made_own"], 1)
            for part in range(2):
                pool.wait_ge(q["made_own"], 1 + part)
                pool.affine_select(out=own, in_=own, compare_op=ALU.not_equal, fill=1.0, base=-M0 - part * T,
                                   pattern=[[-1, T], [0, P]], channel_multiplier=1).then_inc(q["made_own"], 1)

            pool.wait_ge(q["r_zero"], 1)
            pool.iota(rec[:, :, :, 1].bitcast(I32), pattern=[[0, 2], [P, NT]], base=0, channel_multiplier=1).then_inc(q["r_tokens"], 1)
            pool.iota(zrec[:, :, 0].bitcast(I32), pattern=[[P, NT]], base=0, channel_multiplier=1).then_inc(q["r_tokens"], 1)
            pool.wait_ge(q["r_tokens"], 2)
            pool.wait_ge(q["r_zeroed"], 16)

            def place(b, h):
                m = 2 * b + h
                for k in range(4):
                    await_ge(pool, f"r_scat{k}", m * 16)
                    pool.sem_inc(q["pool_went_on"], 1)
                    pool.tensor_copy(recs[:, k:k + 1, :], rec.rearrange("p k t c -> p (k t) c")[:, bass.ds(4 * m + k, 1), :]).then_inc(q["r_copied"], 1)
                    pool.wait_ge(q["r_copied"], 4 * m + k + 1)
                    pool.sem_inc(q["pool_went_on"], 1)
                    pool.indirect_dma_start(out=slot_dram, out_offset=bass.IndirectOffsetOnAxis(ap=recs[:, k, 0:1].bitcast(U32), axis=0),
                                            in_=recs[:, k, 1:3], in_offset=None).then_inc(q[f"r_scat{k}"], 16)
                for k in range(2):
                    await_ge(pool, f"z_scat{k}", m * 16 * NE)
                    pool.sem_inc(q["pool_went_on"], 1)
                    pool.tensor_copy(zrecs[:, k:k + 1, :], zrec[:, bass.ds(2 * m + k, 1), :]).then_inc(q["z_copied"], 1)
                    pool.tensor_copy(zslots[:, k:k + 1, :], glog[:, bass.ds(2 * m + k, 1), :].bitcast(U32)).then_inc(q["z_copied"], 1)
                    pool.wait_ge(q["z_copied"], 4 * m + 2 * k + 2)
                    pool.sem_inc(q["pool_went_on"], 1)
                    for e in range(NE):
                        pool.indirect_dma_start(out=slot_dram, out_offset=bass.IndirectOffsetOnAxis(ap=zslots[:, k, e:e + 1], axis=0),
                                                in_=zrecs[:, k, :], in_offset=None, bounds_check=NB * P - 1,
                                                oob_is_err=False).then_inc(q[f"z_scat{k}"], 16)

            for t in range(T):
                pool.wait_ge(q[f"x1_out{t}"], 16 * B)

            def attended(b, h):
                pool.wait_ge(q["f_o_fin"], b * NG + 2 * h + 2)
                pool.sem_inc(q["pool_went_on"], 1)
                pool.dma_start(out_b[b][:, :, h * (D // 2):(h + 1) * (D // 2)], tmp, accum_op=ALU.add).then_inc(q["f_att_out"], 16)

            place(0, 0)
            with pool.Fori(0, B - 1) as b:
                place(b, 1)
                attended(b, 0)
                place(b + 1, 0)
                attended(b, 1)

            def expert_hi(e):
                pool.wait_ge(q[f"in_ew{e}"], 16)
                for c in range(0, C, 2):
                    pool.tensor_copy(ew[e][:, 0, c:c + 2], full(ew[e][:, 1, c:c + 2])).then_inc(q["m_early_hi"], 2)

            for e in range(EARLY):
                expert_hi(e)
            place(B - 1, 1)
            attended(B - 1, 0)

            pool.wait_ge(q["in_list"], 16)
            pool.wait_ge(q["f_t_full"], B * NH * T)

            def fetch(i, n, k):
                await_ge(pool, f"m_rows{k}", n * 16)
                pool.sem_inc(q["pool_went_on"], 1)
                pool.tensor_copy(idx[:, k:k + 1], lst[:, bass.ds(i, 1), 0].bitcast(U32)).then_inc(q["m_idx"], 1)
                pool.wait_ge(q["m_idx"], i + 1)
                await_ge(pool, "m_tr", i - 3)
                pool.sem_inc(q["pool_went_on"], 1)
                pool.indirect_dma_start(out=rows[k], out_offset=None, in_=h2_dram,
                                        in_offset=bass.IndirectOffsetOnAxis(ap=idx[:, k:k + 1], axis=0)).then_inc(q[f"m_rows{k}"], 16)

            def add(i, k):
                await_ge(pool, "m_added", 16 * (i - 3))
                pool.sem_inc(q["pool_went_on"], 1)
                pool.tensor_copy(idx[:, 4 + k:5 + k], lst[:, bass.ds(i, 1), 0].bitcast(U32)).then_inc(q["m_to"], 1)
                pool.wait_ge(q["m_to"], i + 1)
                pool.wait_ge(q["m_y"], i + 1)
                await_ge(pool, "m_added", 16 * i)
                pool.sem_inc(q["pool_went_on"], 1)
                pool.indirect_dma_start(out=out_rows, out_offset=bass.IndirectOffsetOnAxis(ap=idx[:, 4 + k:5 + k], axis=0),
                                        in_=ysb[k], in_offset=None, compute_op=ALU.add).then_inc(q["m_added"], 16)

            def blocks(n, part):
                for k in range(4):
                    i = 4 * n + k
                    if part != "last":
                        fetch(i + 4, n + 1, k)
                    add(i, k)

            for i in range(4):
                fetch(i, 0, i)
            attended(B - 1, 1)
            pool.wait_ge(q["f_att_out"], 16 * 2 * B)
            blocks(0, "first")
            with pool.Fori(1, NB // 4 - 1) as n:
                blocks(n, "middle")
            blocks(NB // 4 - 1, "last")

        @block.scalar
        def _(act):
            act.dma_start(est[0:E, :, :], ctx.rearrange("b e d -> e b d")).then_inc(q["in_ctx"], 16)
            act.dma_start(bqc[:], bq.rearrange("(c p) -> p c", p=P), allow_slow_non_contiguous=True).then_inc(q["in_bias"], 16)
            act.dma_start(bkc[:], bk.rearrange("(c p) -> p c", p=P), allow_slow_non_contiguous=True).then_inc(q["in_bias"], 16)
            act.dma_start(bv_all[:], bv.rearrange("(a n) -> a n", a=1).broadcast_to([P, D])).then_inc(q["in_bias"], 16)
            act.dma_start(bg_all[:], b_gate.rearrange("(a n) -> a n", a=1).broadcast_to([P, NE])).then_inc(q["in_bg"], 16)
            act.dma_start(gws[:], w_gate.rearrange("(c p) n -> p c n", p=P)).then_inc(q["in_bias"], 16)

            def hi(n, out, src, bias=0.0):
                act.wait_ge(q["set_full"], n + 1)
                act.activation(out, src, ACT.Identity, bias=bias).then_inc(q["set_hi"], 1)

            act.wait_ge(q["in_wk"], 16)
            act.copy(wkp[0], wst[1]).then_inc(q["w_hi"], 1)
            for m in range(C):
                hi(n_wqT + m, wqT[0][:, m, :], bank[m][:])
            for m in range(C):
                hi(n_wkT + m, wkT[0][:, m, :], bank[C + m][:])
            for b in range(B):
                hi(n_eT + b, eT[0][:, :, b * W:b * W + E], bank[b][:, 0:C * W].rearrange("p (c w) -> p c w", c=C)[:, :, 0:E])
            act.wait_ge(q["in_wv"], 16)
            act.copy(wvp[0], wst[2]).then_inc(q["w_hi"], 1)
            act.wait_ge(q["in_bias"], 64)
            act.copy(gw[:, :, 0], gws[:]).then_inc(q["w_hi"], 1)
            act.wait_ge(q["made_ones"], 3)
            for c in range(C):
                act.activation(bqrep[0][:, c, :], ones[:], ACT.Identity, scale=bqc[:, c:c + 1]).then_inc(q["w_hi"], 1)
            for m in range(C):
                for f in range(2):
                    n = n_KE + 2 * m + f
                    hi(n, KE[0][:, m, f * HB * W:(f + 1) * HB * W], bank[n % 8][:, 0:HB * W], bkc[:, m:m + 1])
            for m in range(C):
                hi(n_A + m, A[0][:, m, :], bank[(n_A + m) % 8][:])
            for k in range(2 * C):
                m, f = k // 2, k % 2
                act.wait_ge(q["set_staged"], 2 * k + 2)
                act.copy(G[:, m * B + f * HB:m * B + (f + 1) * HB, 0], gst).then_inc(q["set_hi"], 1)
            for b in range(B):
                act.wait_ge(q["set_staged"], 4 * C + b + 1)
                act.copy(vext[0][0:W, b, :], vst[0:W, :]).then_inc(q["set_hi"], 1)

            def normed(ln, i, u, src, out, mo, name):
                act.wait_ge(q[f"{ln}_rstd"], i + 1)
                act.activation(out, src, ACT.Identity, bias=mo[:, u % 2, 5:6], scale=mo[:, u % 2, 3:4]).then_inc(q[name], 1)

            def h_norm(i, u, bb):
                await_ge(act, "s_step", 4 * i - 5)
                normed("ln1", i, u, xin[:, u, :], h[:, u % 2, :], mo1, "h_ready")

            def h_hi(i, u, bb):
                await_ge(act, "v_full", i - 1)
                act.wait_ge(q["h_tr"], i + 1)
                act.copy(hT[u % 2][0].rearrange("p c n -> p (c n)"), bank[0][:]).then_inc(q["hT_hi"], 1)

            def h2_norm(i, u, bb):
                await_ge(act, "h2_tr", i - 1)
                await_ge(act, f"h2_out{u % 2}", bb * 32 + 16 * (u // 2))
                normed("ln2", i, u, x1[:, u, :], h2[:, u % 2, :], mo2, "h2_ready")

            def h2_hi(i, u, bb):
                await_ge(act, "g_full", i - 1)
                act.wait_ge(q["h2_tr"], i + 1)
                act.copy(h2T[u % 2][0].rearrange("p c n -> p (c n)"), bank[2][:]).then_inc(q["h2T_hi"], 1)

            def p_hi(i, u, bb):
                await_ge(act, "e_full", i)
                act.wait_ge(q["p_tr"], i + 1)
                act.copy(pT[0][0:W, :], bank[6][0:W, 0:P]).then_inc(q["pT_hi"], 1)

            def weigh(i, u, bb):
                act.wait_ge(q["s_max"], i + 1)
                act.activation(sc[:, u % 2, :], sc[:, u % 2, :], ACT.Exp, bias=col[:, u % 2, 1:2],
                               accum_out=col[:, u % 2, 2:3]).then_inc(q["s_exp"], 1)

            def steps(b, part):
                for t in range(T):
                    for d, work in ((-1, p_hi), (0, weigh), (1, h_hi), (2, h_norm), (-2, h2_hi), (-1, h2_norm)):
                        if now := tile(b, t, d, part):
                            work(*now)

            h_norm(0, 0, 0)
            h_norm(1, 1, 0)
            h_hi(0, 0, 0)
            batches(act, steps)

            act.wait_ge(q["in_wqkv"], 16)
            act.wait_ge(q["in_fb"], 32)
            act.wait_ge(q["g_full"], NT)
            act.mul(bqk[:, 0:C], bqk[:, 0:C], HD ** -0.5).then_inc(q["f_wscaled"], 1)
            act.mul(wqkv[0][:, :, 0:D], wraw[:, :, 0:D], HD ** -0.5).then_inc(q["f_whi"], 1)
            for i in (1, 2):
                act.copy(wqkv[0][:, :, i * D:(i + 1) * D], wraw[:, :, i * D:(i + 1) * D]).then_inc(q["f_whi"], 1)

            def split(b, item, n, hn, bank_in, opening=False):
                act.wait_ge(q["f_d_full"], n + 1)
                if item[0] == "H":
                    t = int(item[1])
                    act.copy(fT[0][:, :, t * P:(t + 1) * P], bank_in[:].rearrange("p (c n) -> p c n", c=C)).then_inc(q["f_d_hi"], 1)
                    return
                i, m = piece(item)
                h = 1 if item[0] == "R" else 0
                if item[1] == "0" and not opening:
                    for j in range(HG):
                        slot, fills, used = stack_use(b if h else b + 1, h, j)
                        if j == 3:
                            slot, fills = 3 + (1 - h), b + 1
                        act.wait_ge(q[f"f_stack{slot}"], fills * FILL)
                act.activation(qkp[i][m][0], bank_in[:], ACT.Identity,
                               bias=bqk[:, i * C + 2 * h + m:i * C + 2 * h + m + 1]).then_inc(q["f_d_hi"], 1)

            def exps(b, k, ts):
                for t in ts:
                    act.wait_ge(q["f_max"], (b * NH + k) * T + t + 1)
                    act.activation(bank[SB[t]][:], bank[SB[t]][:], ACT.Exp, bias=nmx[:, k, t:t + 1],
                                   accum_out=Z[:, t, k:k + 1]).then_inc(q["f_exp"], 1)

            def turned(b, k, c):
                if c == 0:
                    await_ge(act, "f_pv", 2 * (b * NG + k // HG) - 1)
                if c == 2:
                    await_ge(act, "f_pv", 2 * (b * NG + k // HG))
                act.wait_ge(q["f_t_full"], (b * NH + k) * T + c + 2)
                act.activation(PT[k % HG][:, c:c + 2, :], banks[0][:], ACT.Exp).then_inc(q["f_pt"], 1)

            def o_out(b, g):
                act.wait_ge(q["f_pv"], 2 * (b * NG + g) + 2)
                act.copy(Osb, bank[6][:]).then_inc(q["f_o_sb"], 1)

            def expert_hi(e, cs):
                act.wait_ge(q[f"in_ew{e}"], 16)
                c = slice(cs[0], cs[-1] + 1)
                act.copy(ew[e][:, 0, c], full(ew[e][:, 1, c])).then_inc(q["m_ehi"], len(cs))

            def batch(b, first, last):
                for k in range(NH):
                    if last and k == 6:
                        act.wait_ge(q["ew_moved"], 16)
                        act.wait_ge(q["f_d_full"], number(b, "R3")[0] + 1)
                        for e in range(EARLY):
                            act.dma_start(full(ew[e][:, 1]), we_dram[e].rearrange("(c p) n -> p c n", p=P)).then_inc(q[f"in_ew{e}"], 16)
                    for what, of, head in plan(b, k, "act", first, last):
                        if what[0] == "E":
                            exps(of, head, (int(what[1]),))
                        elif what[0] == "t":
                            turned(of, head, int(what[1]))
                        elif what == "PV":
                            o_out(of, head)
                        else:
                            split(of, what, *number(of, what), bank[DB[0]])

            for item in BEFORE:
                if item in HIS:
                    n, hn = early(item)
                    split(0, item, n, hn, bank[DB[n % len(DB)]], True)
                if item == "V0":
                    for s in range(NSLOT):
                        act.copy(stk[s][1][M0:M1], ones[M0:M1, 0:1].unsqueeze(2).broadcast_to([2 * T, 2, S])).then_inc(q["f_ones"], 1)
                if item == "H3":
                    act.wait_ge(q["route"], 3)
                    act.activation(temp[2], temp[1], ACT.Exp).then_inc(q["r_gate"], 1)
            batch(0, True, False)
            with act.Fori(1, B - 1) as b:
                batch(b, False, False)
            batch(B - 1, False, True)
            turned(B - 1, NH - 2, 2)
            exps(B - 1, NH - 1, (T - 1,))
            for c in (0, 2):
                turned(B - 1, NH - 1, c)
            o_out(B - 1, NG - 1)
            def rows_hi(i, k):
                act.wait_ge(q["m_tr"], i + 1)
                act.copy(gT[k][:, 0].rearrange("p c n -> p (c n)"), bank[k][:]).then_inc(q["m_hi"], 1)

            def weighted(i, k, n):
                act.wait_ge(q["m_sum"], i + 1)
                act.activation(ysb[k % 4], ysb[k % 4], ACT.Copy, scale=lst[:, bass.ds(i, 1), 1]).then_inc(q["m_y"], 1)

            def blocks(n, part):
                for k in range(4):
                    i = 4 * n + k
                    if not (part == "first" and k == 0) and not (part == "last" and k == 3):
                        rows_hi(i + 1, (k + 1) % 2)
                    if part != "first" or k:
                        weighted(i - 1, k - 1, n)

            for i in range(2):
                rows_hi(i, i)
            for e in range(EARLY, NE):
                expert_hi(e, range(C))
            blocks(0, "first")
            with act.Fori(1, NB // 4 - 1) as n:
                blocks(n, "middle")
            blocks(NB // 4 - 1, "last")
            weighted(NB - 1, 3, NB // 4 - 1)

        @block.tensor
        def _(pe):
            pe.wait_ge(q["made_ident"], 2)

            def slot(n):
                if n >= 8:
                    pe.wait_ge(q["set_free"], n - 7)
                return bank[n % 8]

            for n0, src, name in ((n_wqT, 0, "in_wq"), (n_wkT, 1, "in_wk")):
                pe.wait_ge(q[name], 16)
                for m in range(C):
                    o = slot(n0 + m)
                    for c in range(C):
                        last = pe.transpose(o[:, c * P:(c + 1) * P], wst[src][:, c, m * P:(m + 1) * P], ident[:])
                    last.then_inc(q["set_full"], 1)
            pe.wait_ge(q["in_ctx"], 16)
            for b in range(B):
                o = slot(n_eT + b)
                for c in range(C):
                    last = pe.transpose(o[:, c * W:c * W + E], est[0:E, b, c * P:(c + 1) * P], ident[0:E, 0:E])
                last.then_inc(q["set_full"], 1)
            pe.wait_ge(q["w_ready"], 1)
            pe.wait_ge(q["made_ones"], 3)
            pe.wait_ge(q["set_free"], n_KE)
            half = [slice(f * HB * W, (f + 1) * HB * W) for f in range(2)]
            sl = slice(None)
            for m in range(C):
                for f in range(2):
                    o = slot(n_KE + 2 * m + f)
                    for c in range(C):
                        last = prod3(pe, o[:, 0:HB * W], at(wkp, sl, c, slice(m * P, (m + 1) * P)), at(eT, sl, c, half[f]),
                                     c == 0, c == C - 1)
                    last.then_inc(q["set_full"], 1)
            for m in range(C):
                o = slot(n_A + m)
                for c in range(C):
                    last = prod3(pe, o[:], at(wqT, sl, c, slice(m * P, (m + 1) * P)), at(wkT, sl, c), c == 0, c == C - 1)
                last.then_inc(q["set_full"], 1)
            pe.wait_ge(q["w_ready"], 3 + C)
            o = slot(n_cq)
            for m in range(C):
                for c in range(C):
                    last = prod3(pe, o[:, 2 * m:2 * m + 2], at(wkT, sl, c, slice(m * P, (m + 1) * P)),
                                 at(bqrep, sl, c, slice(0, 2)), c == 0, c == C - 1)
            last.then_inc(q["set_full"], 1)
            pe.wait_ge(q["set_free"], n_A)
            for m in range(C):
                for f in range(2):
                    o = slot(n_G + 2 * m + f)
                    for c in range(C):
                        last = prod3(pe, o[:, 0:HB * W], at(wqT, sl, c, slice(m * P, (m + 1) * P)), at(KE, sl, c, half[f]),
                                     c == 0, c == C - 1)
                    last.then_inc(q["set_full"], 1)
            for f in range(2):
                o = slot(n_sb + f)
                for c in range(C):
                    last = prod3(pe, o[:, 0:HB * W], at(bqrep, sl, c), at(KE, sl, c, half[f]), c == 0, c == C - 1)
                last.then_inc(q["set_full"], 1)
            for b in range(B):
                o = slot(n_ve + b)
                for c in range(C):
                    last = prod3(pe, o[0:W, :], at(eT, sl, c, slice(b * W, (b + 1) * W)), at(wvp, sl, c), c == 0, c == C - 1)
                last.then_inc(q["set_full"], 1)

            def h_turn(i, u, bb):
                await_ge(pe, "hT_ready", i)
                pe.wait_ge(q["h_ready"], i + 1)
                for c in range(C):
                    last = pe.transpose(bank[0][:, c * P:(c + 1) * P], h[:, u % 2, c * P:(c + 1) * P], ident[:])
                last.then_inc(q["h_tr"], 1)

            def score(i, u, bb):
                await_ge(pe, "s_step", 4 * i)
                pe.wait_ge(q["hT_ready"], i + 1)
                for c in range(C):
                    prod3(pe, bank[1][:], at(hT[u % 2], sl, c), at(A, sl, c), c == 0, c == C - 1)
                for c in range(C):
                    place = G.rearrange("p b k w -> p (b k w)")
                    pe.matmul(bank[5][:, 0:2 * W], hT[u % 2][0][:, c], place[:, bass.ds(bb * (2 * W) + c * B * 2 * W, 2 * W)],
                              start=c == 0, stop=False)
                    last = pe.matmul(bank[5][:, 0:W], hT[u % 2][1][:, c], place[:, bass.ds(bb * (2 * W) + c * B * 2 * W, W)],
                                     start=False, stop=c == C - 1)
                last.then_inc(q["s_full"], 1)

            def value(i, u, bb):
                await_ge(pe, "x1_part", i)
                for c in range(C):
                    last = prod3(pe, bank[3][:], at(hT[u % 2], sl, c), at(wvp, sl, c), c == 0, c == C - 1)
                last.then_inc(q["v_full"], 1)

            def p_turn(i, u, bb):
                await_ge(pe, "pT_ready", i)
                pe.wait_ge(q["p_ready"], i + 1)
                pe.transpose(bank[6][0:W, 0:P], sc[:, u % 2, :], ident[:]).then_inc(q["p_tr"], 1)

            def extend(i, u, bb):
                await_ge(pe, "x1_ready", i)
                pe.wait_ge(q["pT_ready"], i + 1)
                prod3(pe, bank[7][:], (pT[0][0:W, :], pT[1][0:W, :]),
                      (vext[0][0:W].rearrange("p b d -> p (b d)")[:, bass.ds(bb * D, D)],
                       vext[1][0:W].rearrange("p b d -> p (b d)")[:, bass.ds(bb * D, D)]),
                      True, True).then_inc(q["e_full"], 1)

            def h2_turn(i, u, bb):
                await_ge(pe, "h2T_ready", i)
                pe.wait_ge(q["h2_ready"], i + 1)
                for c in range(C):
                    last = pe.transpose(bank[2][:, c * P:(c + 1) * P], h2[:, u % 2, c * P:(c + 1) * P], ident[:])
                last.then_inc(q["h2_tr"], 1)

            def gate(i, u, bb):
                await_ge(pe, "g_copied", i)
                pe.wait_ge(q["h2T_ready"], i + 1)
                for c in range(C):
                    pe.matmul(bank[4][:, 0:2 * NE], h2T[u % 2][0][:, c], gw[:, c].rearrange("p k n -> p (k n)"), start=c == 0, stop=False)
                    last = pe.matmul(bank[4][:, 0:NE], h2T[u % 2][1][:, c], gw[:, c, 0], start=False, stop=c == C - 1)
                last.then_inc(q["g_full"], 1)

            def steps(b, part):
                for t in range(T):
                    for d, work in ((0, score), (-1, extend), (1, h_turn), (-2, h2_turn), (-3, gate), (0, value), (0, p_turn)):
                        if now := tile(b, t, d, part):
                            work(*now)

            pe.wait_ge(q["set_free"], n_end)
            h_turn(0, 0, 0)
            batches(pe, steps)

            def prefix():
                pe.wait_ge(q["route"], N_PICKED)
                pe.matmul(bank[6][:, 0:NT * NE], tri[:], temp[9].rearrange("p t e -> p (t e)"), start=True, stop=True)
                pe.matmul(bank[6][:, NT * NE:2 * NT * NE], ones[:], temp[9].rearrange("p t e -> p (t e)"), start=True, stop=True).then_inc(q["r_pref"], 1)

            def dense(b, item, n, o, half=""):
                kind, t = item[0], int(item[1])
                cs = {"": range(C), "a": range(C // 2), "b": range(C // 2, C)}[half]
                if kind == "H":
                    pe.wait_ge(q["f_raw"], b * 16 + 16)
                    for c in range(C):
                        last = pe.transpose(o[:, c * P:(c + 1) * P], h2f[:, t, c * P:(c + 1) * P], ident[:])
                elif kind == "V":
                    for c in cs:
                        last = prod3(pe, o[:], at(fT, sl, c, slice(t * P, (t + 1) * P)),
                                     at(wqkv, sl, c, slice(2 * D, Q3)), c == 0, c == C - 1)
                else:
                    i, m = piece(item)
                    col = i * D + (2 * (kind == "R") + m) * P
                    for c in cs:
                        last = prod3(pe, o[:], at(wqkv, sl, c, slice(col, col + P)), at(fT, sl, c), c == 0, c == C - 1)
                if half != "a":
                    last.then_inc(q["f_d_full"], 1)

            def scores(b, k, t):
                h, j, m = k // 8, k % 8 // 2, k % 2
                slot, fills, used = stack_use(b, h, j)
                if m == 0 and t == 0:
                    pe.wait_ge(q[f"f_stack{slot}"], (fills + 1) * FILL)
                await_ge(pe, "f_exp", (b * NH + k) * T + t - T + 1)
                pe.matmul(bank[SB[t]][:], stk[slot][0][0:M0, m, t * P:(t + 1) * P], stk[slot][1][0:M0, m, :],
                          start=True, stop=True).then_inc(q["f_s_full"], 1)

            def max_turn(b, k):
                pe.wait_ge(q["f_nparts"], b * NH + k + 1)
                await_ge(pe, "f_o_sb", b * NG + (k - 1) // HG)
                await_ge(pe, "f_o_fin", b * NG + (k - 3) // HG)
                pe.matmul(bank[6][M0:M1, 0:P], full(nparts[:].rearrange("p a t -> p (a t)")), ident[:], start=True, stop=True).then_inc(q["f_n_tr"], 1)

            def turn(b, k, cs):
                h, j, m = k // 8, k % 8 // 2, k % 2
                slot = stack_use(b, h, j)[0]
                if cs[0] == 0:
                    pe.wait_ge(q["f_n_in"], b * NH + k + 1)
                await_ge(pe, "f_pt", ((b * NH + k) * T + cs[0]) // 2)
                for c in cs:
                    pe.matmul(bank[c % 2][:], stk[slot][1][0:M1, m, c * P:(c + 1) * P], stk[slot][0][0:M1, m, :],
                              start=True, stop=True).then_inc(q["f_t_full"], 1)

            def pv(b, g, half):
                if half == "a":
                    pe.wait_ge(q["f_pt"], (b * NH + HG * (g + 1)) * T // 2)
                    pe.wait_ge(q["f_v_in"], b * 16 + 16)
                    pe.wait_ge(q["r_zero"], 1)
                    await_ge(pe, "f_o_fin", b * NG + g)
                    heads = b * NH + HG * g + HG + 1
                    pe.wait_ge(q["f_n_in"], min(heads, B * NH) if isinstance(heads, int) else heads)
                for c in (0, 1) if half == "a" else (2, 3):
                    for i in range(HG):
                        jj, m = i // 2, i % 2
                        at_o, head = 2 * m + jj, 8 * (g // 2) + HG * m + 2 * (g % 2) + jj
                        last = pe.matmul(bank[6][at_o * HD:(at_o + 1) * HD, :], V[:, c, head * HD:(head + 1) * HD], PT[i][:, c, :],
                                         start=(c == 0), stop=(c == T - 1))
                last.then_inc(q["f_pv"], 1)

            def o_turn(b, g):
                pe.wait_ge(q["f_o_sb"], b * NG + g + 1)
                heads = b * NH + HG * g + 7
                pe.wait_ge(q["f_n_in"], min(heads, B * NH) if isinstance(heads, int) else heads)
                for t in range(T):
                    last = pe.transpose(bank[6][:, t * P:(t + 1) * P], Osb[:, t * P:(t + 1) * P], ident[:])
                last.then_inc(q["f_ot"], 1)

            def batch(b, first, last):
                for k in range(NH):
                    for what, of, head in plan(b, k, "pe", first, last):
                        if what[0] == "S":
                            scores(of, head, int(what[1]))
                        elif what[0] == "T":
                            turn(of, head, (int(what[1]), int(what[1]) + 1))
                        elif what == "n":
                            max_turn(of, head)
                        elif what[0:2] == "PV":
                            pv(of, head, what[2])
                        elif what == "OT":
                            o_turn(of, head)
                        else:
                            n = number(of, what[0:2])[0]
                            if what[2:] != "b":
                                pe.wait_ge(q["f_d_free"], n)
                            dense(of if what[0] == "R" else of + 1, what[0:2], n, bank[DB[0]], what[2:])

            pe.wait_ge(q["g_copied"], NT)
            for item in BEFORE:
                n = early(item)[0]
                if item == "N0":
                    pe.wait_ge(q["f_d_free"], n)
                if item in ("N0", "N2", "V0"):
                    pe.wait_ge(q["f_wready"], ("N0", "N2", "V0").index(item) + 1)
                if item == "V1":
                    prefix()
                await_ge(pe, "f_d_free", n - len(DB) + 1)
                dense(0, item, n, bank[DB[n % len(DB)]])
            pe.wait_ge(q["f_d_free"], len(BEFORE))
            pe.wait_ge(q["f_ones"], NSLOT)
            pe.wait_ge(q["made_own"], 3)
            batch(0, True, False)
            with pe.Fori(1, B - 1) as b:
                batch(b, False, False)
            batch(B - 1, False, True)
            turn(B - 1, NH - 2, (2, 3))
            max_turn(B - 1, NH - 1)
            turn(B - 1, NH - 1, (0, 1))
            turn(B - 1, NH - 1, (2, 3))
            pv(B - 1, NG - 1, "a")
            pv(B - 1, NG - 1, "b")
            o_turn(B - 1, NG - 1)

            def rows_turn(i, n, k):
                pe.wait_ge(q[f"m_rows{k % 4}"], n * 16 + 16)
                for c in range(C):
                    last = pe.transpose(bank[k % 2][:, c * P:(c + 1) * P], rows[k % 4][:, c * P:(c + 1) * P], ident[:])
                last.then_inc(q["m_tr"], 1)

            def blocks(n, part):
                for k in range(4):
                    i = 4 * n + k
                    if part != "last" or k < 3:
                        await_ge(pe, "m_hT", i)
                        rows_turn(i + 1, n + (k + 1) // 4, k + 1)
                    pe.wait_ge(q["m_hT"], i + 1)
                    await_ge(pe, "m_sum", i - 1)
                    e = pe.value_load(bexp[0:1, bass.ds(i, 1)], min_val=0, max_val=NE - 1)
                    if part == "first":
                        pe.wait_ge(q["m_elo"], e * C + C if k < 2 else NE * C)
                    for c in range(C):
                        last = prod3(pe, bank[2 + k % 2][:], (gT[k % 2][:, 0, c], gT[k % 2][:, 1, c]),
                                     (parts[:, bass.ds(e * EW + c * D, D)], parts[:, bass.ds(e * EW + (C + c) * D, D)]), c == 0, c == C - 1)
                    last.then_inc(q["m_full"], 1)

            rows_turn(0, 0, 0)
            blocks(0, "first")
            with pe.Fori(1, NB // 4 - 1) as n:
                blocks(n, "middle")
            blocks(NB // 4 - 1, "last")

        @block.vector
        def _(dve):
            def lo(n, out, src, high, bias=None):
                dve.wait_ge(q["set_hi"], n + 1)
                if bias is None:
                    ins = dve.tensor_tensor(out, src, full(high), ALU.subtract)
                else:
                    ins = dve.scalar_tensor_tensor(out=out, in0=src, scalar=bias, in1=full(high), op0=ALU.add, op1=ALU.subtract)
                return ins

            dve.wait_ge(q["w_hi"], 1)
            dve.tensor_tensor(wkp[1], wst[1], full(wkp[0]), ALU.subtract).then_inc(q["w_ready"], 1)
            for m in range(C):
                lo(m, wqT[1][:, m, :], bank[m][:], wqT[0][:, m, :]).then_inc(q["set_free"], 1)
            for m in range(C):
                lo(n_wkT + m, wkT[1][:, m, :], bank[C + m][:], wkT[0][:, m, :]).then_inc(q["set_free"], 1)
            for b in range(B):
                cols = slice(b * W, b * W + E)
                lo(n_eT + b, eT[1][:, :, cols], bank[b][:, 0:C * W].rearrange("p (c w) -> p c w", c=C)[:, :, 0:E],
                   eT[0][:, :, cols]).then_inc(q["set_free"], 1)
            dve.wait_ge(q["w_hi"], 2)
            dve.tensor_tensor(wvp[1], wst[2], full(wvp[0]), ALU.subtract).then_inc(q["w_ready"], 1)
            dve.wait_ge(q["w_hi"], 3)
            dve.tensor_tensor(gw[:, :, 1], gws[:], full(gw[:, :, 0]), ALU.subtract).then_inc(q["w_ready"], 1)
            for c in range(C):
                dve.wait_ge(q["w_hi"], 4 + c)
                dve.scalar_tensor_tensor(out=bqrep[1][:, c, :], in0=ones[:], scalar=bqc[:, c:c + 1], in1=full(bqrep[0][:, c, :]),
                                         op0=ALU.mult, op1=ALU.subtract).then_inc(q["w_ready"], 1)
            for m in range(C):
                for f in range(2):
                    n = n_KE + 2 * m + f
                    cols = slice(f * HB * W, (f + 1) * HB * W)
                    lo(n, KE[1][:, m, cols], bank[n % 8][:, 0:HB * W], KE[0][:, m, cols], bkc[:, m:m + 1]).then_inc(q["set_free"], 1)
            for m in range(C):
                n = n_A + m
                lo(n, A[1][:, m, :], bank[n % 8][:], A[0][:, m, :]).then_inc(q["set_free"], 1)
            dve.wait_ge(q["set_full"], n_cq + 1)
            dve.tensor_copy(cq[:], bank[n_cq % 8][:, 0:2 * C]).then_inc(q["set_free"], 1)
            dve.wait_ge(q["set_free"], n_cq + 1)
            flat = gst.rearrange("p b w -> p (b w)")
            for k in range(2 * C):
                n, m, f = n_G + k, k // 2, k % 2
                cols = slice(f * HB * W, (f + 1) * HB * W)
                dve.wait_ge(q["set_full"], n + 1)
                dve.wait_ge(q["set_free"], n)
                dve.tensor_copy(flat, bank[n % 8][:, 0:HB * W]).then_inc(q["set_staged"], 1)
                dve.wait_ge(q["set_staged"], 2 * k + 1)
                dve.tensor_scalar(gst[:, :, E:W], gst[:, :, E:W], cq[:, 2 * m:2 * m + 1], None, ALU.add).then_inc(q["set_staged"], 1)
                lo(n - 1, G[:, m * B + f * HB:m * B + (f + 1) * HB, 1], gst, G[:, m * B + f * HB:m * B + (f + 1) * HB, 0]).then_inc(q["set_free"], 1)
            for f in range(2):
                n = n_sb + f
                dve.wait_ge(q["set_full"], n + 1)
                dve.tensor_copy(sbias[:, f * HB * W:(f + 1) * HB * W], bank[n % 8][:, 0:HB * W]).then_inc(q["set_free"], 1)
            for b in range(B):
                n = n_ve + b
                dve.wait_ge(q["set_full"], n + 1)
                dve.wait_ge(q["set_free"], n)
                dve.tensor_tensor(vst[0:W, :], bank[n % 8][0:W, :], bv_all[0:W, :], ALU.add).then_inc(q["set_staged"], 1)
                lo(n - 3, vext[1][0:W, b, :], vst[0:W, :], vext[0][0:W, b, :]).then_inc(q["set_free"], 1)

            def norm(ln, i, u, src, st, mo, f, normed):
                await_ge(dve, normed, i - 1)
                dve.bn_stats(st[:, u % 2, :], src).then_inc(q[f"{ln}_stats"], 1)
                dve.wait_ge(q[f"{ln}_stats"], i + 1)
                dve.tensor_copy(fence[:, f:f + 1], st[:, u % 2, 0:1])
                dve.bn_aggr(mo[:, u % 2, 0:2], st[:, u % 2, :]).then_inc(q[f"{ln}_var"], 1)

            def h_stats(i, u, bb):
                dve.wait_ge(q[f"x_in{u}"], bb * 16 + 16)
                norm("ln1", i, u, xin[:, u, :], st1, mo1, 0, "h_ready")

            def h_lo(i, u, bb):
                dve.wait_ge(q["hT_hi"], i + 1)
                dve.tensor_tensor(hT[u % 2][1].rearrange("p c n -> p (c n)"), bank[0][:],
                                  full(hT[u % 2][0].rearrange("p c n -> p (c n)")), ALU.subtract).then_inc(q["hT_ready"], 1)

            def p_lo(i, u, bb):
                dve.wait_ge(q["pT_hi"], i + 1)
                dve.tensor_tensor(pT[1][0:W, :], bank[6][0:W, 0:P], full(pT[0][0:W, :]), ALU.subtract).then_inc(q["pT_ready"], 1)

            def x1_begun(i, u, bb):
                dve.wait_ge(q["v_full"], i + 1)
                dve.wait_ge(q["p_ready"], i + 1)
                await_ge(dve, f"x1_out{u}", bb * 16)
                dve.scalar_tensor_tensor(out=x1[:, u, :], in0=bank[3][:], scalar=sc[:, u % 2, E:W],
                                         in1=xin[:, u, :], op0=ALU.mult, op1=ALU.add).then_inc(q["x1_part"], 1)

            def largest(i, u, bb):
                k = u % 2
                dve.wait_ge(q["s_full"], i + 1)
                dve.tensor_reduce(sc[:, k, :], bank[5][:, 0:2 * W].rearrange("p (k w) -> p w k", k=2), AX.X, ALU.add).then_inc(q["s_step"], 1)
                dve.wait_ge(q["s_step"], 4 * i + 1)
                dve.tensor_tensor(sc[:, k, :], sc[:, k, :], sbias[:, bass.ds(bb * W, W)], ALU.add).then_inc(q["s_step"], 1)
                dve.tensor_tensor_reduce(scr, bank[1][:], h[:, k, :], 1.0, 0.0, ALU.mult, ALU.add,
                                         col[:, k, 0:1]).then_inc(q["s_step"], 1)
                dve.wait_ge(q["s_step"], 4 * i + 3)
                dve.tensor_tensor(sc[:, k, E:W], sc[:, k, E:W], col[:, k, 0:1], ALU.add).then_inc(q["s_step"], 1)
                dve.wait_ge(q["s_step"], 4 * i + 4)
                dve.tensor_reduce(col[:, k, 1:2], sc[:, k, :], AX.X, ALU.max, negate=True).then_inc(q["s_max"], 1)

            def x1_whole(i, u, bb):
                dve.wait_ge(q["e_full"], i + 1)
                dve.wait_ge(q["x1_part"], i + 1)
                dve.tensor_tensor(x1[:, u, :], bank[7][:], x1[:, u, :], ALU.add).then_inc(q["x1_ready"], 1)

            def share(i, u, bb):
                k = u % 2
                dve.wait_ge(q["s_exp"], i + 1)
                dve.reciprocal(col[:, k, 3:4], col[:, k, 2:3]).then_inc(q["s_den"], 1)
                dve.wait_ge(q["s_den"], i + 1)
                dve.tensor_scalar(sc[:, k, :], sc[:, k, :], col[:, k, 3:4], None, ALU.mult).then_inc(q["p_ready"], 1)

            def h2_stats(i, u, bb):
                dve.wait_ge(q["x1_ready"], i + 1)
                norm("ln2", i, u, x1[:, u, :], st2, mo2, 1, "h2_ready")

            def h2_lo(i, u, bb):
                dve.wait_ge(q["h2T_hi"], i + 1)
                dve.tensor_tensor(h2T[u % 2][1].rearrange("p c n -> p (c n)"), bank[2][:],
                                  full(h2T[u % 2][0].rearrange("p c n -> p (c n)")), ALU.subtract).then_inc(q["h2T_ready"], 1)

            def g_copy(i, u, bb):
                dve.wait_ge(q["g_full"], i + 1)
                dve.tensor_reduce(glog[:, bass.ds(i, 1), :], bank[4][:, 0:2 * NE].rearrange("p (a k n) -> p a n k", a=1, k=2), AX.X, ALU.add).then_inc(q["g_copied"], 1)

            def steps(b, part):
                for t in range(T):
                    for d, work in ((-1, p_lo), (-1, x1_begun), (2, h_stats), (0, largest), (-1, x1_whole), (0, share),
                                    (-1, h2_stats), (1, h_lo), (-2, h2_lo), (-3, g_copy)):
                        if now := tile(b, t, d, part):
                            work(*now)

            h_stats(0, 0, 0)
            h_stats(1, 1, 0)
            h_lo(0, 0, 0)
            batches(dve, steps)

            dve.wait_ge(q["f_whi"], 1)
            dve.scalar_tensor_tensor(out=wqkv[1][:, :, 0:D], in0=wraw[:, :, 0:D], scalar=HD ** -0.5, in1=full(wqkv[0][:, :, 0:D]),
                                     op0=ALU.mult, op1=ALU.subtract).then_inc(q["f_wready"], 1)
            for i in (1, 2):
                cols = slice(i * D, (i + 1) * D)
                dve.wait_ge(q["f_whi"], i + 1)
                dve.tensor_tensor(wqkv[1][:, :, cols], wraw[:, :, cols], full(wqkv[0][:, :, cols]), ALU.subtract).then_inc(q["f_wready"], 1)

            route = [0]

            def then(ins):
                ins.then_inc(q["route"], 1)
                route[0] += 1
                dve.wait_ge(q["route"], route[0])

            t_lg, t_ex, t_gate, t_first, t_second, t_eq, t_place, t_in, t_sel = (temp[i] for i in (1, 2, 3, 4, 5, 6, 7, 8, 9))
            row = temp[0].rearrange("p t e -> p (t e)")
            mx, den, tie, desc = row[:, 0:NT], row[:, NT:2 * NT], row[:, 2 * NT:3 * NT], row[:, 3 * NT:3 * NT + NE]
            gates = [row[:, 4 * NT:5 * NT], row[:, 5 * NT:6 * NT]]

            def wide(v):
                return v.unsqueeze(2).broadcast_to([P, NT, NE])

            def every(v):
                return v.unsqueeze(1).broadcast_to([P, NT, NE])

            def logits():
                dve.wait_ge(q["g_copied"], NT)
                dve.wait_ge(q["in_bg"], 16)
                dve.wait_ge(q["made_count"], 6)
                then(dve.tensor_tensor(t_lg, glog[:], every(bg_all[:]), ALU.add))
                then(dve.tensor_reduce(mx, t_lg, AX.X, ALU.max))
                then(dve.tensor_tensor(t_lg, t_lg, wide(mx), ALU.subtract))
                then(dve.tensor_scalar(desc, kk[:, 0:NE], -1.0, float(NE), ALU.mult, ALU.add))

            def gate_values():
                dve.wait_ge(q["r_gate"], 1)
                then(dve.tensor_reduce(den, t_ex, AX.X, ALU.add))
                then(dve.reciprocal(den, den))
                then(dve.tensor_tensor(t_gate, t_ex, wide(den), ALU.mult))

            def pick(gate, out, choice):
                then(dve.tensor_reduce(out, gate, AX.X, ALU.max))
                then(dve.tensor_tensor(t_eq, gate, wide(out), ALU.is_equal))
                then(dve.tensor_tensor(t_eq, t_eq, every(desc), ALU.mult))
                then(dve.tensor_reduce(tie, t_eq, AX.X, ALU.max))
                then(dve.tensor_tensor(choice, t_eq, wide(tie), ALU.is_equal))

            def first_choice():
                gate_values()
                pick(t_gate, gates[0], t_first)

            def second_choice():
                then(dve.scalar_tensor_tensor(out=t_gate, in0=t_first, scalar=-2.0, in1=t_gate, op0=ALU.mult, op1=ALU.add))
                pick(t_gate, gates[1], t_second)
                then(dve.tensor_tensor(t_sel, t_first, t_second, ALU.add))
                assert route[0] == N_PICKED

            tot = bank[6][:, NT * NE:2 * NT * NE].rearrange("p (t e) -> p t e", e=NE)
            in_tile = bank[6][:, 0:NT * NE].rearrange("p (t e) -> p t e", e=NE)
            k128 = row[:, 6 * NT:7 * NT]
            small = [row[:, 7 * NT + NE * i:7 * NT + NE * (i + 1)] for i in range(4)]
            count, limit = row[:, 3 * NT + NE:3 * NT + 2 * NE], row[:, 3 * NT + 2 * NE:3 * NT + 3 * NE]
            run, blk, start, base = (t_in, t_lg)[(NT - 1).bit_length() % 2], small[0], small[1 + NE.bit_length() % 2], small[3]

            def running(now, other, n):
                d = 1
                while d < n:
                    then(dve.tensor_copy(other[:, 0:d], now[:, 0:d]))
                    then(dve.tensor_tensor(other[:, d:n], now[:, d:n], now[:, 0:n - d], ALU.add))
                    now, other, d = other, now, 2 * d
                return now, other

            def over_tiles():
                dve.wait_ge(q["r_pref"], 1)
                then(dve.tensor_copy(t_in, tot))
                assert running(t_in, t_lg, NT)[0] is run

            def first_blocks():
                then(dve.tensor_scalar(k128, kk[:, 0:NT], float(P), None, ALU.mult))
                cmp = t_eq.rearrange("p t e -> p (t e)").rearrange("p (e t) -> p e t", t=NT)
                then(dve.tensor_tensor(cmp, run[:, NT - 1, :].unsqueeze(2).broadcast_to([P, NE, NT]),
                                       k128.unsqueeze(1).broadcast_to([P, NE, NT]), ALU.is_gt))
                then(dve.tensor_reduce(blk, cmp, AX.X, ALU.add))
                then(dve.tensor_copy(small[1], blk))
                ends, free = running(small[1], small[2], NE)
                assert free is start
                then(dve.tensor_tensor(start, ends, blk, ALU.subtract))
                then(dve.tensor_scalar(base, start, float(P), None, ALU.mult))

            def places():
                then(dve.tensor_tensor(t_place, run, tot, ALU.subtract))
                then(dve.tensor_tensor(t_place, t_place, in_tile, ALU.add))
                then(dve.tensor_tensor(t_place, t_place, every(base), ALU.add))
                for a, choice in enumerate((t_first, t_second)):
                    then(dve.tensor_tensor(t_eq, choice, t_place, ALU.mult))
                    then(dve.tensor_reduce(mx, t_eq, AX.X, ALU.add))
                    then(dve.tensor_copy(rec[:, a, :, 0].bitcast(U32), mx))
                    then(dve.tensor_copy(rec[:, a, :, 2], gates[a]))

            def block_experts():
                big = area(plain, 3 * C * D + T * D + NT * NE, NB, NE)
                then(dve.tensor_tensor(big, kk[:].unsqueeze(2).broadcast_to([P, NB, NE]), start.unsqueeze(1).broadcast_to([P, NB, NE]), ALU.is_ge))
                then(dve.tensor_reduce(row[:, 0:NB], big, AX.X, ALU.add))
                then(dve.tensor_scalar(bexp, row[:, 0:NB], -1.0, None, ALU.add))
                then(dve.memset(lst, 0.0))
                then(dve.tensor_scalar(lst[:, :, 0].bitcast(U32), iot[:].bitcast(U32), 1023, None, ALU.bitwise_and))
                then(dve.memset(zrec, 0.0))
                dve.sem_inc(q["r_zero"], 1)

            def fillers():
                t_num, t_past = t_eq, t_ex
                then(dve.scalar_tensor_tensor(out=count, in0=base, scalar=2.0, in1=run[:, NT - 1, :], op0=ALU.mult, op1=ALU.add))
                then(dve.scalar_tensor_tensor(out=limit, in0=blk, scalar=float(P), in1=base, op0=ALU.mult, op1=ALU.add))
                then(dve.tensor_tensor(t_num, wide(tok[:]), t_place, ALU.subtract))
                then(dve.tensor_tensor(t_num, t_num, every(count), ALU.add))
                then(dve.tensor_tensor(t_past, t_num, every(limit), ALU.is_ge))
                then(dve.tensor_tensor(t_past, t_past, t_sel, ALU.max))
                then(dve.scalar_tensor_tensor(out=t_num, in0=t_past, scalar=65536.0, in1=t_num, op0=ALU.mult, op1=ALU.add))
                then(dve.tensor_copy(glog[:].bitcast(U32), t_num))

            ROUTING = {"H3": (logits,), "N0": (first_choice,), "N1": (second_choice,), "V0": (over_tiles,), "V1": (first_blocks,),
                       "V2": (places,), "V3": (fillers, block_experts)}

            def split(b, item, n, hn, bank_in, opening=False):
                if item[0] == "V":
                    t = int(item[1])
                    if t == 0 and not opening:
                        dve.wait_ge(q["f_v_in"], b * 16 + 16)
                    dve.wait_ge(q["f_d_full"], n + 1)
                    dve.tensor_tensor(Vst[:, t, :], bank_in[:], bvf[:], ALU.add).then_inc(q["f_d_free"], 1)
                    return
                dve.wait_ge(q["f_d_hi"], hn + 1)
                if item[0] == "H":
                    t = int(item[1])
                    cols = slice(t * P, (t + 1) * P)
                    dve.tensor_tensor(fT[1][:, :, cols], bank_in[:].rearrange("p (c n) -> p c n", c=C),
                                      full(fT[0][:, :, cols]), ALU.subtract).then_inc(q["f_d_free"], 1)
                else:
                    i, m = piece(item)
                    h = 1 if item[0] == "R" else 0
                    dve.scalar_tensor_tensor(out=qkp[i][m][1], in0=bank_in[:], scalar=bqk[:, i * C + 2 * h + m:i * C + 2 * h + m + 1],
                                             in1=full(qkp[i][m][0]), op0=ALU.add, op1=ALU.subtract).then_inc(q["f_d_free"], 1)

            def maxes(b, k, ts):
                for t in ts:
                    dve.wait_ge(q["f_s_full"], (b * NH + k) * T + t + 1)
                    dve.tensor_reduce(nmx[:, k, t:t + 1], bank[SB[t]][:], AX.X, ALU.max, negate=True).then_inc(q["f_max"], 1)

            def max_parts(b, k):
                dve.wait_ge(q["f_max"], (b * NH + k) * T + T)
                dve.tensor_copy(nparts[:, 0], nmx[:, k]).then_inc(q["f_nhi"], 1)
                dve.wait_ge(q["f_nhi"], b * NH + k + 1)
                dve.tensor_tensor(nparts[:, 1], nmx[:, k], full(nparts[:, 0]), ALU.subtract).then_inc(q["f_nparts"], 1)

            def max_in(b, k):
                h, j, m = k // 8, k % 8 // 2, k % 2
                slot = stack_use(b, h, j)[0]
                dve.wait_ge(q["f_n_tr"], b * NH + k + 1)
                dve.tensor_tensor(stk[slot][0][M0:M1, m, :].rearrange("p (t n) -> p t n", t=T),
                                  bank[6][M0:M1, 0:P].unsqueeze(1).broadcast_to([2 * T, T, P]),
                                  own[M0:M1], ALU.mult).then_inc(q["f_n_in"], 1)

            def finish(b, g):
                hs = slice(g * HG, (g + 1) * HG)
                dve.wait_ge(q["f_exp"], b * NH * T + T * HG * (g + 1))
                dve.reciprocal(rZ[:, :, hs], Z[:, :, hs]).then_inc(q["f_rz"], 1)
                dve.wait_ge(q["f_rz"], b * NG + g + 1)
                dve.wait_ge(q["f_ot"], b * NG + g + 1)
                if g % 2 == 0:
                    await_ge(dve, "f_att_out", (2 * b + g // 2) * 16)
                for m in range(2):
                    ins = dve.tensor_tensor(
                        tmp[:, :, m * P + g % 2 * 2 * HD:m * P + (g % 2 + 1) * 2 * HD].rearrange("p t (j d) -> p t j d", j=2),
                        bank[6][:].rearrange("p (t j d) -> p t j d", t=T, j=HG)[:, :, 2 * m:2 * m + 2],
                        rZ[:, :, g * HG + m:g * HG + m + 3:2].unsqueeze(3).broadcast_to([P, T, 2, HD]), ALU.mult)
                ins.then_inc(q["f_o_fin"], 1)

            def expert_lo(e, cs):
                if e < EARLY:
                    dve.wait_ge(q["m_early_hi"], e * C + cs[-1] + 1)
                else:
                    dve.wait_ge(q["m_ehi"], (e - EARLY) * C + cs[-1] + 1)
                c = slice(cs[0], cs[-1] + 1)
                dve.tensor_tensor(ew[e][:, 1, c], full(ew[e][:, 1, c]), full(ew[e][:, 0, c]), ALU.subtract).then_inc(q["m_elo"], len(cs))

            def batch(b, first, last):
                for k in range(NH):
                    for what, of, head in plan(b, k, "dve", first, last):
                        if what[0] == "m":
                            maxes(of, head, (int(what[1]),))
                        elif what == "s":
                            max_parts(of, head)
                        elif what == "n":
                            max_in(of, head)
                            if last and k >= NH - 2 * EARLY:
                                expert_lo((k - NH + 2 * EARLY) // 2, range(k % 2 * C // 2, (k % 2 + 1) * C // 2))
                        elif what == "OT":
                            finish(of, head)
                        else:
                            split(of, what, *number(of, what), bank[DB[0]])

            for item in BEFORE:
                n, hn = early(item)
                split(0, item, n, hn, bank[DB[n % len(DB)]], True)
                for step in ROUTING.get(item, ()):
                    step()
            batch(0, True, False)
            with dve.Fori(1, B - 1) as b:
                batch(b, False, False)
            batch(B - 1, False, True)
            max_parts(B - 1, NH - 1)
            max_in(B - 1, NH - 1)
            finish(B - 1, NG - 1)
            def rows_lo(i, k):
                dve.wait_ge(q["m_hi"], i + 1)
                dve.tensor_tensor(gT[k][:, 1].rearrange("p c n -> p (c n)"), bank[k][:],
                                  full(gT[k][:, 0].rearrange("p c n -> p (c n)")), ALU.subtract).then_inc(q["m_hT"], 1)

            def blocks(n, part):
                for k in range(4):
                    i = 4 * n + k
                    if not (part == "first" and k == 0) and not (part == "last" and k == 3):
                        rows_lo(i + 1, (k + 1) % 2)
                    e = dve.value_load(bexp[0:1, bass.ds(i, 1)], min_val=0, max_val=NE - 1)
                    dve.wait_ge(q["m_full"], i + 1)
                    await_ge(dve, "m_added", 16 * (i - 3))
                    dve.tensor_tensor(ysb[k], bank[2 + k % 2][:], be_all[:, bass.ds(e * D, D)], ALU.add).then_inc(q["m_sum"], 1)

            for i in range(2):
                rows_lo(i, i)
            for e in range(EARLY, NE):
                expert_lo(e, range(C))
            dve.wait_ge(q["in_be"], 16)
            blocks(0, "first")
            with dve.Fori(1, NB // 4 - 1) as n:
                blocks(n, "middle")
            blocks(NB // 4 - 1, "last")


_INS = ("x", "ctx_1024", "L0_xattn_Wq", "L0_xattn_bq", "L0_xattn_Wk", "L0_xattn_bk", "L0_xattn_Wv", "L0_xattn_bv",
        "L0_ffn_W_qkv", "L0_ffn_b_qkv", "L0_ffn_W_gate", "L0_ffn_b_gate", "L0_ffn_W_experts", "L0_ffn_b_experts")
_OUTS = (((8, 512, 512), "float32"),)


def kernel(**inputs):
    import numpy as _np
    import concourse.bacc as _bacc
    from concourse import mybir as _mybir
    from concourse.bass_utils import run_bass_kernel_spmd as _run

    nc = _bacc.Bacc("TRN2", target_bir_lowering=False, num_devices=1)
    arrays, args = {}, []
    for name in _INS:
        a = _np.ascontiguousarray(inputs[name])
        arrays[f"in_{name}_dram"] = a
        args.append(nc.dram_tensor(f"in_{name}_dram", a.shape, _mybir.dt.from_np(a.dtype), kind="ExternalInput").ap())
    for i, (shape, dtype) in enumerate(_OUTS):
        dt = _mybir.dt.from_np(_np.dtype(dtype))
        args.append(nc.dram_tensor(f"out_{i}_dram", shape, dt, kind="ExternalOutput").ap())
    program(nc, *args)
    r = _run(nc, [arrays], core_ids=[0])
    got = tuple(r.results[0][f"out_{i}_dram"] for i in range(len(_OUTS)))
    return got[0]
```
